# Optimizing a Trainium2 kernel written in Bass

```python
import numpy as np
import jax
import jax.numpy as jnp

def _softmax(x, axis=-1):
    return jax.nn.softmax(x, axis=axis)

def _gelu(x):
    return jax.nn.gelu(x, approximate=True)

def _silu(x):
    return jax.nn.silu(x)

def _sigmoid(x):
    return jax.nn.sigmoid(x)

def _layernorm(x, axis=-1, eps=1e-05):
    m = jnp.mean(x, axis=axis, keepdims=True)
    v = jnp.var(x, axis=axis, keepdims=True)
    return (x - m) / jnp.sqrt(v + eps)

def _scatter_add(tgt, idx, src, axis=0):
    return tgt.at[idx].add(src)

def _segment_sum(src, seg, n):
    return jax.ops.segment_sum(src, seg, n)
kernel_name = 'mk_seq_postln_d1_jaxref_r4_e3fa3f'

def setup_inputs(seed: int=0):
    np.random.seed(seed)
    _w = jnp.asarray

    def _L0_attn_setup():
        import jax, jax.numpy as jnp
        import numpy as np
        B, L, C = (2, 512, 256)
        H, POS = (8, 16)
        D = C // H
        MAXS = 32
        S = MAXS + 1
        MAX_FREQ, MIN_FREQ = (16.0, 1.0)
        SCALE = POS ** (-0.5)
        key = jax.random.key(seed)
        ks = jax.random.split(key, 12)

        def w(k, shape, s=0.02):
            return jax.random.normal(k, shape, dtype=jnp.float32) * s
        return {'x': jax.random.normal(ks[0], (B, L, C), dtype=jnp.float32), 'w_wave': w(ks[1], (C, 3 * H)), 'b_wave': w(ks[2], (3 * H,)), 'w_query': w(ks[3], (C, H * POS)), 'b_query': w(ks[4], (H * POS,)), 'key_weight': w(ks[5], (POS,)), 'w_se1': w(ks[6], (C, C // 4)), 'b_se1': w(ks[7], (C // 4,)), 'w_se2': w(ks[8], (C // 4, C)), 'b_se2': w(ks[9], (C,)), 'w_out': w(ks[10], (C, C))}
    _L0_attn_in = _L0_attn_setup()

    def _L0_ffn_setup():
        import jax, jax.numpy as jnp
        import numpy as np
        B, N, D, H, E = (4, 256, 256, 16, 8)
        DK = D // H
        HID = 4 * D
        EPS = 1e-05

        def _layernorm(x, w, b):
            m = jnp.mean(x, axis=-1, keepdims=True)
            v = jnp.mean(jnp.square(x - m), axis=-1, keepdims=True)
            return (x - m) * jax.lax.rsqrt(v + EPS) * w + b

        def _msa(x, w_qkv, w_proj):
            b, n, d = x.shape
            qkv = (x @ w_qkv).reshape(b, n, 3, H, DK)
            q = qkv[:, :, 0].transpose(0, 2, 1, 3)
            k = qkv[:, :, 1].transpose(0, 2, 1, 3)
            v = qkv[:, :, 2].transpose(0, 2, 1, 3)
            attn = jnp.einsum('bhnd,bhmd->bhnm', q, k) * (1.0 / np.sqrt(DK))
            attn = jax.nn.softmax(attn, axis=-1)
            y = jnp.einsum('bhnm,bhmd->bhnd', attn, v)
            y = y.transpose(0, 2, 1, 3).reshape(b, n, d)
            return y @ w_proj

        def _moe_mlp(x, gate_w, gate_b, w1, w2):
            b, n, d = x.shape
            xf = x.reshape(b * n, d)
            logits = xf @ gate_w + gate_b
            one_hot = jax.nn.one_hot(jnp.argmax(logits, axis=-1), E, dtype=xf.dtype)
            h = jax.nn.gelu(jnp.einsum('td,edh->teh', xf, w1), approximate=True)
            y = jnp.einsum('teh,ehd->ted', h, w2)
            out = jnp.einsum('te,ted->td', one_hot, y)
            return out.reshape(b, n, d)
        key = jax.random.key(seed)
        ks = jax.random.split(key, 8)
        s = 0.02
        return {'x': jax.random.normal(ks[0], (B, N, D), jnp.float32), 'ln1_w': jnp.ones((D,), jnp.float32), 'ln1_b': jnp.zeros((D,), jnp.float32), 'w_qkv': jax.random.normal(ks[1], (D, 3 * D), jnp.float32) * s, 'w_proj': jax.random.normal(ks[2], (D, D), jnp.float32) * s, 'ln2_w': jnp.ones((D,), jnp.float32), 'ln2_b': jnp.zeros((D,), jnp.float32), 'gate_w': jax.random.normal(ks[3], (D, E), jnp.float32) * s, 'gate_b': jnp.zeros((E,), jnp.float32), 'w1': jax.random.normal(ks[4], (E, D, HID), jnp.float32) * s, 'w2': jax.random.normal(ks[5], (E, HID, D), jnp.float32) * s}
    _L0_ffn_in = _L0_ffn_setup()
    _d = {'L0_attn_x': _L0_attn_in['x'], 'L0_attn_w_wave': _L0_attn_in['w_wave'], 'L0_attn_b_wave': _L0_attn_in['b_wave'], 'L0_attn_w_query': _L0_attn_in['w_query'], 'L0_attn_b_query': _L0_attn_in['b_query'], 'L0_attn_key_weight': _L0_attn_in['key_weight'], 'L0_attn_w_se1': _L0_attn_in['w_se1'], 'L0_attn_b_se1': _L0_attn_in['b_se1'], 'L0_attn_w_se2': _L0_attn_in['w_se2'], 'L0_attn_b_se2': _L0_attn_in['b_se2'], 'L0_attn_w_out': _L0_attn_in['w_out'], 'L0_ffn_ln1_w': _L0_ffn_in['ln1_w'], 'L0_ffn_ln1_b': _L0_ffn_in['ln1_b'], 'L0_ffn_w_qkv': _L0_ffn_in['w_qkv'], 'L0_ffn_w_proj': _L0_ffn_in['w_proj'], 'L0_ffn_ln2_w': _L0_ffn_in['ln2_w'], 'L0_ffn_ln2_b': _L0_ffn_in['ln2_b'], 'L0_ffn_gate_w': _L0_ffn_in['gate_w'], 'L0_ffn_gate_b': _L0_ffn_in['gate_b'], 'L0_ffn_w1': _L0_ffn_in['w1'], 'L0_ffn_w2': _L0_ffn_in['w2']}
    _x0 = _d['L0_attn_x']
    _d['L0_attn_x'] = jax.random.normal(jax.random.fold_in(jax.random.key(seed), 1), (4, 1024, 256), dtype=_x0.dtype)
    del _x0
    return _d

def reference(L0_attn_x, L0_attn_w_wave, L0_attn_b_wave, L0_attn_w_query, L0_attn_b_query, L0_attn_key_weight, L0_attn_w_se1, L0_attn_b_se1, L0_attn_w_se2, L0_attn_b_se2, L0_attn_w_out, L0_ffn_ln1_w, L0_ffn_ln1_b, L0_ffn_w_qkv, L0_ffn_w_proj, L0_ffn_ln2_w, L0_ffn_ln2_b, L0_ffn_gate_w, L0_ffn_gate_b, L0_ffn_w1, L0_ffn_w2):

    def _L0_attn_ref(x, w_wave, b_wave, w_query, b_query, key_weight, w_se1, b_se1, w_se2, b_se2, w_out):
        import jax, jax.numpy as jnp
        import numpy as np
        B, L, C = (2, 512, 256)
        H, POS = (8, 16)
        D = C // H
        MAXS = 32
        S = MAXS + 1
        MAX_FREQ, MIN_FREQ = (16.0, 1.0)
        SCALE = POS ** (-0.5)
        b, l, c = x.shape
        stride_grid = jnp.arange(-MAXS // 2, MAXS // 2 + 1, dtype=x.dtype)
        wp = jax.nn.silu(x @ w_wave + b_wave).reshape(b, l, 3, H)
        freq = jax.nn.sigmoid(wp[:, :, 0, :]) * (MAX_FREQ - MIN_FREQ) + MIN_FREQ
        phase = jnp.tanh(wp[:, :, 1, :]) * MAX_FREQ
        decay = jax.nn.sigmoid(wp[:, :, 2, :]) * 9.5 + 0.5
        freq_avg = freq.mean(-1)
        phase_avg = phase.mean(-1)
        decay_avg = decay.mean(-1)
        q = jax.nn.silu(x @ w_query + b_query).reshape(b, l, H, POS)
        centers = jnp.arange(l, dtype=x.dtype)
        sample_pos = centers[None, :, None] + stride_grid[None, None, :] * freq_avg[..., None] + phase_avg[..., None]
        valid = (sample_pos >= 0) & (sample_pos < l)
        idx = jnp.clip(sample_pos.astype(jnp.int32), 0, l - 1)
        values = jnp.take_along_axis(x[:, :, None, :], idx[:, :, :, None], axis=1)
        values = values.reshape(b, l, S, H, D).transpose(0, 1, 3, 2, 4)
        rel = jnp.abs(stride_grid)[None, None, None, :] * freq_avg[:, :, None, None]
        qk = jnp.einsum('blhd,d->blh', q, key_weight)
        scores = qk[..., None] * rel * SCALE
        env = jnp.exp(-rel / jnp.clip(decay_avg, 0.1, None)[:, :, None, None])
        mask = valid[:, :, None, :]
        scores = jnp.where(mask, scores, -jnp.inf)
        attn = jax.nn.softmax(scores, axis=-1) * env * mask.astype(x.dtype)
        attn = attn / (attn.sum(-1, keepdims=True) + 1e-08)
        out = jnp.einsum('blhsd,blhs->blhd', values, attn).reshape(b, l, c)
        se = jax.nn.sigmoid(jax.nn.silu(out @ w_se1 + b_se1) @ w_se2 + b_se2)
        out = out * se
        out = jax.nn.silu(out @ w_out)
        return out

    def _L0_ffn_ref(x, ln1_w, ln1_b, w_qkv, w_proj, ln2_w, ln2_b, gate_w, gate_b, w1, w2):
        import jax, jax.numpy as jnp
        import numpy as np
        B, N, D, H, E = (4, 256, 256, 16, 8)
        DK = D // H
        HID = 4 * D
        EPS = 1e-05

        def _layernorm(x, w, b):
            m = jnp.mean(x, axis=-1, keepdims=True)
            v = jnp.mean(jnp.square(x - m), axis=-1, keepdims=True)
            return (x - m) * jax.lax.rsqrt(v + EPS) * w + b

        def _msa(x, w_qkv, w_proj):
            b, n, d = x.shape
            qkv = (x @ w_qkv).reshape(b, n, 3, H, DK)
            q = qkv[:, :, 0].transpose(0, 2, 1, 3)
            k = qkv[:, :, 1].transpose(0, 2, 1, 3)
            v = qkv[:, :, 2].transpose(0, 2, 1, 3)
            attn = jnp.einsum('bhnd,bhmd->bhnm', q, k) * (1.0 / np.sqrt(DK))
            attn = jax.nn.softmax(attn, axis=-1)
            y = jnp.einsum('bhnm,bhmd->bhnd', attn, v)
            y = y.transpose(0, 2, 1, 3).reshape(b, n, d)
            return y @ w_proj

        def _moe_mlp(x, gate_w, gate_b, w1, w2):
            b, n, d = x.shape
            xf = x.reshape(b * n, d)
            logits = xf @ gate_w + gate_b
            one_hot = jax.nn.one_hot(jnp.argmax(logits, axis=-1), E, dtype=xf.dtype)
            h = jax.nn.gelu(jnp.einsum('td,edh->teh', xf, w1), approximate=True)
            y = jnp.einsum('teh,ehd->ted', h, w2)
            out = jnp.einsum('te,ted->td', one_hot, y)
            return out.reshape(b, n, d)
        x = x + _msa(_layernorm(x, ln1_w, ln1_b), w_qkv, w_proj)
        x = x + _moe_mlp(_layernorm(x, ln2_w, ln2_b), gate_w, gate_b, w1, w2)
        return x
    x = L0_attn_x
    x = _layernorm(x + _L0_attn_ref(x, L0_attn_w_wave, L0_attn_b_wave, L0_attn_w_query, L0_attn_b_query, L0_attn_key_weight, L0_attn_w_se1, L0_attn_b_se1, L0_attn_w_se2, L0_attn_b_se2, L0_attn_w_out), axis=-1)
    x = _layernorm(x + _L0_ffn_ref(x, L0_ffn_ln1_w, L0_ffn_ln1_b, L0_ffn_w_qkv, L0_ffn_w_proj, L0_ffn_ln2_w, L0_ffn_ln2_b, L0_ffn_gate_w, L0_ffn_gate_b, L0_ffn_w1, L0_ffn_w2), axis=-1)
    return x

_drawn_inputs = setup_inputs


def setup_inputs(seed=0):
    import zlib

    import numpy as np

    out = dict(_drawn_inputs(seed))
    spreads = {'L0_ffn_ln1_w': (1.0, 0.6),
     'L0_ffn_ln1_b': (0.0, 0.8),
     'L0_ffn_ln2_w': (1.0, 0.6),
     'L0_ffn_ln2_b': (0.0, 2.0),
     'L0_ffn_gate_b': (0.0, 0.75)}
    factors = {'L0_attn_b_wave': 4.817,
     'L0_attn_w_query': 8.0,
     'L0_attn_b_query': 21.73,
     'L0_attn_key_weight': 8.0,
     'L0_attn_w_se1': 8.0,
     'L0_attn_b_se1': 53.975,
     'L0_attn_w_se2': 8.0,
     'L0_attn_b_se2': 42.81,
     'L0_ffn_w_qkv': 6.678,
     'L0_ffn_w_proj': 7.295,
     'L0_ffn_gate_w': 3.828,
     'L0_ffn_w1': 3.577,
     'L0_ffn_w2': 3.571}
    for name, (base, spread) in spreads.items():
        noise = np.random.default_rng([zlib.crc32(name.encode()), seed]).standard_normal(out[name].shape)
        drawn = base * np.exp(spread * noise) if base else spread * noise
        out[name] = jnp.asarray(drawn.astype(out[name].dtype))
    for name, factor in factors.items():
        out[name] = (out[name] * factor).astype(out[name].dtype)
    return out
```

```python
import concourse.bass as bass
from concourse import mybir
from contextlib import ExitStack

F32 = mybir.dt.float32
BF16 = mybir.dt.bfloat16
I32 = mybir.dt.int32
ALU = mybir.AluOpType
ACT = mybir.ActivationFunctionType
AX = mybir.AxisListType
P = 128

B, L, C = 4, 1024, 256
TOKENS = B * L
TILES = TOKENS // P
BT = L // P
KC = C // P
WH, POS, REACH = 8, 16, 16
WD = C // WH
STEPS = 2 * REACH + 1
NW = 3 * WH + WH * POS
SE = C // 4
H, DK = 16, 16
QUADS = H // 4
E, HID = 8, 1024
MT = TILES + E - 1
EPS = 1e-5


class Chain:

    def __init__(self, eng, sem, base=0):
        self.eng, self.sem, self.base, self.n = eng, sem, base, 0

    def did(self, ins):
        ins.then_inc(self.sem, 1)
        self.n += 1
        return self.n

    def wait(self, n=None):
        self.eng.wait_ge(self.sem, self.base + (self.n if n is None else n))

    def link(self, ins):
        self.did(ins)
        self.wait()


def build(nc, io, dr):
    with ExitStack() as top:
        sems = {}

        def sem(name):
            assert name not in sems
            sems[name] = top.enter_context(nc.semaphore(name))
            return sems[name]

        def sb(ctx, name, shape, dt=F32):
            return ctx.enter_context(nc.sbuf_tensor(name, shape, dt))

        def ps(ctx, name, shape, dt=F32):
            return ctx.enter_context(nc.psum_tensor(name, shape, dt))

        ident = sb(top, "ident", [P, P])
        identb = sb(top, "identb", [P, P], BF16)
        constants(nc, sem, ident, identb)
        with ExitStack() as wave:
            par = {n: sb(wave, "par_" + n, [P, TILES]) for n in ("freq", "phase", "invf", "mid", "kmax")}
            par["lpos"] = sb(wave, "par_lpos", [P, TILES])
            par["alpha"] = sb(wave, "par_alpha", [P, TILES, WH])
            par["beta"] = sb(wave, "par_beta", [P, TILES, WH])
            wave_parameters(nc, sem, sb, ps, io, dr, ident, par)
            wave_sampling(nc, sem, sb, ps, io, dr, ident, identb, par)
        with ExitStack() as ctx:
            gate_and_project(nc, sem, lambda *a: sb(ctx, *a), lambda *a: ps(ctx, *a), io, dr, ident)
        w1 = sb(top, "w1", [P, KC, E, HID])
        w2 = sb(top, "w2", [P, HID // P, E, C])
        w_in = sem("experts_in")
        with ExitStack() as ctx:
            attention(nc, sem, lambda *a: sb(ctx, *a), lambda *a: ps(ctx, *a), io, dr, ident, w1, w2, w_in)
        slot = sb(top, "slot", [P, TILES], I32)
        expert = sb(top, "expert", [1, MT], I32)
        with ExitStack() as outer:
            logits = sb(outer, "logits", [P, TILES, E])
            n2 = sb(outer, "n2", [P, TILES, C])
            with ExitStack() as ctx:
                project_and_gate(nc, sem, lambda *a: sb(ctx, *a), lambda *a: ps(ctx, *a), io, dr, ident, n2, logits)
            with ExitStack() as ctx:
                dispatch(nc, sem, lambda *a: sb(ctx, *a), lambda *a: ps(ctx, *a), dr, n2, logits, slot, expert)
        with ExitStack() as ctx:
            experts(nc, sem, lambda *a: sb(ctx, *a), lambda *a: ps(ctx, *a), io, dr, ident, w1, w2, expert)
        with ExitStack() as ctx:
            combine(nc, sem, lambda *a: sb(ctx, *a), io, dr, slot)


def constants(nc, sem, ident, identb):
    zeroed, made = sem("ident_zeroed"), sem("ident_made")
    with nc.Block() as block:
        @block.gpsimd
        def _(pool):
            nc.gpsimd.memset(ident[:], 0.0).then_inc(zeroed, 1)
            pool.wait_ge(zeroed, 1)
            nc.gpsimd.affine_select(out=ident[:], in_=ident[:], compare_op=ALU.not_equal, fill=1.0, base=0,
                                    pattern=[[-1, P]], channel_multiplier=1).then_inc(made, 1)

        @block.vector
        def _(dve):
            dve.wait_ge(made, 1)
            nc.vector.tensor_copy(identb[:], ident[:])


def wave_parameters(nc, sem, sb, ps, io, dr, ident, par):
    with ExitStack() as ctx:
        tanhs = sb(ctx, "wp_tanh", [P, TILES, 3, WH])
        qk = sb(ctx, "wp_qk", [P, TILES, WH])
        kw = sb(ctx, "wp_kw", [P, POS])
        with ExitStack() as inner:
            project_waves(nc, sem, lambda *a: sb(inner, *a), lambda *a: ps(inner, *a), io, ident, kw, tanhs, qk)
        with ExitStack() as inner:
            wave_normalisers(nc, sem, lambda *a: sb(inner, *a), par, tanhs, qk, dr)


def project_waves(nc, sem, sb, ps, io, ident, kw, tanhs, qk):
    xb = sb("pw_x", [P, BT, C])
    xT = sb("pw_xT", [P, KC, L])
    w = sb("pw_w", [P, KC, NW])
    bias = sb("pw_bias", [P, NW])
    pre = sb("pw_pre", [P, BT, NW])
    act = sb("pw_act", [P, BT, NW])
    prod = sb("pw_prod", [P, BT, WH * POS])
    pT = ps("pw_pT", [P, KC, L])
    pW = ps("pw_pW", [P, BT // 2, 2, C])
    w_in, x_in = sem("wave_w_in"), sem("wave_x_in")
    turned, evac, mm = sem("wave_x_turned"), sem("wave_xT_ready"), sem("wave_projected")
    biased, silued, tanhed, qprod, qkd = (sem("wave_" + n) for n in ("biased", "silued", "tanhed", "qk_products", "qk_summed"))
    pW3 = pW[:, :, :, 0:NW]
    act4 = act[:, :, 0:3 * WH].rearrange("p t (g h) -> p t g h", g=3)
    x = io["L0_attn_x"].rearrange("b (t p) c -> b p t c", p=P)

    def row(a, n):
        return a.rearrange("(o n) -> o n", o=1).to_broadcast([P, n])

    with nc.Block() as block:
        @block.sync
        def _(sp):
            def each(b):
                sp.wait_ge(turned, b)
                sp.dma_start(xb[:], x[b]).then_inc(x_in, 16)

            each(0)
            with sp.Fori(1, B) as b:
                each(b)

        @block.scalar
        def _(a):
            a.dma_start(w[:, :, 0:3 * WH], io["L0_attn_w_wave"].rearrange("(k p) n -> p k n", p=P)).then_inc(w_in, 16)
            a.dma_start(w[:, :, 3 * WH:NW], io["L0_attn_w_query"].rearrange("(k p) n -> p k n", p=P)).then_inc(w_in, 16)
            a.dma_start(bias[:, 0:3 * WH], row(io["L0_attn_b_wave"], 3 * WH)).then_inc(w_in, 16)
            a.dma_start(bias[:, 3 * WH:NW], row(io["L0_attn_b_query"], WH * POS)).then_inc(w_in, 16)
            a.dma_start(kw[:], row(io["L0_attn_key_weight"], POS)).then_inc(w_in, 16)
            def each(b):
                a.wait_ge(turned, b + 1)
                a.wait_ge(mm, b)
                nc.scalar.copy(xT[:, 1, :], pT[:, 1, :]).then_inc(evac, 1)
                a.wait_ge(biased, b + 1)
                a.wait_ge(qkd, b)
                nc.scalar.activation(act[:], pre[:], ACT.Silu).then_inc(silued, 1)
                a.wait_ge(silued, b + 1)
                at = tanhs[:, bass.ds(b * BT, BT), :, :]
                nc.scalar.activation(at[:, :, 0:3:2, :], act4[:, :, 0:3:2, :], ACT.Tanh, scale=0.5).then_inc(tanhed, 1)
                nc.scalar.activation(at[:, :, 1, :], act4[:, :, 1, :], ACT.Tanh).then_inc(tanhed, 1)

            each(0)
            with a.Fori(1, B) as b:
                each(b)
            a.wait_ge(tanhed, 2 * B)

        @block.tensor
        def _(pe):
            pe.wait_ge(w_in, 5 * 16)
            def each(b):
                pe.wait_ge(x_in, 16 * b + 16)
                pe.wait_ge(evac, 2 * b)
                for k in range(KC):
                    for t in range(BT):
                        last = nc.tensor.transpose(pT[:, k, t * P:(t + 1) * P], xb[:, t, k * P:(k + 1) * P], ident[:])
                last.then_inc(turned, 1)
                pe.wait_ge(evac, 2 * b + 2)
                pe.wait_ge(biased, b)
                for t in range(BT):
                    for k in range(KC):
                        last = nc.tensor.matmul(pW[:, t // 2, t % 2, 0:NW], xT[:, k, t * P:(t + 1) * P], w[:, k, :],
                                                start=(k == 0), stop=(k == KC - 1))
                last.then_inc(mm, 1)

            each(0)
            with pe.Fori(1, B) as b:
                each(b)

        @block.vector
        def _(dve):
            dve.wait_ge(w_in, 5 * 16)
            def each(b):
                dve.wait_ge(turned, b + 1)
                dve.wait_ge(mm, b)
                nc.vector.tensor_copy(xT[:, 0, :], pT[:, 0, :]).then_inc(evac, 1)
                dve.wait_ge(mm, b + 1)
                dve.wait_ge(silued, b)
                nc.vector.tensor_tensor(pre[:].rearrange("p (s t) n -> p s t n", t=2), pW3,
                                        bias[:].unsqueeze(1).unsqueeze(1).to_broadcast([P, BT // 2, 2, NW]),
                                        ALU.add).then_inc(biased, 1)
                dve.wait_ge(silued, b + 1)
                nc.vector.tensor_tensor(prod[:].rearrange("p t (h d) -> p (t h) d", h=WH),
                                        act[:, :, 3 * WH:NW].rearrange("p t (h d) -> p t h d", h=WH),
                                        kw[:].unsqueeze(1).to_broadcast([P, BT * WH, POS]).rearrange("p (t h) d -> p t h d", h=WH),
                                        ALU.mult).then_inc(qprod, 1)
                dve.wait_ge(qprod, b + 1)
                nc.vector.reduce_sum(qk[:, bass.ds(b * BT, BT), :], prod[:].rearrange("p t (h d) -> p t h d", h=WH),
                                     AX.X).then_inc(qkd, 1)

            each(0)
            with dve.Fori(1, B) as b:
                each(b)
            dve.wait_ge(qkd, B)


def wave_normalisers(nc, sem, sb, par, tanhs, qk, dr):
    NK = REACH + 1
    mean = sb("wn_sum", [P, TILES, 3])
    steps = sb("wn_steps", [P, STEPS])
    ks = sb("wn_ks", [P, NK])
    far = sb("wn_far", [P, NK])
    pos = sb("wn_pos", [P, TILES, STEPS])
    pos2 = sb("wn_pos2", [P, TILES, STEPS])
    inside = sb("wn_inside", [P, TILES, STEPS])
    cnt = sb("wn_count", [P, TILES, NK])
    any_ = sb("wn_any", [P, TILES, NK])
    tk = sb("wn_tk", [P, TILES, NK])
    tk2 = sb("wn_tk2", [P, TILES, NK])
    env = sb("wn_env", [P, TILES, NK])
    dec, g, kmin = (sb("wn_" + n, [P, TILES]) for n in ("dec", "g", "kmin"))
    a_, m1, m2, Z, Es, lnD = (sb("wn_" + n, [P, TILES, WH]) for n in ("a", "m1", "m2", "Z", "E", "lnD"))
    big = sb("wn_big", [P, TILES, WH, NK])
    big2 = sb("wn_big2", [P, TILES, WH, NK])
    consts, d, acted, asked = sem("wn_consts"), sem("wn_dve"), sem("wn_acted"), sem("wn_asked")
    freq, phase, invf, mid, kmax, lpos = (par[n] for n in ("freq", "phase", "invf", "mid", "kmax", "lpos"))
    alpha, beta = par["alpha"], par["beta"]

    def over(a, n):
        return a[:].unsqueeze(2).to_broadcast([P, TILES, n])

    def heads(a):
        return a[:].unsqueeze(3).to_broadcast([P, TILES, WH, NK])

    def dist(a):
        return a[:].unsqueeze(2).to_broadcast([P, TILES, WH, NK])

    with nc.Block() as block:
        @block.gpsimd
        def _(pool):
            nc.gpsimd.iota(lpos[:], pattern=[[0, B], [P, BT]], base=0, channel_multiplier=1,
                           allow_small_or_imprecise_dtypes=True).then_inc(consts, 1)
            nc.gpsimd.iota(steps[:], pattern=[[1, STEPS]], base=-REACH, channel_multiplier=0,
                           allow_small_or_imprecise_dtypes=True).then_inc(consts, 1)
            nc.gpsimd.iota(ks[:], pattern=[[1, NK]], base=0, channel_multiplier=0,
                           allow_small_or_imprecise_dtypes=True).then_inc(consts, 1)
            nc.gpsimd.iota(far[:], pattern=[[-1, NK]], base=1000, channel_multiplier=0,
                           allow_small_or_imprecise_dtypes=True).then_inc(consts, 1)

        @block.vector
        def _(dve):
            v = nc.vector
            c = Chain(dve, d)
            c.link(v.reduce_sum(mean[:], tanhs[:], AX.X))
            c.did(v.tensor_scalar(freq[:], mean[:, :, 0], 7.5 / WH, 8.5, ALU.mult, ALU.add))
            c.did(v.tensor_scalar(phase[:], mean[:, :, 1], 16.0 / WH, None, ALU.mult))
            c.link(v.tensor_scalar(dec[:], mean[:, :, 2], 4.75 / WH, 5.25, ALU.mult, ALU.add))
            c.did(v.tensor_scalar(dec[:], dec[:], 0.1, None, ALU.max))
            c.link(v.reciprocal(invf[:], freq[:]))
            c.link(v.reciprocal(g[:], dec[:]))
            dve.wait_ge(consts, 4)
            c.link(v.tensor_tensor(g[:], g[:], freq[:], ALU.mult))
            c.did(v.tensor_tensor(pos[:], steps[:].unsqueeze(1).to_broadcast([P, TILES, STEPS]), over(freq, STEPS), ALU.mult))
            c.link(v.tensor_tensor(mid[:], lpos[:], phase[:], ALU.add))
            c.did(v.tensor_tensor(pos2[:], pos[:], over(lpos, STEPS), ALU.add))
            c.link(v.tensor_scalar(mid[:], mid[:], -1.0, 0.5, ALU.mult, ALU.add))
            c.did(v.tensor_tensor(pos[:], pos2[:], over(phase, STEPS), ALU.add))
            c.link(v.tensor_tensor(mid[:], mid[:], invf[:], ALU.mult))
            c.link(v.tensor_scalar(pos2[:], pos[:], float(L), None, ALU.is_lt))
            c.link(v.scalar_tensor_tensor(out=inside[:], in0=pos[:], scalar=0.0, in1=pos2[:], op0=ALU.is_ge, op1=ALU.mult))
            c.did(v.tensor_copy(cnt[:, :, 0], inside[:, :, REACH]))
            c.link(v.tensor_tensor(cnt[:, :, 1:NK], inside[:, :, REACH + 1:STEPS], inside[:, :, REACH - 1::-1], ALU.add))
            c.link(v.tensor_scalar(any_[:], cnt[:], 0.0, None, ALU.is_gt))
            c.did(v.tensor_tensor(tk[:], any_[:], ks[:].unsqueeze(1).to_broadcast([P, TILES, NK]), ALU.mult))
            c.link(v.tensor_tensor(tk2[:], any_[:], far[:].unsqueeze(1).to_broadcast([P, TILES, NK]), ALU.mult))
            c.did(v.tensor_reduce(kmax[:], tk[:], AX.X, ALU.max))
            c.link(v.tensor_reduce(kmin[:], tk2[:], AX.X, ALU.max))
            c.did(v.tensor_scalar(kmin[:], kmin[:], -1.0, 1000.0, ALU.mult, ALU.add))
            c.link(v.scalar_tensor_tensor(out=a_[:], in0=qk[:], scalar=float(POS) ** -0.5, in1=over(freq, WH),
                                          op0=ALU.mult, op1=ALU.mult))
            c.did(v.tensor_tensor(m1[:], a_[:], over(kmax, WH), ALU.mult))
            c.link(v.tensor_tensor(m2[:], a_[:], over(kmin, WH), ALU.mult))
            c.did(v.tensor_tensor(big[:], heads(a_), ks[:].unsqueeze(1).unsqueeze(1).to_broadcast([P, TILES, WH, NK]), ALU.mult))
            c.link(v.tensor_tensor(m1[:], m1[:], m2[:], ALU.max))
            c.did(v.tensor_tensor(tk[:], over(g, NK), ks[:].unsqueeze(1).to_broadcast([P, TILES, NK]), ALU.mult))
            c.link(v.tensor_tensor(big2[:], big[:], heads(m1), ALU.subtract))
            v.tensor_scalar(big2[:], big2[:], 0.0, None, ALU.min).then_inc(asked, 1)
            dve.wait_ge(acted, 2)
            c.did(v.tensor_tensor(big2[:], big[:], dist(cnt), ALU.mult))
            c.link(v.tensor_tensor(alpha[:], a_[:], over(g, WH), ALU.subtract))
            c.did(v.reduce_sum(Z[:], big2[:], AX.X))
            c.link(v.tensor_tensor(beta[:], alpha[:], over(kmax, WH), ALU.mult))
            c.did(v.tensor_tensor(big[:], big2[:], dist(env), ALU.mult))
            c.link(v.tensor_tensor(beta[:], beta[:], m1[:], ALU.subtract))
            c.link(v.reduce_sum(Es[:], big[:], AX.X))
            v.scalar_tensor_tensor(out=lnD[:], in0=Z[:], scalar=1e-8, in1=Es[:], op0=ALU.mult, op1=ALU.add).then_inc(asked, 1)
            dve.wait_ge(acted, 3)
            c.link(v.tensor_tensor(beta[:], beta[:], m2[:], ALU.subtract))

        @block.scalar
        def _(a):
            a.wait_ge(asked, 1)
            nc.scalar.activation(big[:], big2[:], ACT.Exp).then_inc(acted, 1)
            nc.scalar.activation(env[:], tk[:], ACT.Exp, scale=-1.0).then_inc(acted, 1)
            a.wait_ge(asked, 2)
            nc.scalar.activation(m2[:], lnD[:], ACT.Ln).then_inc(acted, 1)


def wave_sampling(nc, sem, sb, ps, io, dr, ident, identb, par):
    MAGIC = 1.5 * 2.0 ** 23
    NEAR = 3
    G = 4
    assert (REACH * 16.0 + 16.0) < NEAR * P

    def near(g, r):
        i = G * g + r
        return list(range(max(0, i - NEAR), min(BT - 1, i + NEAR) + 1))

    width = [[len(near(g, r)) * P for r in range(G)] for g in range(2)]
    off = [[sum(width[g][:r]) for r in range(G)] for g in range(2)]
    slots = [[(j, r) for j in range(BT) for r in range(G) if j in near(g, r)] for g in range(2)]
    NS = len(slots[0])
    assert NS == len(slots[1])
    CH = 8
    chunks = [range(s, min(s + CH, NS)) for s in range(0, NS, CH)]
    NCH = len(chunks)
    UCH = NCH * (1 + WH)
    WMAX = max(map(max, width))
    FULL0, FREE0, READY0, MM0, OUT0, R0 = 2 * UCH, 2, WH * G, 2, 2, 2

    with ExitStack() as ctx:
        A = [sb(ctx, f"ws_A{i}", [P, NS * P]) for i in range(2)]
        AT = [sb(ctx, f"ws_AT{h}", [P, NS, P]) for h in range(WH)]
        KB, HB, HT = ([sb(ctx, f"ws_{n}{g}", [P, NS * P], BF16) for g in range(2)] for n in ("steps", "hit", "hitT"))
        step, pos = ([sb(ctx, f"ws_{n}{i}", [P, WMAX]) for i in range(2)] for n in ("step", "pos"))
        raw = [sb(ctx, f"ws_raw{i}", [P, WMAX]) for i in range(2)]
        below = [sb(ctx, f"ws_below{i}", [P, WMAX], BF16) for i in range(2)]
        xb = sb(ctx, "ws_x", [P, BT, C])
        rows = sb(ctx, "ws_rows", [P, L])
        ot = [sb(ctx, f"ws_ot{i}", [P, G * P]) for i in range(2)]
        pA = [ps(ctx, f"ws_pA{i}", [P, CH * P]) for i in range(2)]
        acc = [ps(ctx, f"ws_acc{i}", [P, G * P]) for i in range(2)]
        rows_made, x_in = sem("ws_rows_made"), sem("ws_x_in")
        raw_ready, clamped, rounded, placed, kstep = (sem("ws_" + n) for n in ("raw", "clamped", "rounded", "placed", "kgen"))
        ready, full, free, mm, acc_out = (sem("ws_" + n) for n in ("exp", "chunk_full", "chunk_free", "products", "acc_out"))
        ot_out = [sem(f"ws_ot_out{i}") for i in range(2)]
        KSTEPS = 5
        x = io["L0_attn_x"].rearrange("b (t p) c -> b p t c", p=P)
        outT = dr["outT"].rearrange("(q p) n -> q p n", p=P)

        def cols(g, r):
            return slice(off[g][r], off[g][r] + width[g][r])

        def mrows(g, r):
            return rows[:, near(g, r)[0] * P:(near(g, r)[-1] + 1) * P]

        with nc.Block() as block:
            def schedule(unit, kgen, eng):
                unit(0, 0, True, False)
                with eng.Fori(0, B - 1) as i:
                    unit(i * 2 + 1, 1, False, False)
                    unit(i * 2 + 2, 0, False, False)
                unit(2 * B - 1, 1, False, True)

            @block.sync
            def _(sp):
                def load_x(b):
                    sp.dma_start(xb[:], x[b]).then_inc(x_in, 16)

                def store(n, hq):
                    sp.wait_ge(acc_out, OUT0 + n * 2 + hq + 1)
                    sp.dma_start(outT[hq, :, bass.ds(n * (G * P), G * P)], ot[hq][:]).then_inc(ot_out[hq], 16)

                load_x(0)
                store(0, 0)
                with sp.Fori(0, B - 1) as i:
                    store(i * 2, 1)
                    store(i * 2 + 1, 0)
                    sp.wait_ge(mm, MM0 + i * 4 + 4)
                    load_x(i + 1)
                    store(i * 2 + 1, 1)
                    store(i * 2 + 2, 0)
                store(2 * B - 2, 1)
                store(2 * B - 1, 0)
                store(2 * B - 1, 1)
                for hq in range(2):
                    sp.wait_ge(ot_out[hq], 16 * 2 * B)

            @block.gpsimd
            def _(pool):
                nc.gpsimd.iota(rows[:], pattern=[[1, L]], base=0, channel_multiplier=0,
                               allow_small_or_imprecise_dtypes=True).then_inc(rows_made, 1)

            @block.scalar
            def _(a):
                a.sem_inc(ready, READY0)
                a.sem_inc(acc_out, OUT0)

                def locate(n, g, r):
                    t = bass.ds(n * G + r, 1)
                    a.wait_ge(rounded, n * G + (r - 1 if r else 0))
                    nc.scalar.activation(raw[r % 2][:, 0:width[g][r]], mrows(g, r), ACT.Identity,
                                         bias=par["mid"][:, t], scale=par["invf"][:, t]).then_inc(raw_ready, 1)

                def place(n, g, r):
                    w, t = width[g][r], bass.ds(n * G + r, 1)
                    a.wait_ge(rounded, n * G + r + 1)
                    nc.scalar.activation(pos[r % 2][:, 0:w], step[r % 2][:, 0:w], ACT.Identity,
                                         bias=par["lpos"][:, t], scale=par["freq"][:, t]).then_inc(placed, 1)

                def exps(n, g, h):
                    a.wait_ge(full, FULL0 + n * UCH + NCH * h if h >= 2 else FULL0 + (n - 1) * UCH + NCH * (WH + h))
                    for r in range(G):
                        t = bass.ds(n * G + r, 1)
                        nc.scalar.activation(A[h % 2][:, cols(g, r)], KB[g][:, cols(g, r)], ACT.Exp,
                                             bias=par["beta"][:, t, h], scale=par["alpha"][:, t, h]).then_inc(ready, 1)

                def drain(n, hq):
                    a.wait_ge(mm, MM0 + n * 2 + hq + 1)
                    a.wait_ge(ot_out[hq], n * 16)
                    nc.scalar.copy(ot[hq][:], acc[hq][:]).then_inc(acc_out, 1)

                def unit(n, g, first, last):
                    a.wait_ge(kstep, (n + 1) * G * KSTEPS)
                    for h in range(WH):
                        exps(n, g, h)
                        if h == 2 and not first:
                            drain(n - 1, 1)
                        if h == 6:
                            drain(n, 0)
                        if not last:
                            if 0 <= h - 2 < G:
                                place(n + 1, 1 - g, h - 2)
                            if 0 <= h - 1 < G:
                                locate(n + 1, 1 - g, h - 1)

                a.wait_ge(rows_made, 1)
                for r in range(G):
                    if r:
                        place(0, 0, r - 1)
                    locate(0, 0, r)
                place(0, 0, G - 1)
                unit(0, 0, True, False)
                with a.Fori(0, B - 1) as i:
                    unit(i * 2 + 1, 1, False, False)
                    unit(i * 2 + 2, 0, False, False)
                unit(2 * B - 1, 1, False, True)
                drain(2 * B - 1, 1)

            @block.vector
            def _(dve):
                v = nc.vector
                dve.sem_inc(free, FREE0)
                dve.wait_ge(rows_made, 1)

                def whole(n, g, r):
                    w, k = width[g][r], n * G + r
                    dve.wait_ge(raw_ready, k + 1)
                    v.tensor_scalar(raw[r % 2][:, 0:w], raw[r % 2][:, 0:w], float(REACH), float(-REACH),
                                    ALU.min, ALU.max).then_inc(clamped, 1)
                    dve.wait_ge(clamped, k + 1)
                    v.tensor_scalar(step[r % 2][:, 0:w], raw[r % 2][:, 0:w], MAGIC, MAGIC, ALU.add, ALU.subtract).then_inc(rounded, 1)

                def mark(n, g, r):
                    w, k = width[g][r], n * G + r
                    t, u = bass.ds(n * G + r, 1), r % 2
                    dve.wait_ge(placed, k + 1)
                    c = Chain(dve, kstep, k * KSTEPS)
                    c.did(v.scalar_tensor_tensor(out=pos[u][:, 0:w], in0=pos[u][:, 0:w], scalar=par["phase"][:, t],
                                                 in1=mrows(g, r), op0=ALU.add, op1=ALU.subtract))
                    bits = step[u][:, 0:w].bitcast(I32)
                    c.link(v.tensor_scalar(bits, bits, 0x7FFFFFFF, None, ALU.bitwise_and))
                    c.link(v.tensor_scalar(below[u][:, 0:w], pos[u][:, 0:w], 1.0, None, ALU.is_lt))
                    dve.wait_ge(full, FULL0 + n * UCH - 2 * UCH + NCH)
                    c.link(v.scalar_tensor_tensor(out=HB[g][:, cols(g, r)], in0=pos[u][:, 0:w], scalar=0.0,
                                                  in1=below[u][:, 0:w], op0=ALU.is_ge, op1=ALU.mult))
                    dve.wait_ge(ready, READY0 + (n - 1) * (WH * G))
                    c.did(v.scalar_tensor_tensor(out=KB[g][:, cols(g, r)], in0=step[u][:, 0:w],
                                                 scalar=par["kmax"][:, t], in1=HB[g][:, cols(g, r)],
                                                 op0=ALU.subtract, op1=ALU.mult))
                    assert c.n == KSTEPS

                def drain(n, g, c, h):
                    q = (c if h is None else NCH * (1 + h) + c)
                    dve.wait_ge(full, FULL0 + n * UCH + q + 1)
                    m = chunks[c]
                    w = len(m) * P
                    cs = slice(m[0] * P, m[0] * P + w)
                    p = pA[(g * UCH + q) % 2]
                    if h is None:
                        v.tensor_copy(HT[g][:, cs], p[:].bitcast(BF16)[:, 0:w]).then_inc(free, 1)
                    else:
                        v.tensor_tensor(AT[h][:].rearrange("p s l -> p (s l)")[:, cs], p[:, 0:w], HT[g][:, cs],
                                        ALU.mult).then_inc(free, 1)

                def unit(n, g, first, last):
                    dve.wait_ge(kstep, (n + 1) * G * KSTEPS)
                    for c in range(NCH):
                        drain(n, g, c, None)
                    dve.wait_ge(free, FREE0 + n * UCH + NCH)
                    for h in range(WH):
                        if h % 4 == 0:
                            dve.wait_ge(mm, MM0 + (n - 1) * 2 + h // 4 + 1)
                        for c in range(NCH):
                            drain(n, g, c, h)
                        if not last:
                            if 0 <= h - 2 < G:
                                whole(n + 1, 1 - g, h - 2)
                            if 0 <= h - 3 < G:
                                mark(n + 1, 1 - g, h - 3)

                for r in range(G):
                    whole(0, 0, r)
                    if r:
                        mark(0, 0, r - 1)
                mark(0, 0, G - 1)
                unit(0, 0, True, False)
                with dve.Fori(0, B - 1) as i:
                    unit(i * 2 + 1, 1, False, False)
                    unit(i * 2 + 2, 0, False, False)
                unit(2 * B - 1, 1, False, True)

            @block.tensor
            def _(pe):
                pe.sem_inc(full, FULL0)
                pe.sem_inc(mm, MM0)

                def turn(n, g, h):
                    if h is None:
                        pe.wait_ge(kstep, (n + 1) * G * KSTEPS)
                    else:
                        pe.wait_ge(ready, READY0 + (n * WH + h + 1) * G)
                    for c, m in enumerate(chunks):
                        q = (c if h is None else NCH * (1 + h) + c)
                        pe.wait_ge(free, n * UCH + q + 1)
                        p = pA[(g * UCH + q) % 2]
                        for s in m:
                            j, r = slots[g][s]
                            at = off[g][r] + (j - near(g, r)[0]) * P
                            to = slice((s - m[0]) * P, (s - m[0] + 1) * P)
                            if h is None:
                                last = nc.tensor.transpose(p[:].bitcast(BF16)[:, to], HB[g][:, at:at + P], identb[:])
                            else:
                                last = nc.tensor.transpose(p[:, to], A[h % 2][:, at:at + P], ident[:])
                        last.then_inc(full, 1)

                def products(n, g, hq):
                    pe.wait_ge(free, FREE0 + n * UCH + NCH * (1 + 4 * (hq + 1)))
                    pe.wait_ge(acc_out, OUT0 + (n - 1) * 2 + hq + 1)
                    order = list(range(BT)) if g == 0 else list(range(BT - 1, -1, -1))
                    order = [j for j in order if any(jj == j for jj, _ in slots[g])]
                    for j in order:
                        rs = [r for jj, r in slots[g] if jj == j]
                        s = slots[g].index((j, rs[0]))
                        for h4 in range(4):
                            h = 4 * hq + h4
                            last = nc.tensor.matmul(acc[hq][h4 * WD:(h4 + 1) * WD, rs[0] * P:(rs[-1] + 1) * P],
                                                    xb[:, j, h * WD:(h + 1) * WD],
                                                    AT[h][:, s:s + len(rs), :],
                                                    start=(j == order[0]), stop=(j == order[-1]))
                    last.then_inc(mm, 1)

                def unit(n, g, first, last):
                    turn(n, g, None)
                    for h in range(WH):
                        turn(n, g, h)
                        if h == 0 and not first:
                            products(n - 1, 1 - g, 1)
                        if h == 4:
                            if g == 0:
                                pe.wait_ge(x_in, n * 8 + 16)
                            products(n, g, 0)

                unit(0, 0, True, False)
                with pe.Fori(0, B - 1) as i:
                    unit(i * 2 + 1, 1, False, False)
                    unit(i * 2 + 2, 0, False, False)
                unit(2 * B - 1, 1, False, True)
                products(2 * B - 1, 1, 1)


def gate_and_project(nc, sem, sb, ps, io, dr, ident):
    T = 4
    N = T * P
    CHUNKS = TOKENS // N
    PARTS = 6
    wse1, wse2, wout = sb("gp_wse1", [P, KC, SE]), sb("gp_wse2", [SE, KC, P]), sb("gp_wout", [P, KC, C])
    wqkv = sb("gp_wqkv", [P, KC, 3 * C])
    bse1, bse2, hb2 = sb("gp_bse1", [SE, 1]), sb("gp_bse2", [P, KC]), sb("gp_hb2", [P, KC])
    ln_w, ln_b = sb("gp_lnw", [P, KC]), sb("gp_lnb", [P, KC])
    oT, xc = sb("gp_oT", [P, KC, N]), sb("gp_x", [P, T, C])
    s1, th, gated = sb("gp_s1", [SE, N]), sb("gp_th", [P, KC, N]), sb("gp_gated", [P, KC, N])
    so, res, y0, n1 = sb("gp_so", [P, T, C]), sb("gp_res", [P, T, C]), sb("gp_y0", [P, T, C]), sb("gp_n1", [P, T, C])
    st, mv = sb("gp_st", [P, T, 6]), sb("gp_mv", [P, T, 2])
    eps, power = sb("gp_eps", [P, T]), sb("gp_power", [P, T])
    seen = sb("gp_seen", [P, 1])
    ve, rs, vn, rs2 = (sb("gp_" + n, [P, T]) for n in ("ve", "rs", "vn", "rs2"))
    zT = sb("gp_zT", [P, KC, N])
    rest = [sb(f"gp_rest{i}", [P, N]) for i in range(2)]
    split = [sb(f"gp_split{i}", [P, 3, N], BF16) for i in range(2)]
    vb = sb("gp_v", [P, T, H, 2 * DK])
    p1, pA, pO = ps("gp_p1", [SE, N]), ps("gp_pA", [P, KC, N]), ps("gp_pO", [P, T, C])
    pQ = [ps(f"gp_pQ{i}", [P, N]) for i in range(3)]
    w_in, o_in, x_in, ones, half = (sem("gp_" + n) for n in ("w_in", "o_in", "x_in", "consts", "half_bias"))
    se1, silu1, se2, tanhed, gate, outed, silu3 = (sem("gp_" + n) for n in ("se1", "silu1", "se2", "tanh", "gated", "wout", "silu3"))
    added, stats, aggred, inv, y0d, n1d, turned, zd = (sem("gp_" + n) for n in ("added", "stats", "aggr", "rstd", "y0", "n1", "turned", "z"))
    part, hi, left, midd, lo, vd = (sem("gp_" + n) for n in ("part", "hi", "rest", "mid", "lo", "v"))
    y_out, v_out, waited = sem("gp_y_out"), sem("gp_v_out"), sem("gp_waited")
    s_out = [sem(f"gp_split_out{i}") for i in range(2)]
    INV = 6
    oT_d = dr["outT"].rearrange("(k p) n -> p k n", p=P)
    x_d = io["L0_attn_x"].rearrange("b l c -> (b l) c")
    LOADS = [(wse1[:], io["L0_attn_w_se1"].rearrange("(k p) n -> p k n", p=P)),
             (wse2[:], io["L0_attn_w_se2"].rearrange("s (k p) -> s k p", p=P)),
             (wout[:], io["L0_attn_w_out"].rearrange("(k p) n -> p k n", p=P)),
             (wqkv[:], io["L0_ffn_w_qkv"].rearrange("(k p) n -> p k n", p=P)),
             (bse1[:], io["L0_attn_b_se1"].rearrange("(s o) -> s o", o=1)),
             (bse2[:], io["L0_attn_b_se2"].rearrange("(k p) -> p k", p=P)),
             (ln_w[:], io["L0_ffn_ln1_w"].rearrange("(k p) -> p k", p=P)),
             (ln_b[:], io["L0_ffn_ln1_b"].rearrange("(k p) -> p k", p=P))]
    WAITS = 16 * len(LOADS)

    def tokens(d, i):
        return d[bass.ds(i * N, N), :].rearrange("(t p) c -> p t c", p=P)

    with nc.Block() as block, nc.allow_non_contiguous_dma(reason="per-channel vectors"):
        @block.sync
        def _(sp):
            def load_sums(i):
                sp.wait_ge(gate, i)
                sp.dma_start(oT[:], oT_d[:, :, bass.ds(i * N, N)]).then_inc(o_in, 16)

            def load_x(i):
                sp.wait_ge(added, i)
                sp.dma_start(xc[:], tokens(x_d, i)).then_inc(x_in, 16)

            def store_split(c, q):
                sp.wait_ge(lo, c * 4 + q + 1)
                dst = dr["qs"] if q < 2 else dr["ks"]
                sp.dma_start(dst.rearrange("s (k p) n -> k p s n", p=P)[q % 2, :, :, bass.ds(c * N, N)],
                             split[q % 2][:]).then_inc(s_out[q % 2], 16)

            def store_v(c):
                sp.wait_ge(vd, c * 2 + 2)
                sp.dma_start(tokens(dr["v"], c), vb[:].rearrange("p t h d -> p t (h d)")).then_inc(v_out, 16)

            def chunk(i, prev, more):
                if prev is not None:
                    store_split(prev, 0)
                if more:
                    load_sums(i + 1)
                if prev is not None:
                    store_split(prev, 1)
                    store_split(prev, 2)
                if more:
                    load_x(i + 1)
                sp.wait_ge(y0d, i * T + T)
                sp.dma_start(tokens(dr["y0"], i), y0[:]).then_inc(y_out, 16)
                if prev is not None:
                    store_split(prev, 3)
                    store_v(prev)

            load_sums(0)
            load_x(0)
            chunk(0, None, True)
            chunk(1, 0, True)
            with sp.Fori(2, CHUNKS - 1) as i:
                chunk(i, i - 1, True)
            chunk(CHUNKS - 1, CHUNKS - 2, False)
            for q in range(4):
                store_split(CHUNKS - 1, q)
            store_v(CHUNKS - 1)
            sp.wait_ge(y_out, 16 * CHUNKS)
            sp.wait_ge(v_out, 16 * CHUNKS)
            for u in range(2):
                sp.wait_ge(s_out[u], 16 * CHUNKS * 2)

        @block.scalar
        def _(a):
            for dst, src in LOADS:
                a.dma_start(dst, src).then_inc(w_in, 16)
            a.wait_ge(half, 1)

            def gate_in(i):
                a.wait_ge(se1, i + 1)
                nc.scalar.activation(s1[:], p1[:], ACT.Silu, bias=bse1[:, 0:1]).then_inc(silu1, 1)

            def gate_out(i):
                for k in range(KC):
                    a.wait_ge(se2, i * KC + k + 1)
                    nc.scalar.activation(th[:, k, :], pA[:, k, :], ACT.Tanh, bias=hb2[:, k:k + 1], scale=0.5).then_inc(tanhed, 1)

            def output(i):
                a.wait_ge(outed, i + 1)
                a.wait_ge(added, i)
                nc.scalar.activation(so[:], pO[:], ACT.Silu, scale=0.5).then_inc(silu3, 1)

            def z(i):
                a.wait_ge(turned, i + 1)
                for k in range(KC):
                    nc.scalar.activation(zT[:, k, :], pA[:, k, :], ACT.Identity, bias=ln_b[:, k:k + 1],
                                         scale=ln_w[:, k:k + 1]).then_inc(zd, 1)

            def top(c, q):
                u = q % 2
                a.wait_ge(part, c * PARTS + q + 1)
                a.wait_ge(s_out[u], (c * 2 + q // 2) * 16)
                a.activation(split[u][:, 0, :], pQ[q % 3][:], ACT.Copy, scale=DK ** -0.5 if q < 2 else 1.0).then_inc(hi, 1)
                a.wait_ge(left, c * 4 + q + 1)
                a.activation(split[u][:, 1, :], rest[u][:], ACT.Copy).then_inc(midd, 1)

            def values(c, q):
                a.wait_ge(part, c * PARTS + q + 1)
                a.wait_ge(v_out, c * 16)
                a.copy(vb[:, 2 * (q - 4):2 * (q - 4) + 2, :, 0:DK],
                       pQ[q % 3][:].rearrange("p (t h d) -> p t h d", t=2, h=H)).then_inc(vd, 1)

            def chunk(i, prev):
                gate_in(i)
                if prev is not None:
                    top(prev, 0)
                gate_out(i)
                if prev is not None:
                    top(prev, 1)
                    top(prev, 2)
                output(i)
                if prev is not None:
                    top(prev, 3)
                    values(prev, 4)
                    values(prev, 5)
                z(i)

            chunk(0, None)
            chunk(1, 0)
            with a.Fori(2, CHUNKS) as i:
                chunk(i, i - 1)
            for q in range(4):
                top(CHUNKS - 1, q)
            for q in range(4, 6):
                values(CHUNKS - 1, q)

        @block.vector
        def _(dve):
            v = nc.vector
            dve.wait_ge(w_in, WAITS)
            v.tensor_scalar(hb2[:], bse2[:], 0.5, None, ALU.mult).then_inc(half, 1)

            def remain(c, q):
                u = q % 2
                dve.wait_ge(hi, c * 4 + q + 1)
                dve.wait_ge(lo, c * 4 + q - 1) if q >= 2 else dve.wait_ge(lo, c * 4)
                v.scalar_tensor_tensor(out=rest[u][:], in0=pQ[q % 3][:], scalar=DK ** -0.5 if q < 2 else 1.0,
                                       in1=split[u][:, 0, :], op0=ALU.mult, op1=ALU.subtract).then_inc(left, 1)

            def chunk(i, prev):
                if prev is not None:
                    remain(prev, 0)
                dve.wait_ge(tanhed, i * KC + KC)
                dve.wait_ge(outed, i)
                v.scalar_tensor_tensor(out=gated[:], in0=th[:], scalar=1.0, in1=oT[:], op0=ALU.add,
                                       op1=ALU.mult).then_inc(gate, 1)
                if prev is not None:
                    remain(prev, 1)
                    remain(prev, 2)
                dve.wait_ge(silu3, i + 1)
                dve.wait_ge(x_in, i * 16 + 16)
                v.tensor_tensor(res[:], so[:], xc[:], ALU.add).then_inc(added, 1)
                dve.wait_ge(added, i + 1)
                for t in range(T):
                    v.bn_stats(st[:, t, :], res[:, t, :]).then_inc(stats, 1)
                dve.wait_ge(stats, i * T + T)
                v.tensor_copy(seen[:], st[:, T - 1, 0:1]).then_inc(waited, 1)
                for t in range(T):
                    v.bn_aggr(mv[:, t, :], st[:, t, :]).then_inc(aggred, 1)
                dve.wait_ge(inv, i * INV + 2)
                dve.wait_ge(y_out, i * 16)
                for t in range(T):
                    v.tensor_scalar(y0[:, t, :], res[:, t, :], mv[:, t, 0:1], rs[:, t:t + 1],
                                    ALU.subtract, ALU.mult).then_inc(y0d, 1)
                dve.wait_ge(inv, i * INV + INV)
                for t in range(T):
                    dve.wait_ge(y0d, i * T + t + 1)
                    v.tensor_scalar(n1[:, t, :], y0[:, t, :], rs2[:, t:t + 1], None, ALU.mult).then_inc(n1d, 1)
                if prev is not None:
                    remain(prev, 3)

            chunk(0, None)
            chunk(1, 0)
            with dve.Fori(2, CHUNKS) as i:
                chunk(i, i - 1)
            for q in range(4):
                remain(CHUNKS - 1, q)

        @block.gpsimd
        def _(pool):
            g = nc.gpsimd
            g.memset(eps[:], EPS).then_inc(ones, 1)
            g.memset(power[:], -0.5).then_inc(ones, 1)
            g.memset(vb[:, :, :, DK:2 * DK], 1.0).then_inc(ones, 1)
            pool.wait_ge(ones, 3)

            def low(c, q):
                u = q % 2
                pool.wait_ge(midd, c * 4 + q + 1)
                g.tensor_tensor(split[u][:, 2, :], rest[u][:], split[u][:, 1, :], ALU.subtract).then_inc(lo, 1)

            def chunk(i, prev):
                if prev is not None:
                    for q in range(3):
                        low(prev, q)
                c = Chain(pool, inv, i * INV)
                pool.wait_ge(aggred, i * T + T)
                pool.wait_ge(n1d, i * T)
                c.link(g.tensor_tensor(ve[:], mv[:, :, 1], eps[:], ALU.add))
                c.link(g.tensor_tensor(rs[:], ve[:], power[:], ALU.pow))
                c.link(g.tensor_tensor(vn[:], mv[:, :, 1], rs[:], ALU.mult))
                c.link(g.tensor_tensor(ve[:], vn[:], rs[:], ALU.mult))
                c.link(g.tensor_tensor(vn[:], ve[:], eps[:], ALU.add))
                c.link(g.tensor_tensor(rs2[:], vn[:], power[:], ALU.pow))
                if prev is not None:
                    low(prev, 3)

            chunk(0, None)
            chunk(1, 0)
            with pool.Fori(2, CHUNKS) as i:
                chunk(i, i - 1)
            for q in range(4):
                low(CHUNKS - 1, q)

        @block.tensor
        def _(pe):
            pe.wait_ge(w_in, WAITS)

            def parts(c, q):
                pe.wait_ge(zd, c * KC + KC)
                if q < 3:
                    pe.wait_ge(vd, c * 2)
                    pe.wait_ge(left, c * 4)
                else:
                    pe.wait_ge(left, c * 4 + q - 2)
                if q < 4:
                    for k in range(KC):
                        last = nc.tensor.matmul(pQ[q % 3][:], wqkv[:, k, q * P:(q + 1) * P], zT[:, k, :],
                                                start=(k == 0), stop=(k == KC - 1))
                else:
                    for t in range(2):
                        for k in range(KC):
                            tile = 2 * (q - 4) + t
                            last = nc.tensor.matmul(pQ[q % 3][:, t * C:(t + 1) * C], zT[:, k, tile * P:(tile + 1) * P],
                                                    wqkv[:, k, 2 * C:3 * C], start=(k == 0), stop=(k == KC - 1))
                last.then_inc(part, 1)

            def chunk(i, prev):
                pe.wait_ge(o_in, i * 16 + 16)
                pe.wait_ge(silu1, i)
                for k in range(KC):
                    last = nc.tensor.matmul(p1[:], wse1[:, k, :], oT[:, k, :], start=(k == 0), stop=(k == KC - 1))
                last.then_inc(se1, 1)
                if prev is not None:
                    parts(prev, 0)
                pe.wait_ge(silu1, i + 1)
                pe.wait_ge(zd, i * KC)
                for k in range(KC):
                    nc.tensor.matmul(pA[:, k, :], wse2[:, k, :], s1[:], start=True, stop=True).then_inc(se2, 1)
                if prev is not None:
                    parts(prev, 1)
                    parts(prev, 2)
                pe.wait_ge(gate, i + 1)
                pe.wait_ge(silu3, i)
                for t in range(T):
                    for k in range(KC):
                        last = nc.tensor.matmul(pO[:, t, :], gated[:, k, t * P:(t + 1) * P], wout[:, k, :],
                                                start=(k == 0), stop=(k == KC - 1))
                last.then_inc(outed, 1)
                if prev is not None:
                    for q in range(3, PARTS):
                        parts(prev, q)
                pe.wait_ge(tanhed, i * KC + KC)
                for t in range(T):
                    pe.wait_ge(n1d, i * T + t + 1)
                    for k in range(KC):
                        last = nc.tensor.transpose(pA[:, k, t * P:(t + 1) * P], n1[:, t, k * P:(k + 1) * P], ident[:])
                last.then_inc(turned, 1)

            chunk(0, None)
            chunk(1, 0)
            with pe.Fori(2, CHUNKS) as i:
                chunk(i, i - 1)
            for q in range(PARTS):
                parts(CHUNKS - 1, q)


def attention(nc, sem, sb, ps, io, dr, ident, w1, w2, w_in):
    UNITS = B * QUADS
    STACK = [(0, 0), (0, 1), (1, 0), (1, 1), (0, 2), (2, 0)]
    ROWS = DK * len(STACK)
    FULL = ROWS + 3
    HALF = 512
    STEPS_ = 2 * BT
    PIECES = 4 * BT
    PV0, RED0 = 2, 2
    LOADS = 2 * len(STACK) * 16

    qst = [sb(f"at_q{i}", [FULL, 4, L], BF16) for i in range(2)]
    kst = [sb(f"at_k{i}", [FULL, 4, L], BF16) for i in range(2)]
    vst = [sb(f"at_v{i}", [P, BT, 4, 2 * DK]) for i in range(2)]
    pt = [sb(f"at_p{i}", [P, 2, HALF]) for i in range(4)]
    mx, top_ = sb("at_mx", [P, PIECES, 2]), sb("at_top", [P, PIECES])
    tail = sb("at_tail", [PIECES, P])
    top3 = [sb(f"at_top3{i}", [PIECES, 3, P], BF16) for i in range(2)]
    oe = sb("at_oe", [P, HALF])
    rden, yn = sb("at_rden", [P, 4, 4]), [sb(f"at_yn{i}", [P, 4, 4, DK]) for i in range(2)]
    pst = [ps(f"at_pst{i}", [P, 2, HALF]) for i in range(2)]
    pmx = [ps(f"at_pmx{i}", [P, HALF]) for i in range(2)]
    pacc, pm = ps("at_pacc", [P, HALF]), ps("at_pm", [P, 4, 4, 2 * DK])
    one_rows = sem("at_ones")
    ld = [[sem(f"at_load{i}{j}") for j in range(2)] for i in range(2)]
    v_in = [sem(f"at_v_in{i}") for i in range(2)]
    scored, exped, pv, red, mxmm = (sem("at_" + n) for n in ("scored", "exp", "pv", "reduced", "maxima"))
    topped, topT, split, rows_in, oed, oT, yd, rd = (sem("at_" + n) for n in ("top", "topT", "top_split", "top_rows", "acc_out", "outT", "y", "rden"))
    y_out = [sem(f"at_y_out{i}") for i in range(2)]
    TOPS = 4

    with nc.Block() as block:
        TOPSTEP = 14

        def plan(s):
            at = [min(2 * PIECES, 2 * PIECES * k // 13) for k in range(STEPS_ + 1)]
            return range(at[s - 1], at[s]) if s else range(0)

        def both(eng, unit, start):
            start()
            unit(0, 0, 0, True)
            unit(1, 0, 1, True)
            with eng.Fori(1, UNITS // 2 - 1) as j:
                for u in range(2):
                    unit(j * 2 + u, j, u, True)
            j = UNITS // 2 - 1
            unit(j * 2, j, 0, True)
            unit(j * 2 + 1, j, 1, False)

        @block.sync
        def _(sp):
            def load(w, j, u):
                b, q = j // 2, (j % 2) * 2 + u
                def part(d, n, h2):
                    return d[n, bass.ds(q * (4 * DK) + h2 * 2 * DK, 2 * DK), bass.ds(b * L, L)].rearrange("(h d) n -> d h n", d=DK)
                for h2 in range(2):
                    for n, (pq, pk) in enumerate(STACK):
                        rows = slice(n * DK, (n + 1) * DK)
                        sp.dma_start(qst[u][rows, 2 * h2:2 * h2 + 2, :], part(dr["qs"], pq, h2)).then_inc(ld[u][h2], 16)
                        sp.dma_start(kst[u][rows, 2 * h2:2 * h2 + 2, :], part(dr["ks"], pk, h2)).then_inc(ld[u][h2], 16)
                sp.dma_start(vst[u][:].rearrange("p t h d -> p t (h d)"),
                             dr["v"][bass.ds(b * L, L), bass.ds(q * (8 * DK), 8 * DK)].rearrange("(t p) n -> p t n", p=P)).then_inc(v_in[u], 16)

            def store_top(w, u):
                sp.wait_ge(split, w * TOPS + TOPS)
                for n in range(3):
                    sp.dma_start(qst[u][ROWS + n:ROWS + n + 1, :, :].rearrange("o h (t n) -> o (h t) n", t=BT),
                                 top3[u][:, n, :]).then_inc(rows_in, 16)

            def store_y(w, j, u, half):
                b, q = j // 2, (j % 2) * 2 + u
                sp.wait_ge(yd, w * 2 + half + 1)
                sp.dma_start(dr["Y"][bass.ds(b * L + half * HALF, HALF), bass.ds(q * (4 * DK), 4 * DK)].rearrange("(t p) c -> p t c", p=P),
                             yn[half][:].rearrange("p t h d -> p t (h d)")).then_inc(y_out[half], 16)

            def unit(w, j, u, more):
                if more:
                    sp.wait_ge(pv, PV0 + w * STEPS_)
                    load(w + 1, j + u, 1 - u)
                sp.dma_start(w1[:, u, bass.ds(j, 1), :], io["L0_ffn_w1"][bass.ds(j, 1), u * P:(u + 1) * P, :].rearrange("e p n -> p e n")).then_inc(w_in, 16)
                hc = HID // P // 2
                sp.dma_start(w2[:, u * hc:(u + 1) * hc, bass.ds(j, 1), :],
                             io["L0_ffn_w2"][bass.ds(j, 1), u * hc * P:(u + 1) * hc * P, :].rearrange("e (t p) n -> p t e n", p=P)).then_inc(w_in, 16)
                store_y(w, j, u, 0)
                if more:
                    store_top(w + 1, 1 - u)
                store_y(w, j, u, 1)

            def start():
                load(0, 0, 0)
                store_top(0, 0)

            both(sp, unit, start)
            for half in range(2):
                sp.wait_ge(y_out[half], 16 * UNITS)
            sp.wait_ge(w_in, 16 * 2 * UNITS)

        @block.gpsimd
        def _(pool):
            for k in kst:
                nc.gpsimd.memset(k[ROWS:FULL, :, :], 1.0).then_inc(one_rows, 1)

        @block.scalar
        def _(a):
            def unit(w, j, u, more):
                for s in range(STEPS_):
                    for p in range(2):
                        a.wait_ge(scored, w * (2 * STEPS_) + 2 * s + p + 1)
                        a.wait_ge(pv, w * STEPS_ + s + 1)
                        a.activation(pt[(2 * s + p) % 4][:], pst[p][:], ACT.Exp).then_inc(exped, 1)
                    if s == BT:
                        out(w, 0)
                out(w, 1)

            def out(w, half):
                a.wait_ge(pv, PV0 + w * STEPS_ + (half + 1) * BT)
                a.wait_ge(oT, w * 2 + half)
                a.copy(oe[:], pacc[:]).then_inc(oed, 1)

            both(a, unit, lambda: None)

        @block.vector
        def _(dve):
            v = nc.vector

            def maximum(w, m):
                i, kh = m // 2, m % 2
                dve.wait_ge(mxmm, w * (2 * PIECES) + m + 1)
                v.reduce_max(mx[:, i, kh:kh + 1], pmx[kh][:], AX.X).then_inc(red, 1)

            def tops(w, u):
                dve.wait_ge(red, RED0 + (w + 1) * 2 * PIECES)
                v.tensor_tensor(top_[:], mx[:, :, 0], mx[:, :, 1], ALU.max).then_inc(topped, 1)

            def split_tops(w, u):
                c = Chain(dve, split, w * TOPS)
                t = top3[u]
                negT = pm[0:PIECES, 0, :, :].rearrange("p h d -> p (h d)")
                dve.wait_ge(topT, w + 1)
                c.link(v.tensor_scalar(t[:, 0, :], negT, -1.0, None, ALU.mult))
                c.link(v.scalar_tensor_tensor(out=tail[:], in0=negT, scalar=-1.0, in1=t[:, 0, :], op0=ALU.mult, op1=ALU.subtract))
                c.link(v.tensor_copy(t[:, 1, :], tail[:]))
                c.did(v.tensor_tensor(t[:, 2, :], tail[:], t[:, 1, :], ALU.subtract))
                assert c.n == TOPS

            def normalise(w, half):
                dve.wait_ge(oT, w * 2 + half + 1)
                v.reciprocal(rden[:], pm[:, :, :, DK]).then_inc(rd, 1)
                dve.wait_ge(rd, w * 2 + half + 1)
                dve.wait_ge(y_out[half], w * 16)
                v.tensor_tensor(yn[half][:], pm[:, :, :, 0:DK], rden[:].unsqueeze(3).to_broadcast([P, 4, 4, DK]),
                                ALU.mult).then_inc(yd, 1)

            def unit(w, j, u, more):
                for s in range(STEPS_):
                    if more:
                        for m in plan(s):
                            maximum(w + 1, m)
                    if s == BT + 1:
                        normalise(w, 0)
                    if s == TOPSTEP and more:
                        tops(w + 1, 1 - u)
                        split_tops(w + 1, 1 - u)
                normalise(w, 1)

            def start():
                dve.sem_inc(red, RED0)
                for m in range(2 * PIECES):
                    maximum(0, m)
                tops(0, 0)
                split_tops(0, 0)

            both(dve, unit, start)

        @block.tensor
        def _(pe):
            def maximum(w, u, m, loaded):
                i, kh = m // 2, m % 2
                h, nt = i // BT, i % BT
                if m % (4 * BT) == 0:
                    pe.wait_ge(ld[u][h // 2], loaded)
                pe.wait_ge(red, w * (2 * PIECES) + m + 1)
                nc.tensor.matmul(pmx[kh][:], qst[u][0:ROWS, h, nt * P:(nt + 1) * P],
                                 kst[u][0:ROWS, h, kh * HALF:(kh + 1) * HALF], start=True, stop=True).then_inc(mxmm, 1)

            def turn_tops(w):
                pe.wait_ge(topped, w + 1)
                nc.tensor.transpose(pm[0:PIECES, 0, :, :].rearrange("p h d -> p (h d)"), top_[:], ident[:]).then_inc(topT, 1)

            def turn_out(w, half):
                pe.wait_ge(yd, w * 2 + half)
                pe.wait_ge(oed, w * 2 + half + 1)
                pmf = pm[:].rearrange("p t h d -> p t (h d)")
                for t in range(4):
                    last = nc.tensor.transpose(pmf[:, t, :], oe[:, t * P:(t + 1) * P], ident[:])
                last.then_inc(oT, 1)

            def scores(w, u, s, p):
                half, mt = s // BT, s % BT
                pe.wait_ge(exped, w * (2 * STEPS_) + 2 * s + p - 1) if s else pe.wait_ge(exped, w * (2 * STEPS_))
                for n in range(2):
                    h = 2 * p + n
                    last = nc.tensor.matmul(pst[p][:, n, :], kst[u][:, h, mt * P:(mt + 1) * P],
                                            qst[u][:, h, half * HALF:(half + 1) * HALF], start=True, stop=True)
                last.then_inc(scored, 1)

            def values(w, u, s):
                mt = s % BT
                pe.wait_ge(exped, w * (2 * STEPS_) + 2 * s + 2)
                if mt == 0:
                    pe.wait_ge(oed, w * 2 + s // BT)
                for h in range(4):
                    last = nc.tensor.matmul(pacc[h * 2 * DK:(h + 1) * 2 * DK, :], vst[u][:, mt, h, :],
                                            pt[(2 * s + h // 2) % 4][:, h % 2, :], start=(mt == 0), stop=(mt == BT - 1))
                last.then_inc(pv, 1)

            def unit(w, j, u, more):
                pe.wait_ge(rows_in, (w + 1) * 48)
                pe.wait_ge(v_in[u], (j + 1) * 16)
                for s in range(STEPS_):
                    ms = list(plan(s)) if more else []
                    scores(w, u, s, 0)
                    for m in ms[0:1]:
                        maximum(w + 1, 1 - u, m, (j + u + 1) * LOADS)
                    scores(w, u, s, 1)
                    for m in ms[1:2]:
                        maximum(w + 1, 1 - u, m, (j + u + 1) * LOADS)
                    if s:
                        values(w, u, s - 1)
                    for m in ms[2:]:
                        maximum(w + 1, 1 - u, m, (j + u + 1) * LOADS)
                    if s == BT + 1:
                        turn_out(w, 0)
                    if s == TOPSTEP and more:
                        pe.wait_ge(yd, w * 2 + 1)
                        turn_tops(w + 1)
                values(w, u, STEPS_ - 1)
                if more:
                    pe.wait_ge(split, (w + 1) * TOPS + 2)
                turn_out(w, 1)

            def start():
                pe.sem_inc(pv, PV0)
                pe.wait_ge(one_rows, 2)
                for m in range(2 * PIECES):
                    maximum(0, 0, m, LOADS)
                turn_tops(0)

            both(pe, unit, start)


def project_and_gate(nc, sem, sb, ps, io, dr, ident, n2, logits):
    T = 4
    N = T * P
    CHUNKS = TOKENS // N
    INV = 2
    wp, gw, gb = sb("pg_wproj", [P, KC, C]), sb("pg_gw", [P, KC, E]), sb("pg_gb", [P, E])
    ln_w, ln_b = sb("pg_lnw", [P, KC]), sb("pg_lnb", [P, KC])
    yc, y0 = sb("pg_y", [P, T, C]), sb("pg_y0", [P, T, C])
    yT, zT = sb("pg_yT", [P, KC, N]), sb("pg_zT", [P, KC, N])
    x3 = sb("pg_x3", [P, T, C])
    x2, nc2 = sb("pg_x2", [P, T, C]), sb("pg_n2", [P, T, C])
    st, mv, seen = sb("pg_st", [P, T, 6]), sb("pg_mv", [P, T, 2]), sb("pg_seen", [P, 1])
    eps, power, ve, rs = (sb("pg_" + n, [P, T]) for n in ("eps", "power", "ve", "rs"))
    zero = sb("pg_zero", [P, C])
    pY, pO, pN, pG = ps("pg_pY", [P, KC, N]), ps("pg_pO", [P, T, C]), ps("pg_pN", [P, KC, N]), ps("pg_pG", [P, T, E])
    kept, summed = sem("pg_kept"), sem("pg_summed")
    w_in, y_in, y0_in, consts, zeroed = (sem("pg_" + n) for n in ("w_in", "y_in", "y0_in", "consts", "zeroed"))
    turned, yTd, outed, added, stats, waited, aggred, inv, n2d, nT, zd, gated, logd, x3_out = (sem("pg_" + n) for n in (
        "turned", "yT", "projected", "added", "stats", "waited", "aggr", "rstd", "n2", "n2T", "zT", "gate", "logits", "x3_out"))
    LOADS = [(wp[:], io["L0_ffn_w_proj"].rearrange("(k p) n -> p k n", p=P)),
             (gw[:], io["L0_ffn_gate_w"].rearrange("(k p) n -> p k n", p=P)),
             (gb[:], io["L0_ffn_gate_b"].rearrange("(o n) -> o n", o=1).to_broadcast([P, E])),
             (ln_w[:], io["L0_ffn_ln2_w"].rearrange("(k p) -> p k", p=P)),
             (ln_b[:], io["L0_ffn_ln2_b"].rearrange("(k p) -> p k", p=P))]
    WAITS = 16 * len(LOADS)

    def tokens(d, i):
        return d[bass.ds(i * N, N), :].rearrange("(t p) c -> p t c", p=P)

    def skewed(eng, chunk):
        chunk(0, None)
        chunk(1, 0)
        with eng.Fori(2, CHUNKS) as i:
            chunk(i, i - 1)
        chunk(None, CHUNKS - 1)

    with nc.Block() as block, nc.allow_non_contiguous_dma(reason="per-channel vectors"):
        @block.sync
        def _(sp):
            def each(i):
                sp.wait_ge(turned, i)
                sp.dma_start(yc[:], tokens(dr["Y"], i)).then_inc(y_in, 16)
                sp.wait_ge(summed, i)
                sp.dma_start(y0[:], tokens(dr["y0"], i)).then_inc(y0_in, 16)

            each(0)
            with sp.Fori(1, CHUNKS) as i:
                each(i)
            sp.wait_ge(consts, 3)
            sp.dma_start(dr["zs"].rearrange("(t p) c -> p t c", p=P),
                         zero[:].unsqueeze(1).to_broadcast([P, MT, C])).then_inc(zeroed, 16)
            sp.wait_ge(zeroed, 16)

        @block.gpsimd
        def _(pool):
            g = nc.gpsimd
            g.memset(eps[:], EPS).then_inc(consts, 1)
            g.memset(power[:], -0.5).then_inc(consts, 1)
            g.memset(zero[:], 0.0).then_inc(consts, 1)
            pool.wait_ge(consts, 3)
            def each(i):
                pool.wait_ge(added, i + 1)
                pool.wait_ge(x3_out, i * 16)
                g.tensor_tensor(x3[:], x2[:], y0[:], ALU.add).then_inc(summed, 1)
                c = Chain(pool, inv, i * INV)
                pool.wait_ge(aggred, i * T + T)
                pool.wait_ge(n2d, i * T)
                c.link(g.tensor_tensor(ve[:], mv[:, :, 1], eps[:], ALU.add))
                c.link(g.tensor_tensor(rs[:], ve[:], power[:], ALU.pow))
                assert c.n == INV

            each(0)
            with pool.Fori(1, CHUNKS) as i:
                each(i)

        @block.scalar
        def _(a):
            for dst, src in LOADS:
                a.dma_start(dst, src).then_inc(w_in, 16)

            def chunk(i, prev):
                if i is not None:
                    a.wait_ge(turned, i + 1)
                    a.wait_ge(outed, i)
                    a.copy(yT[:], pY[:]).then_inc(yTd, 1)
                if prev is not None:
                    a.wait_ge(nT, prev + 1)
                    a.wait_ge(gated, prev)
                    a.wait_ge(w_in, WAITS)
                    for k in range(KC):
                        a.activation(zT[:, k, :], pN[:, k, :], ACT.Identity, bias=ln_b[:, k:k + 1],
                                     scale=ln_w[:, k:k + 1]).then_inc(zd, 1)
                if i is not None:
                    a.wait_ge(summed, i + 1)
                    a.dma_start(tokens(dr["x3"], i), x3[:]).then_inc(x3_out, 16)
                    a.wait_ge(n2d, i * T + T)
                    a.copy(n2[:, bass.ds(i * T, T), :], nc2[:]).then_inc(kept, 1)

            a.wait_ge(w_in, WAITS)
            chunk(0, None)
            chunk(1, 0)
            with a.Fori(2, CHUNKS) as i:
                chunk(i, i - 1)
            chunk(None, CHUNKS - 1)
            a.wait_ge(x3_out, 16 * CHUNKS)

        @block.vector
        def _(dve):
            v = nc.vector
            dve.wait_ge(w_in, WAITS)

            def chunk(i, prev):
                if i is not None:
                    dve.wait_ge(outed, i + 1)
                    dve.wait_ge(y0_in, i * 16 + 16)
                    dve.wait_ge(summed, i)
                    v.tensor_tensor(x2[:], pO[:], y0[:], ALU.add).then_inc(added, 1)
                    dve.wait_ge(added, i + 1)
                    for t in range(T):
                        v.bn_stats(st[:, t, :], x2[:, t, :]).then_inc(stats, 1)
                    dve.wait_ge(stats, i * T + T)
                    v.tensor_copy(seen[:], st[:, T - 1, 0:1]).then_inc(waited, 1)
                    for t in range(T):
                        v.bn_aggr(mv[:, t, :], st[:, t, :]).then_inc(aggred, 1)
                if prev is not None:
                    dve.wait_ge(gated, prev + 1)
                    v.tensor_tensor(logits[:, bass.ds(prev * T, T), :], pG[:], gb[:].unsqueeze(1).to_broadcast([P, T, E]),
                                    ALU.add).then_inc(logd, 1)
                if i is not None:
                    dve.wait_ge(inv, i * INV + INV)
                    dve.wait_ge(nT, i)
                    dve.wait_ge(kept, i)
                    for t in range(T):
                        v.tensor_scalar(nc2[:, t, :], x2[:, t, :], mv[:, t, 0:1], rs[:, t:t + 1],
                                        ALU.subtract, ALU.mult).then_inc(n2d, 1)

            skewed(dve, chunk)

        @block.tensor
        def _(pe):
            pe.wait_ge(w_in, WAITS)

            def chunk(i, prev):
                if i is not None:
                    pe.wait_ge(y_in, i * 16 + 16)
                    pe.wait_ge(yTd, i)
                    for t in range(T):
                        for k in range(KC):
                            last = nc.tensor.transpose(pY[:, k, t * P:(t + 1) * P], yc[:, t, k * P:(k + 1) * P], ident[:])
                    last.then_inc(turned, 1)
                if prev is not None:
                    pe.wait_ge(zd, prev * KC)
                    pe.wait_ge(n2d, prev * T + T)
                    for t in range(T):
                        for k in range(KC):
                            last = nc.tensor.transpose(pN[:, k, t * P:(t + 1) * P], nc2[:, t, k * P:(k + 1) * P], ident[:])
                    last.then_inc(nT, 1)
                if i is not None:
                    pe.wait_ge(yTd, i + 1)
                    pe.wait_ge(added, i)
                    for t in range(T):
                        for k in range(KC):
                            last = nc.tensor.matmul(pO[:, t, :], yT[:, k, t * P:(t + 1) * P], wp[:, k, :],
                                                    start=(k == 0), stop=(k == KC - 1))
                    last.then_inc(outed, 1)
                if prev is not None:
                    pe.wait_ge(zd, prev * KC + KC)
                    pe.wait_ge(logd, prev)
                    for t in range(T):
                        for k in range(KC):
                            last = nc.tensor.matmul(pG[:, t, :], zT[:, k, t * P:(t + 1) * P], gw[:, k, :],
                                                    start=(k == 0), stop=(k == KC - 1))
                    last.then_inc(gated, 1)

            skewed(pe, chunk)


def dispatch(nc, sem, sb, ps, dr, n2, logits, slot, expert):
    top1, m8, first = sb("ds_max", [P, TILES]), sb("ds_m8", [P, TILES, E]), sb("ds_first", [P, TILES])
    eq, hot = sb("ds_eq", [P, TILES, E]), sb("ds_hot", [P, TILES, E])
    es, back = sb("ds_es", [P, E]), sb("ds_back", [P, E])
    lower, ones = sb("ds_lower", [P, P]), sb("ds_ones", [P, P])
    run = [sb(f"ds_run{i}", [P, TILES, E]) for i in range(2)]
    tot = sb("ds_tot", [P, TILES, E])
    cum = [sb(f"ds_cum{i}", [P, E]) for i in range(2)]
    tiles, start = sb("ds_tiles", [P, E]), sb("ds_start", [P, E])
    slotf = sb("ds_slotf", [P, TILES])
    js, past, exf = sb("ds_js", [1, MT]), sb("ds_past", [1, MT, E]), sb("ds_exf", [1, MT])
    pW, pT = ps("ds_pW", [P, TILES * E]), ps("ds_pT", [P, TILES * E])
    consts, d, hotd, counted, placed, sent = (sem("ds_" + n) for n in ("consts", "dve", "hot", "counted", "placed", "sent"))
    MAGIC = 1.5 * 2.0 ** 23

    with nc.Block() as block:
        @block.gpsimd
        def _(pool):
            g = nc.gpsimd
            g.iota(es[:], pattern=[[1, E]], base=0, channel_multiplier=0, allow_small_or_imprecise_dtypes=True).then_inc(consts, 1)
            g.iota(back[:], pattern=[[-1, E]], base=E, channel_multiplier=0, allow_small_or_imprecise_dtypes=True).then_inc(consts, 1)
            g.iota(js[:], pattern=[[1, MT]], base=0, channel_multiplier=0, allow_small_or_imprecise_dtypes=True).then_inc(consts, 1)
            g.memset(ones[:], 1.0).then_inc(consts, 1)
            pool.wait_ge(consts, 4)
            g.affine_select(out=lower[:], in_=ones[:], compare_op=ALU.is_gt, fill=0.0, base=0,
                            pattern=[[1, P]], channel_multiplier=-1).then_inc(consts, 1)
            pool.wait_ge(placed, 1)
            for t in range(TILES):
                pool.indirect_dma_start(out=dr["zs"], out_offset=bass.IndirectOffsetOnAxis(ap=slot[:, t:t + 1], axis=0),
                                        in_=n2[:, t, :], in_offset=None).then_inc(sent, 16)
            pool.wait_ge(sent, 16 * TILES)

        @block.tensor
        def _(pe):
            pe.wait_ge(consts, 5)
            pe.wait_ge(hotd, 1)
            h = hot[:].rearrange("p t e -> p (t e)")
            nc.tensor.matmul(pW[:], lower[:], h, start=True, stop=True)
            nc.tensor.matmul(pT[:], ones[:], h, start=True, stop=True).then_inc(counted, 1)

        @block.vector
        def _(dve):
            v = nc.vector
            c = Chain(dve, d)

            def over(a):
                return a[:].unsqueeze(2).to_broadcast([P, TILES, E])

            def row(a):
                return a[:].unsqueeze(1).to_broadcast([P, TILES, E])

            dve.wait_ge(consts, 5)
            c.link(v.tensor_reduce(top1[:], logits[:], AX.X, ALU.max))
            c.link(v.tensor_tensor(eq[:], logits[:], over(top1), ALU.is_equal))
            c.link(v.tensor_tensor(m8[:], eq[:], row(back), ALU.mult))
            c.link(v.tensor_reduce(first[:], m8[:], AX.X, ALU.max))
            v.tensor_tensor(hot[:], over(first), row(back), ALU.is_equal).then_inc(hotd, 1)
            dve.wait_ge(counted, 1)
            c.did(v.tensor_copy(tot[:].rearrange("p t e -> p (t e)"), pT[:]))
            c.link(v.tensor_copy(run[0][:].rearrange("p t e -> p (t e)"), pT[:]))
            u, n = 0, 1
            while n < TILES:
                c.did(v.tensor_copy(run[1 - u][:, 0:n, :], run[u][:, 0:n, :]))
                c.link(v.tensor_tensor(run[1 - u][:, n:, :], run[u][:, n:, :], run[u][:, :TILES - n, :], ALU.add))
                u, n = 1 - u, 2 * n
            c.link(v.tensor_scalar(tiles[:], run[u][:, TILES - 1, :], 1.0 / P, 127.0 / P - 0.5 + 1.0 / 256, ALU.mult, ALU.add))
            c.link(v.tensor_scalar(tiles[:], tiles[:], MAGIC, MAGIC, ALU.add, ALU.subtract))
            c.link(v.tensor_copy(cum[0][:], tiles[:]))
            w, n = 0, 1
            while n < E:
                c.did(v.tensor_copy(cum[1 - w][:, 0:n], cum[w][:, 0:n]))
                c.link(v.tensor_tensor(cum[1 - w][:, n:], cum[w][:, n:], cum[w][:, :E - n], ALU.add))
                w, n = 1 - w, 2 * n
            c.link(v.tensor_tensor(start[:], cum[w][:], tiles[:], ALU.subtract))
            c.link(v.tensor_scalar(start[:], start[:], float(P), None, ALU.mult))
            c.link(v.tensor_tensor(run[u][:], run[u][:], tot[:], ALU.subtract))
            c.link(v.tensor_tensor(tot[:].rearrange("p t e -> p (t e)"), pW[:], run[u][:].rearrange("p t e -> p (t e)"), ALU.add))
            c.link(v.tensor_tensor(run[u][:], tot[:], row(start), ALU.add))
            c.link(v.tensor_tensor(tot[:], run[u][:], hot[:], ALU.mult))
            c.link(v.reduce_sum(slotf[:], tot[:], AX.X))
            v.tensor_copy(slot[:], slotf[:]).then_inc(placed, 1)
            c.link(v.tensor_tensor(past[:], js[:].unsqueeze(2).to_broadcast([1, MT, E]),
                                   cum[w][0:1, :].unsqueeze(1).to_broadcast([1, MT, E]), ALU.is_ge))
            c.link(v.reduce_sum(exf[:], past[:], AX.X))
            c.link(v.tensor_scalar(exf[:], exf[:], float(E - 1), None, ALU.min))
            c.link(v.tensor_copy(expert[:], exf[:]))


def experts(nc, sem, sb, ps, io, dr, ident, w1, w2, expert):
    HC = HID // P
    ln_w, ln_b = sb("ex_lnw", [P, KC]), sb("ex_lnb", [P, KC])
    z = [sb(f"ex_z{i}", [P, C]) for i in range(2)]
    zT = sb("ex_zT", [P, KC, P])
    hs, hT, ys = sb("ex_h", [P, HID]), sb("ex_hT", [P, HC, P]), sb("ex_y", [P, C])
    pZ, pH, pT, pY = ps("ex_pZ", [P, KC, P]), ps("ex_pH", [P, HID]), ps("ex_pT", [P, HC, P]), ps("ex_pY", [P, C])
    w_in, z_in, turned, zd, up, gelu, hturned, hTd, down, yd, y_out = (sem("ex_" + n) for n in (
        "w_in", "z_in", "turned", "zT", "up", "gelu", "h_turned", "hT", "down", "y", "y_out"))

    def skewed(eng, tile):
        tile(0, None, True)
        tile(1, 0, True)
        with eng.Fori(2, MT - 1) as j:
            tile(j, j - 1, True)
        tile(MT - 1, MT - 2, False)
        tile(None, MT - 1, False)

    with nc.Block() as block, nc.allow_non_contiguous_dma(reason="per-channel vectors"):
        @block.sync
        def _(sp):
            sp.dma_start(ln_w[:], io["L0_ffn_ln2_w"].rearrange("(k p) -> p k", p=P)).then_inc(w_in, 16)
            sp.dma_start(ln_b[:], io["L0_ffn_ln2_b"].rearrange("(k p) -> p k", p=P)).then_inc(w_in, 16)

            def load(j):
                sp.wait_ge(turned, j)
                sp.dma_start(z[0][:], dr["zs"][bass.ds(j * P, P), :]).then_inc(z_in, 16)

            def tile(j, prev, more):
                if more:
                    load(j + 1)
                if prev is not None:
                    sp.wait_ge(yd, prev + 1)
                    sp.dma_start(dr["ys"][bass.ds(prev * P, P), :], ys[:]).then_inc(y_out, 16)

            load(0)
            skewed(sp, tile)
            sp.wait_ge(y_out, 16 * MT)

        @block.scalar
        def _(a):
            a.wait_ge(w_in, 32)

            def norm(j):
                a.wait_ge(turned, j + 1)
                a.wait_ge(up, j)
                for k in range(KC):
                    a.activation(zT[:, k, :], pZ[:, k, :], ACT.Identity, bias=ln_b[:, k:k + 1], scale=ln_w[:, k:k + 1]).then_inc(zd, 1)

            def tile(j, prev, more):
                if j is not None:
                    a.wait_ge(up, j + 1)
                    a.wait_ge(hturned, j)
                    a.activation(hs[:], pH[:], ACT.Gelu_apprx_tanh).then_inc(gelu, 1)
                if prev is not None:
                    a.wait_ge(down, prev + 1)
                    a.wait_ge(y_out, prev * 16)
                    a.copy(ys[:], pY[:]).then_inc(yd, 1)
                if more:
                    norm(j + 1)

            norm(0)
            skewed(a, tile)

        @block.vector
        def _(dve):
            def each(j):
                dve.wait_ge(hturned, j + 1)
                dve.wait_ge(down, j)
                nc.vector.tensor_copy(hT[:], pT[:]).then_inc(hTd, 1)

            each(0)
            with dve.Fori(1, MT) as j:
                each(j)

        @block.tensor
        def _(pe):
            def turn(j):
                pe.wait_ge(z_in, j * 16 + 16)
                pe.wait_ge(zd, j * KC)
                for k in range(KC):
                    last = nc.tensor.transpose(pZ[:, k, :], z[0][:, k * P:(k + 1) * P], ident[:])
                last.then_inc(turned, 1)

            def which(j):
                return pe.value_load(expert[0:1, bass.ds(j, 1)], min_val=0, max_val=E - 1)

            def tile(j, prev, more):
                if j is not None:
                    e = which(j)
                    pe.wait_ge(zd, j * KC + KC)
                    pe.wait_ge(gelu, j)
                    for n in range(HID // 512):
                        for k in range(KC):
                            last = nc.tensor.matmul(pH[:, n * 512:(n + 1) * 512], zT[:, k, :],
                                                    w1[:, k, bass.ds(e, 1), n * 512:(n + 1) * 512], start=(k == 0), stop=(k == KC - 1))
                    last.then_inc(up, 1)
                if more:
                    turn(j + 1)
                if prev is not None:
                    e = which(prev)
                    pe.wait_ge(hTd, prev + 1)
                    pe.wait_ge(yd, prev)
                    for c in range(HC):
                        last = nc.tensor.matmul(pY[:], hT[:, c, :], w2[:, c, bass.ds(e, 1), :], start=(c == 0), stop=(c == HC - 1))
                    last.then_inc(down, 1)
                if j is not None:
                    pe.wait_ge(gelu, j + 1)
                    pe.wait_ge(hTd, j)
                    for c in range(HC):
                        last = nc.tensor.transpose(pT[:, c, :], hs[:, c * P:(c + 1) * P], ident[:])
                    last.then_inc(hturned, 1)

            turn(0)
            skewed(pe, tile)


def combine(nc, sem, sb, io, dr, slot):
    T = 4
    N = T * P
    CHUNKS = TOKENS // N
    g_, x2, xo = ([sb(f"cb_{n}{i}", [P, T, C]) for i in range(2)] for n in ("g", "x2", "out"))
    st, mv, seen = sb("cb_st", [P, T, 6]), sb("cb_mv", [P, T, 2]), sb("cb_seen", [P, 1])
    eps, power, ve, rs = (sb("cb_" + n, [P, T]) for n in ("eps", "power", "ve", "rs"))
    consts, added, stats, waited, aggred, inv, outd = (sem("cb_" + n) for n in ("consts", "added", "stats", "waited", "aggr", "rstd", "out"))
    g_in, x_in, o_out = ([sem(f"cb_{n}{i}") for i in range(2)] for n in ("g_in", "x_in", "o_out"))
    out = io["out"].rearrange("b l c -> (b l) c")

    def tokens(d, i):
        return d[i * N:(i + 1) * N, :].rearrange("(t p) c -> p t c", p=P)

    with nc.Block() as block:
        @block.gpsimd
        def _(pool):
            nc.gpsimd.memset(eps[:], EPS).then_inc(consts, 1)
            nc.gpsimd.memset(power[:], -0.5).then_inc(consts, 1)
            pool.wait_ge(consts, 2)

            def gather(i):
                if i >= 2:
                    pool.wait_ge(added, i - 1)
                for t in range(T):
                    pool.indirect_dma_start(out=g_[i % 2][:, t, :], out_offset=None, in_=dr["ys"],
                                            in_offset=bass.IndirectOffsetOnAxis(ap=slot[:, i * T + t:i * T + t + 1], axis=0)
                                            ).then_inc(g_in[i % 2], 16)

            gather(0)
            for i in range(CHUNKS):
                if i + 1 < CHUNKS:
                    gather(i + 1)
                pool.wait_ge(aggred, (i + 1) * T)
                pool.wait_ge(outd, i * T)
                nc.gpsimd.tensor_tensor(ve[:], mv[:, :, 1], eps[:], ALU.add).then_inc(inv, 1)
                pool.wait_ge(inv, 2 * i + 1)
                nc.gpsimd.tensor_tensor(rs[:], ve[:], power[:], ALU.pow).then_inc(inv, 1)

        @block.sync
        def _(sp):
            for i in range(CHUNKS):
                if i >= 2:
                    sp.wait_ge(outd, (i - 1) * T)
                sp.dma_start(x2[i % 2][:], tokens(dr["x3"], i)).then_inc(x_in[i % 2], 16)

        @block.scalar
        def _(a):
            for i in range(CHUNKS):
                a.wait_ge(outd, (i + 1) * T)
                a.dma_start(tokens(out, i), xo[i % 2][:]).then_inc(o_out[i % 2], 16)
            for u in range(2):
                a.wait_ge(o_out[u], 16 * CHUNKS // 2)

        @block.vector
        def _(dve):
            v = nc.vector
            for i in range(CHUNKS):
                u = i % 2
                dve.wait_ge(g_in[u], 16 * T * (i // 2 + 1))
                dve.wait_ge(x_in[u], 16 * (i // 2 + 1))
                v.tensor_tensor(x2[u][:], x2[u][:], g_[u][:], ALU.add).then_inc(added, 1)
                dve.wait_ge(added, i + 1)
                for t in range(T):
                    v.bn_stats(st[:, t, :], x2[u][:, t, :]).then_inc(stats, 1)
                for t in range(T):
                    dve.wait_ge(stats, i * T + t + 1)
                    v.bn_aggr(mv[:, t, :], st[:, t, :]).then_inc(aggred, 1)
                dve.wait_ge(inv, 2 * i + 2)
                if i >= 2:
                    dve.wait_ge(o_out[u], 16 * (i // 2))
                for t in range(T):
                    v.tensor_scalar(xo[u][:, t, :], x2[u][:, t, :], mv[:, t, 0:1], rs[:, t:t + 1],
                                    ALU.subtract, ALU.mult).then_inc(outd, 1)


SCRATCH = {
    "outT": ([C, TOKENS], F32),
    "y0": ([TOKENS, C], F32),
    "qs": ([3, C, TOKENS], BF16),
    "ks": ([3, C, TOKENS], BF16),
    "v": ([TOKENS, H * 2 * DK], F32),
    "Y": ([TOKENS, C], F32),
    "x3": ([TOKENS, C], F32),
    "zs": ([MT * P, C], F32),
    "ys": ([MT * P, C], F32),
}


_INS = ["L0_attn_x", "L0_attn_w_wave", "L0_attn_b_wave", "L0_attn_w_query", "L0_attn_b_query", "L0_attn_key_weight",
        "L0_attn_w_se1", "L0_attn_b_se1", "L0_attn_w_se2", "L0_attn_b_se2", "L0_attn_w_out",
        "L0_ffn_ln1_w", "L0_ffn_ln1_b", "L0_ffn_w_qkv", "L0_ffn_w_proj", "L0_ffn_ln2_w", "L0_ffn_ln2_b",
        "L0_ffn_gate_w", "L0_ffn_gate_b", "L0_ffn_w1", "L0_ffn_w2"]


def kernel(**inputs):
    import numpy as _np
    import concourse.bacc as _bacc
    from concourse.bass_utils import run_bass_kernel_spmd as _run

    nc = _bacc.Bacc("TRN2", target_bir_lowering=False, num_devices=1)
    arrays, io = {}, {}
    for name in _INS:
        a = _np.ascontiguousarray(inputs[name])
        arrays[f"in_{name}"] = a
        io[name] = nc.dram_tensor(f"in_{name}", list(a.shape), mybir.dt.from_np(a.dtype), kind="ExternalInput").ap()
    io["out"] = nc.dram_tensor("out_0", [B, L, C], F32, kind="ExternalOutput").ap()
    dr = {n: nc.dram_tensor(f"scratch_{n}", shape, dt, kind="Internal").ap() for n, (shape, dt) in SCRATCH.items()}
    build(nc, io, dr)
    r = _run(nc, [arrays], core_ids=[0])
    return r.results[0]["out_0"]
```

```python
import concourse.bass as bass
from concourse import mybir
from contextlib import ExitStack

F32 = mybir.dt.float32
BF16 = mybir.dt.bfloat16
I32 = mybir.dt.int32
ALU = mybir.AluOpType
ACT = mybir.ActivationFunctionType
AX = mybir.AxisListType
P = 128

B, L, C = 4, 1024, 256
TOKENS = B * L
TILES = TOKENS // P
BT = L // P
KC = C // P
WH, POS, REACH = 8, 16, 16
WD = C // WH
STEPS = 2 * REACH + 1
NW = 3 * WH + WH * POS
SE = C // 4
H, DK = 16, 16
QUADS = H // 4
E, HID = 8, 1024
MT = TILES + E - 1
EPS = 1e-5


class Chain:

    def __init__(self, eng, sem, base=0):
        self.eng, self.sem, self.base, self.n = eng, sem, base, 0

    def did(self, ins):
        ins.then_inc(self.sem, 1)
        self.n += 1
        return self.n

    def wait(self, n=None):
        self.eng.wait_ge(self.sem, self.base + (self.n if n is None else n))

    def link(self, ins):
        self.did(ins)
        self.wait()


def build(nc, io, dr):
    with ExitStack() as top:
        sems = {}

        def sem(name):
            assert name not in sems
            sems[name] = top.enter_context(nc.semaphore(name))
            return sems[name]

        def sb(ctx, name, shape, dt=F32):
            return ctx.enter_context(nc.sbuf_tensor(name, shape, dt))

        def ps(ctx, name, shape, dt=F32):
            return ctx.enter_context(nc.psum_tensor(name, shape, dt))

        ident = sb(top, "ident", [P, P])
        identb = sb(top, "identb", [P, P], BF16)
        constants(nc, sem, ident, identb)
        with ExitStack() as wave:
            par = {n: sb(wave, "par_" + n, [P, TILES]) for n in ("freq", "phase", "invf", "mid", "kmax")}
            par["lpos"] = sb(wave, "par_lpos", [P, TILES])
            par["alpha"] = sb(wave, "par_alpha", [P, TILES, WH])
            par["beta"] = sb(wave, "par_beta", [P, TILES, WH])
            wave_parameters(nc, sem, sb, ps, io, dr, ident, par)
            wave_sampling(nc, sem, sb, ps, io, dr, ident, identb, par)
        with ExitStack() as ctx:
            gate_and_project(nc, sem, lambda *a: sb(ctx, *a), lambda *a: ps(ctx, *a), io, dr, ident)
        w1 = sb(top, "w1", [P, KC, E, HID])
        w2 = sb(top, "w2", [P, HID // P, E, C])
        w_in = sem("experts_in")
        with ExitStack() as ctx:
            attention(nc, sem, lambda *a: sb(ctx, *a), lambda *a: ps(ctx, *a), io, dr, ident, w1, w2, w_in)
        slot = sb(top, "slot", [P, TILES], I32)
        expert = sb(top, "expert", [1, MT], I32)
        with ExitStack() as outer:
            logits = sb(outer, "logits", [P, TILES, E])
            n2 = sb(outer, "n2", [P, TILES, C])
            with ExitStack() as ctx:
                project_and_gate(nc, sem, lambda *a: sb(ctx, *a), lambda *a: ps(ctx, *a), io, dr, ident, n2, logits)
            with ExitStack() as ctx:
                dispatch(nc, sem, lambda *a: sb(ctx, *a), lambda *a: ps(ctx, *a), dr, n2, logits, slot, expert)
        with ExitStack() as ctx:
            experts(nc, sem, lambda *a: sb(ctx, *a), lambda *a: ps(ctx, *a), io, dr, ident, w1, w2, expert)
        with ExitStack() as ctx:
            combine(nc, sem, lambda *a: sb(ctx, *a), io, dr, slot)


def constants(nc, sem, ident, identb):
    zeroed, made = sem("ident_zeroed"), sem("ident_made")
    with nc.Block() as block:
        @block.gpsimd
        def _(pool):
            nc.gpsimd.memset(ident[:], 0.0).then_inc(zeroed, 1)
            pool.wait_ge(zeroed, 1)
            nc.gpsimd.affine_select(out=ident[:], in_=ident[:], compare_op=ALU.not_equal, fill=1.0, base=0,
                                    pattern=[[-1, P]], channel_multiplier=1).then_inc(made, 1)

        @block.vector
        def _(dve):
            dve.wait_ge(made, 1)
            nc.vector.tensor_copy(identb[:], ident[:])


def wave_parameters(nc, sem, sb, ps, io, dr, ident, par):
    with ExitStack() as ctx:
        tanhs = sb(ctx, "wp_tanh", [P, TILES, 3, WH])
        qk = sb(ctx, "wp_qk", [P, TILES, WH])
        kw = sb(ctx, "wp_kw", [P, POS])
        with ExitStack() as inner:
            project_waves(nc, sem, lambda *a: sb(inner, *a), lambda *a: ps(inner, *a), io, ident, kw, tanhs, qk)
        with ExitStack() as inner:
            wave_normalisers(nc, sem, lambda *a: sb(inner, *a), par, tanhs, qk, dr)


def project_waves(nc, sem, sb, ps, io, ident, kw, tanhs, qk):
    xb = sb("pw_x", [P, BT, C])
    xT = sb("pw_xT", [P, KC, L])
    w = sb("pw_w", [P, KC, NW])
    bias = sb("pw_bias", [P, NW])
    pre = sb("pw_pre", [P, BT, NW])
    act = sb("pw_act", [P, BT, NW])
    prod = sb("pw_prod", [P, BT, WH * POS])
    pT = ps("pw_pT", [P, KC, L])
    pW = ps("pw_pW", [P, BT // 2, 2, C])
    w_in, x_in = sem("wave_w_in"), sem("wave_x_in")
    turned, evac, mm = sem("wave_x_turned"), sem("wave_xT_ready"), sem("wave_projected")
    biased, silued, tanhed, qprod, qkd = (sem("wave_" + n) for n in ("biased", "silued", "tanhed", "qk_products", "qk_summed"))
    pW3 = pW[:, :, :, 0:NW]
    act4 = act[:, :, 0:3 * WH].rearrange("p t (g h) -> p t g h", g=3)
    x = io["L0_attn_x"].rearrange("b (t p) c -> b p t c", p=P)

    def row(a, n):
        return a.rearrange("(o n) -> o n", o=1).to_broadcast([P, n])

    with nc.Block() as block:
        @block.sync
        def _(sp):
            def each(b):
                sp.wait_ge(turned, b)
                sp.dma_start(xb[:], x[b]).then_inc(x_in, 16)

            each(0)
            with sp.Fori(1, B) as b:
                each(b)

        @block.scalar
        def _(a):
            a.dma_start(w[:, :, 0:3 * WH], io["L0_attn_w_wave"].rearrange("(k p) n -> p k n", p=P)).then_inc(w_in, 16)
            a.dma_start(w[:, :, 3 * WH:NW], io["L0_attn_w_query"].rearrange("(k p) n -> p k n", p=P)).then_inc(w_in, 16)
            a.dma_start(bias[:, 0:3 * WH], row(io["L0_attn_b_wave"], 3 * WH)).then_inc(w_in, 16)
            a.dma_start(bias[:, 3 * WH:NW], row(io["L0_attn_b_query"], WH * POS)).then_inc(w_in, 16)
            a.dma_start(kw[:], row(io["L0_attn_key_weight"], POS)).then_inc(w_in, 16)
            def each(b):
                a.wait_ge(turned, b + 1)
                a.wait_ge(mm, b)
                nc.scalar.copy(xT[:, 1, :], pT[:, 1, :]).then_inc(evac, 1)
                a.wait_ge(biased, b + 1)
                a.wait_ge(qkd, b)
                nc.scalar.activation(act[:], pre[:], ACT.Silu).then_inc(silued, 1)
                a.wait_ge(silued, b + 1)
                at = tanhs[:, bass.ds(b * BT, BT), :, :]
                nc.scalar.activation(at[:, :, 0:3:2, :], act4[:, :, 0:3:2, :], ACT.Tanh, scale=0.5).then_inc(tanhed, 1)
                nc.scalar.activation(at[:, :, 1, :], act4[:, :, 1, :], ACT.Tanh).then_inc(tanhed, 1)

            each(0)
            with a.Fori(1, B) as b:
                each(b)
            a.wait_ge(tanhed, 2 * B)

        @block.tensor
        def _(pe):
            pe.wait_ge(w_in, 5 * 16)
            def each(b):
                pe.wait_ge(x_in, 16 * b + 16)
                pe.wait_ge(evac, 2 * b)
                for k in range(KC):
                    for t in range(BT):
                        last = nc.tensor.transpose(pT[:, k, t * P:(t + 1) * P], xb[:, t, k * P:(k + 1) * P], ident[:])
                last.then_inc(turned, 1)
                pe.wait_ge(evac, 2 * b + 2)
                pe.wait_ge(biased, b)
                for t in range(BT):
                    for k in range(KC):
                        last = nc.tensor.matmul(pW[:, t // 2, t % 2, 0:NW], xT[:, k, t * P:(t + 1) * P], w[:, k, :],
                                                start=(k == 0), stop=(k == KC - 1))
                last.then_inc(mm, 1)

            each(0)
            with pe.Fori(1, B) as b:
                each(b)

        @block.vector
        def _(dve):
            dve.wait_ge(w_in, 5 * 16)
            def each(b):
                dve.wait_ge(turned, b + 1)
                dve.wait_ge(mm, b)
                nc.vector.tensor_copy(xT[:, 0, :], pT[:, 0, :]).then_inc(evac, 1)
                dve.wait_ge(mm, b + 1)
                dve.wait_ge(silued, b)
                nc.vector.tensor_tensor(pre[:].rearrange("p (s t) n -> p s t n", t=2), pW3,
                                        bias[:].unsqueeze(1).unsqueeze(1).to_broadcast([P, BT // 2, 2, NW]),
                                        ALU.add).then_inc(biased, 1)
                dve.wait_ge(silued, b + 1)
                nc.vector.tensor_tensor(prod[:].rearrange("p t (h d) -> p (t h) d", h=WH),
                                        act[:, :, 3 * WH:NW].rearrange("p t (h d) -> p t h d", h=WH),
                                        kw[:].unsqueeze(1).to_broadcast([P, BT * WH, POS]).rearrange("p (t h) d -> p t h d", h=WH),
                                        ALU.mult).then_inc(qprod, 1)
                dve.wait_ge(qprod, b + 1)
                nc.vector.reduce_sum(qk[:, bass.ds(b * BT, BT), :], prod[:].rearrange("p t (h d) -> p t h d", h=WH),
                                     AX.X).then_inc(qkd, 1)

            each(0)
            with dve.Fori(1, B) as b:
                each(b)
            dve.wait_ge(qkd, B)


def wave_normalisers(nc, sem, sb, par, tanhs, qk, dr):
    NK = REACH + 1
    mean = sb("wn_sum", [P, TILES, 3])
    steps = sb("wn_steps", [P, STEPS])
    ks = sb("wn_ks", [P, NK])
    far = sb("wn_far", [P, NK])
    pos = sb("wn_pos", [P, TILES, STEPS])
    pos2 = sb("wn_pos2", [P, TILES, STEPS])
    inside = sb("wn_inside", [P, TILES, STEPS])
    cnt = sb("wn_count", [P, TILES, NK])
    any_ = sb("wn_any", [P, TILES, NK])
    tk = sb("wn_tk", [P, TILES, NK])
    tk2 = sb("wn_tk2", [P, TILES, NK])
    env = sb("wn_env", [P, TILES, NK])
    dec, g, kmin = (sb("wn_" + n, [P, TILES]) for n in ("dec", "g", "kmin"))
    a_, m1, m2, Z, Es, lnD = (sb("wn_" + n, [P, TILES, WH]) for n in ("a", "m1", "m2", "Z", "E", "lnD"))
    big = sb("wn_big", [P, TILES, WH, NK])
    big2 = sb("wn_big2", [P, TILES, WH, NK])
    consts, d, acted, asked = sem("wn_consts"), sem("wn_dve"), sem("wn_acted"), sem("wn_asked")
    freq, phase, invf, mid, kmax, lpos = (par[n] for n in ("freq", "phase", "invf", "mid", "kmax", "lpos"))
    alpha, beta = par["alpha"], par["beta"]

    def over(a, n):
        return a[:].unsqueeze(2).to_broadcast([P, TILES, n])

    def heads(a):
        return a[:].unsqueeze(3).to_broadcast([P, TILES, WH, NK])

    def dist(a):
        return a[:].unsqueeze(2).to_broadcast([P, TILES, WH, NK])

    with nc.Block() as block:
        @block.gpsimd
        def _(pool):
            nc.gpsimd.iota(lpos[:], pattern=[[0, B], [P, BT]], base=0, channel_multiplier=1,
                           allow_small_or_imprecise_dtypes=True).then_inc(consts, 1)
            nc.gpsimd.iota(steps[:], pattern=[[1, STEPS]], base=-REACH, channel_multiplier=0,
                           allow_small_or_imprecise_dtypes=True).then_inc(consts, 1)
            nc.gpsimd.iota(ks[:], pattern=[[1, NK]], base=0, channel_multiplier=0,
                           allow_small_or_imprecise_dtypes=True).then_inc(consts, 1)
            nc.gpsimd.iota(far[:], pattern=[[-1, NK]], base=1000, channel_multiplier=0,
                           allow_small_or_imprecise_dtypes=True).then_inc(consts, 1)

        @block.vector
        def _(dve):
            v = nc.vector
            c = Chain(dve, d)
            c.link(v.reduce_sum(mean[:], tanhs[:], AX.X))
            c.did(v.tensor_scalar(freq[:], mean[:, :, 0], 7.5 / WH, 8.5, ALU.mult, ALU.add))
            c.did(v.tensor_scalar(phase[:], mean[:, :, 1], 16.0 / WH, None, ALU.mult))
            c.link(v.tensor_scalar(dec[:], mean[:, :, 2], 4.75 / WH, 5.25, ALU.mult, ALU.add))
            c.did(v.tensor_scalar(dec[:], dec[:], 0.1, None, ALU.max))
            c.link(v.reciprocal(invf[:], freq[:]))
            c.link(v.reciprocal(g[:], dec[:]))
            dve.wait_ge(consts, 4)
            c.link(v.tensor_tensor(g[:], g[:], freq[:], ALU.mult))
            c.did(v.tensor_tensor(pos[:], steps[:].unsqueeze(1).to_broadcast([P, TILES, STEPS]), over(freq, STEPS), ALU.mult))
            c.link(v.tensor_tensor(mid[:], lpos[:], phase[:], ALU.add))
            c.did(v.tensor_tensor(pos2[:], pos[:], over(lpos, STEPS), ALU.add))
            c.link(v.tensor_scalar(mid[:], mid[:], -1.0, 0.5, ALU.mult, ALU.add))
            c.did(v.tensor_tensor(pos[:], pos2[:], over(phase, STEPS), ALU.add))
            c.link(v.tensor_tensor(mid[:], mid[:], invf[:], ALU.mult))
            c.link(v.tensor_scalar(pos2[:], pos[:], float(L), None, ALU.is_lt))
            c.link(v.scalar_tensor_tensor(out=inside[:], in0=pos[:], scalar=0.0, in1=pos2[:], op0=ALU.is_ge, op1=ALU.mult))
            c.did(v.tensor_copy(cnt[:, :, 0], inside[:, :, REACH]))
            c.link(v.tensor_tensor(cnt[:, :, 1:NK], inside[:, :, REACH + 1:STEPS], inside[:, :, REACH - 1::-1], ALU.add))
            c.link(v.tensor_scalar(any_[:], cnt[:], 0.0, None, ALU.is_gt))
            c.did(v.tensor_tensor(tk[:], any_[:], ks[:].unsqueeze(1).to_broadcast([P, TILES, NK]), ALU.mult))
            c.link(v.tensor_tensor(tk2[:], any_[:], far[:].unsqueeze(1).to_broadcast([P, TILES, NK]), ALU.mult))
            c.did(v.tensor_reduce(kmax[:], tk[:], AX.X, ALU.max))
            c.link(v.tensor_reduce(kmin[:], tk2[:], AX.X, ALU.max))
            c.did(v.tensor_scalar(kmin[:], kmin[:], -1.0, 1000.0, ALU.mult, ALU.add))
            c.link(v.scalar_tensor_tensor(out=a_[:], in0=qk[:], scalar=float(POS) ** -0.5, in1=over(freq, WH),
                                          op0=ALU.mult, op1=ALU.mult))
            c.did(v.tensor_tensor(m1[:], a_[:], over(kmax, WH), ALU.mult))
            c.link(v.tensor_tensor(m2[:], a_[:], over(kmin, WH), ALU.mult))
            c.did(v.tensor_tensor(big[:], heads(a_), ks[:].unsqueeze(1).unsqueeze(1).to_broadcast([P, TILES, WH, NK]), ALU.mult))
            c.link(v.tensor_tensor(m1[:], m1[:], m2[:], ALU.max))
            c.did(v.tensor_tensor(tk[:], over(g, NK), ks[:].unsqueeze(1).to_broadcast([P, TILES, NK]), ALU.mult))
            c.link(v.tensor_tensor(big2[:], big[:], heads(m1), ALU.subtract))
            v.tensor_scalar(big2[:], big2[:], 0.0, None, ALU.min).then_inc(asked, 1)
            dve.wait_ge(acted, 2)
            c.did(v.tensor_tensor(big2[:], big[:], dist(cnt), ALU.mult))
            c.link(v.tensor_tensor(alpha[:], a_[:], over(g, WH), ALU.subtract))
            c.did(v.reduce_sum(Z[:], big2[:], AX.X))
            c.link(v.tensor_tensor(beta[:], alpha[:], over(kmax, WH), ALU.mult))
            c.did(v.tensor_tensor(big[:], big2[:], dist(env), ALU.mult))
            c.link(v.tensor_tensor(beta[:], beta[:], m1[:], ALU.subtract))
            c.link(v.reduce_sum(Es[:], big[:], AX.X))
            v.scalar_tensor_tensor(out=lnD[:], in0=Z[:], scalar=1e-8, in1=Es[:], op0=ALU.mult, op1=ALU.add).then_inc(asked, 1)
            dve.wait_ge(acted, 3)
            c.link(v.tensor_tensor(beta[:], beta[:], m2[:], ALU.subtract))

        @block.scalar
        def _(a):
            a.wait_ge(asked, 1)
            nc.scalar.activation(big[:], big2[:], ACT.Exp).then_inc(acted, 1)
            nc.scalar.activation(env[:], tk[:], ACT.Exp, scale=-1.0).then_inc(acted, 1)
            a.wait_ge(asked, 2)
            nc.scalar.activation(m2[:], lnD[:], ACT.Ln).then_inc(acted, 1)


def wave_sampling(nc, sem, sb, ps, io, dr, ident, identb, par):
    MAGIC = 1.5 * 2.0 ** 23
    NEAR = 3
    G = 4
    assert (REACH * 16.0 + 16.0) < NEAR * P

    def near(g, r):
        i = G * g + r
        return list(range(max(0, i - NEAR), min(BT - 1, i + NEAR) + 1))

    width = [[len(near(g, r)) * P for r in range(G)] for g in range(2)]
    off = [[sum(width[g][:r]) for r in range(G)] for g in range(2)]
    slots = [[(j, r) for j in range(BT) for r in range(G) if j in near(g, r)] for g in range(2)]
    NS = len(slots[0])
    assert NS == len(slots[1])
    CH = 8
    chunks = [range(s, min(s + CH, NS)) for s in range(0, NS, CH)]
    NCH = len(chunks)
    UCH = NCH * (1 + WH)
    WMAX = max(map(max, width))
    RING = 3
    FULL0, FREE0, READY0, MM0, OUT0 = 2 * UCH, RING, WH * G, 2, 2
    assert UCH % RING == 0

    with ExitStack() as ctx:
        A = [sb(ctx, f"ws_A{i}", [P, NS * P]) for i in range(2)]
        AT = [sb(ctx, f"ws_AT{h}", [P, NS, P]) for h in range(WH)]
        KB, HB, HT = ([sb(ctx, f"ws_{n}{g}", [P, NS * P], BF16) for g in range(2)] for n in ("steps", "hit", "hitT"))
        step, pos = ([sb(ctx, f"ws_{n}{i}", [P, WMAX]) for i in range(2)] for n in ("step", "pos"))
        raw = [sb(ctx, f"ws_raw{i}", [P, WMAX]) for i in range(2)]
        below = [sb(ctx, f"ws_below{i}", [P, WMAX], BF16) for i in range(2)]
        xb = sb(ctx, "ws_x", [P, BT, C])
        rows = sb(ctx, "ws_rows", [P, L])
        ot = [sb(ctx, f"ws_ot{i}", [P, G * P]) for i in range(2)]
        pA = [ps(ctx, f"ws_pA{i}", [P, CH * P]) for i in range(RING)]
        acc = [ps(ctx, f"ws_acc{i}", [P, G * P]) for i in range(2)]
        rows_made, x_in = sem("ws_rows_made"), sem("ws_x_in")
        raw_ready, clamped, rounded, placed, kstep = (sem("ws_" + n) for n in ("raw", "clamped", "rounded", "placed", "kgen"))
        ready, full, free, mm, acc_out = (sem("ws_" + n) for n in ("exp", "chunk_full", "chunk_free", "products", "acc_out"))
        ot_out = [sem(f"ws_ot_out{i}") for i in range(2)]
        KSTEPS = 5
        x = io["L0_attn_x"].rearrange("b (t p) c -> b p t c", p=P)
        outT = dr["outT"].rearrange("(q p) n -> q p n", p=P)

        def cols(g, r):
            return slice(off[g][r], off[g][r] + width[g][r])

        def mrows(g, r):
            return rows[:, near(g, r)[0] * P:(near(g, r)[-1] + 1) * P]

        with nc.Block() as block:
            def schedule(unit, kgen, eng):
                unit(0, 0, True, False)
                with eng.Fori(0, B - 1) as i:
                    unit(i * 2 + 1, 1, False, False)
                    unit(i * 2 + 2, 0, False, False)
                unit(2 * B - 1, 1, False, True)

            @block.sync
            def _(sp):
                def load_x(b):
                    sp.dma_start(xb[:], x[b]).then_inc(x_in, 16)

                def store(n, hq):
                    sp.wait_ge(acc_out, OUT0 + n * 2 + hq + 1)
                    sp.dma_start(outT[hq, :, bass.ds(n * (G * P), G * P)], ot[hq][:]).then_inc(ot_out[hq], 16)

                load_x(0)
                store(0, 0)
                with sp.Fori(0, B - 1) as i:
                    store(i * 2, 1)
                    store(i * 2 + 1, 0)
                    sp.wait_ge(mm, MM0 + i * 4 + 4)
                    load_x(i + 1)
                    store(i * 2 + 1, 1)
                    store(i * 2 + 2, 0)
                store(2 * B - 2, 1)
                store(2 * B - 1, 0)
                store(2 * B - 1, 1)
                for hq in range(2):
                    sp.wait_ge(ot_out[hq], 16 * 2 * B)

            @block.gpsimd
            def _(pool):
                nc.gpsimd.iota(rows[:], pattern=[[1, L]], base=0, channel_multiplier=0,
                               allow_small_or_imprecise_dtypes=True).then_inc(rows_made, 1)

            @block.scalar
            def _(a):
                a.sem_inc(ready, READY0)
                a.sem_inc(acc_out, OUT0)

                def locate(n, g, r):
                    t = bass.ds(n * G + r, 1)
                    a.wait_ge(rounded, n * G + (r - 1 if r else 0))
                    nc.scalar.activation(raw[r % 2][:, 0:width[g][r]], mrows(g, r), ACT.Identity,
                                         bias=par["mid"][:, t], scale=par["invf"][:, t]).then_inc(raw_ready, 1)

                def place(n, g, r):
                    w, t = width[g][r], bass.ds(n * G + r, 1)
                    a.wait_ge(rounded, n * G + r + 1)
                    nc.scalar.activation(pos[r % 2][:, 0:w], step[r % 2][:, 0:w], ACT.Identity,
                                         bias=par["lpos"][:, t], scale=par["freq"][:, t]).then_inc(placed, 1)

                def exps(n, g, h):
                    a.wait_ge(full, FULL0 + n * UCH + NCH * h if h >= 2 else FULL0 + (n - 1) * UCH + NCH * (WH + h))
                    for r in range(G):
                        t = bass.ds(n * G + r, 1)
                        if h == 0:
                            a.wait_ge(kstep, (n * G + r + 1) * KSTEPS)
                        nc.scalar.activation(A[h % 2][:, cols(g, r)], KB[g][:, cols(g, r)], ACT.Exp,
                                             bias=par["beta"][:, t, h], scale=par["alpha"][:, t, h]).then_inc(ready, 1)

                def drain(n, hq):
                    a.wait_ge(mm, MM0 + n * 2 + hq + 1)
                    a.wait_ge(ot_out[hq], n * 16)
                    nc.scalar.copy(ot[hq][:], acc[hq][:]).then_inc(acc_out, 1)

                def unit(n, g, first, last):
                    for h in range(WH):
                        exps(n, g, h)
                        if h == 1 and not first:
                            drain(n - 1, 0)
                        if h == 5 and not first:
                            drain(n - 1, 1)
                        if not last:
                            if h in PLACE:
                                place(n + 1, 1 - g, PLACE.index(h))
                            if h in LOCATE:
                                locate(n + 1, 1 - g, LOCATE.index(h))

                PLACE, LOCATE = (2, 3, 4, 6), (0, 1, 2, 3)
                a.wait_ge(rows_made, 1)
                for r in range(G):
                    if r:
                        place(0, 0, r - 1)
                    locate(0, 0, r)
                place(0, 0, G - 1)
                unit(0, 0, True, False)
                with a.Fori(0, B - 1) as i:
                    unit(i * 2 + 1, 1, False, False)
                    unit(i * 2 + 2, 0, False, False)
                unit(2 * B - 1, 1, False, True)
                drain(2 * B - 1, 0)
                drain(2 * B - 1, 1)

            @block.vector
            def _(dve):
                v = nc.vector
                dve.sem_inc(free, FREE0)
                dve.wait_ge(rows_made, 1)

                def steps(n, g, r, link):
                    w, k = width[g][r], n * G + r
                    t, u = bass.ds(n * G + r, 1), r % 2
                    bits = step[u][:, 0:w].bitcast(I32)
                    if link == 0:
                        dve.wait_ge(raw_ready, k + 1)
                        v.tensor_scalar(raw[u][:, 0:w], raw[u][:, 0:w], float(REACH), float(-REACH),
                                        ALU.min, ALU.max).then_inc(clamped, 1)
                    elif link == 1:
                        dve.wait_ge(clamped, k + 1)
                        v.tensor_scalar(step[u][:, 0:w], raw[u][:, 0:w], MAGIC, MAGIC, ALU.add, ALU.subtract).then_inc(rounded, 1)
                    elif link == 3:
                        dve.wait_ge(placed, k + 1)
                        v.scalar_tensor_tensor(out=pos[u][:, 0:w], in0=pos[u][:, 0:w], scalar=par["phase"][:, t],
                                               in1=mrows(g, r), op0=ALU.add, op1=ALU.subtract).then_inc(kstep, 1)
                    elif link == 4:
                        v.tensor_scalar(bits, bits, 0x7FFFFFFF, None, ALU.bitwise_and).then_inc(kstep, 1)
                    elif link == 5:
                        dve.wait_ge(kstep, k * KSTEPS + 1)
                        v.tensor_scalar(below[u][:, 0:w], pos[u][:, 0:w], 1.0, None, ALU.is_lt).then_inc(kstep, 1)
                    elif link == 6:
                        dve.wait_ge(kstep, k * KSTEPS + 3)
                        dve.wait_ge(full, FULL0 + n * UCH - 2 * UCH + NCH)
                        v.scalar_tensor_tensor(out=HB[g][:, cols(g, r)], in0=pos[u][:, 0:w], scalar=0.0,
                                               in1=below[u][:, 0:w], op0=ALU.is_ge, op1=ALU.mult).then_inc(kstep, 1)
                    elif link == 7:
                        dve.wait_ge(kstep, k * KSTEPS + 4)
                        dve.wait_ge(ready, READY0 + (n - 1) * (WH * G))
                        v.scalar_tensor_tensor(out=KB[g][:, cols(g, r)], in0=step[u][:, 0:w],
                                               scalar=par["kmax"][:, t], in1=HB[g][:, cols(g, r)],
                                               op0=ALU.subtract, op1=ALU.mult).then_inc(kstep, 1)

                def drain(n, g, c, h):
                    q = (c if h is None else NCH * (1 + h) + c)
                    dve.wait_ge(full, FULL0 + n * UCH + q + 1)
                    m = chunks[c]
                    w = len(m) * P
                    cs = slice(m[0] * P, m[0] * P + w)
                    p = pA[q % RING]
                    if h is None:
                        v.tensor_copy(HT[g][:, cs], p[:].bitcast(BF16)[:, 0:w]).then_inc(free, 1)
                    else:
                        v.tensor_tensor(AT[h][:].rearrange("p s l -> p (s l)")[:, cs], p[:, 0:w], HT[g][:, cs],
                                        ALU.mult).then_inc(free, 1)

                def unit(n, g, first, last):
                    dve.wait_ge(kstep, (n + 1) * G * KSTEPS)
                    for c in range(NCH):
                        drain(n, g, c, None)
                    dve.wait_ge(free, FREE0 + n * UCH + NCH)
                    for h in range(WH):
                        if h % 4 == 0:
                            dve.wait_ge(mm, MM0 + (n - 1) * 2 + h // 4 + 1)
                        for c in range(NCH):
                            drain(n, g, c, h)
                            for r in range(G):
                                if not last and 0 <= h * NCH + c - APART * r < LINKS:
                                    steps(n + 1, 1 - g, r, h * NCH + c - APART * r)

                APART, LINKS = 4, 8
                for i in range(APART * (G - 1) + LINKS):
                    for r in range(G):
                        if 0 <= i - APART * r < LINKS:
                            steps(0, 0, r, i - APART * r)
                unit(0, 0, True, False)
                with dve.Fori(0, B - 1) as i:
                    unit(i * 2 + 1, 1, False, False)
                    unit(i * 2 + 2, 0, False, False)
                unit(2 * B - 1, 1, False, True)

            @block.tensor
            def _(pe):
                pe.sem_inc(full, FULL0)
                pe.sem_inc(mm, MM0)

                def turn(n, g, h, c):
                    if c == 0 and h is None:
                        pe.wait_ge(kstep, (n + 1) * G * KSTEPS)
                    elif c == 0:
                        pe.wait_ge(ready, READY0 + (n * WH + h + 1) * G)
                    q = (c if h is None else NCH * (1 + h) + c)
                    pe.wait_ge(free, n * UCH + q + 1)
                    p, m = pA[q % RING], chunks[c]
                    for s in m:
                        j, r = slots[g][s]
                        at = off[g][r] + (j - near(g, r)[0]) * P
                        to = slice((s - m[0]) * P, (s - m[0] + 1) * P)
                        if h is None:
                            last = nc.tensor.transpose(p[:].bitcast(BF16)[:, to], HB[g][:, at:at + P], identb[:])
                        else:
                            last = nc.tensor.transpose(p[:, to], A[h % 2][:, at:at + P], ident[:])
                    last.then_inc(full, 1)

                def products(n, g, hq, i):
                    order = [j for j in range(BT) if any(jj == j for jj, _ in slots[g])]
                    if g:
                        order.reverse()
                    if i == 0:
                        pe.wait_ge(free, FREE0 + n * UCH + NCH * (1 + 4 * (hq + 1)))
                        pe.wait_ge(acc_out, OUT0 + (n - 1) * 2 + hq + 1)
                    j = order[i]
                    rs = [r for jj, r in slots[g] if jj == j]
                    s = slots[g].index((j, rs[0]))
                    for h4 in range(4):
                        h = 4 * hq + h4
                        last = nc.tensor.matmul(acc[hq][h4 * WD:(h4 + 1) * WD, rs[0] * P:(rs[-1] + 1) * P],
                                                xb[:, j, h * WD:(h + 1) * WD],
                                                AT[h][:, s:s + len(rs), :],
                                                start=(i == 0), stop=(i == len(order) - 1))
                    if i == len(order) - 1:
                        last.then_inc(mm, 1)

                NJ = G + NEAR
                AT0, AT1 = (18, 19, 21, 22, 24, 25, 26), (3, 5, 7, 8, 10, 12, 14)
                assert NCH * 5 + RING <= AT0[0] and RING <= AT1[0] and len(AT0) == len(AT1) == NJ

                def unit(n, g, first, last):
                    for q in range(UCH):
                        turn(n, g, q // NCH - 1 if q >= NCH else None, q % NCH)
                        if q in AT1 and not first:
                            products(n - 1, 1 - g, 1, AT1.index(q))
                        if q in AT0:
                            if q == AT0[0] and g == 0:
                                pe.wait_ge(x_in, n * 8 + 16)
                            products(n, g, 0, AT0.index(q))

                unit(0, 0, True, False)
                with pe.Fori(0, B - 1) as i:
                    unit(i * 2 + 1, 1, False, False)
                    unit(i * 2 + 2, 0, False, False)
                unit(2 * B - 1, 1, False, True)
                for i in range(NJ):
                    products(2 * B - 1, 1, 1, i)


def gate_and_project(nc, sem, sb, ps, io, dr, ident):
    T = 4
    N = T * P
    CHUNKS = TOKENS // N
    PARTS = 6
    wse1, wse2, wout = sb("gp_wse1", [P, KC, SE]), sb("gp_wse2", [SE, KC, P]), sb("gp_wout", [P, KC, C])
    wqkv = sb("gp_wqkv", [P, KC, 3 * C])
    bse1, bse2, hb2 = sb("gp_bse1", [SE, 1]), sb("gp_bse2", [P, KC]), sb("gp_hb2", [P, KC])
    ln_w, ln_b = sb("gp_lnw", [P, KC]), sb("gp_lnb", [P, KC])
    oT, xc = sb("gp_oT", [P, KC, N]), sb("gp_x", [P, T, C])
    s1, th, gated = sb("gp_s1", [SE, N]), sb("gp_th", [P, KC, N]), sb("gp_gated", [P, KC, N])
    so, res, y0, n1 = sb("gp_so", [P, T, C]), sb("gp_res", [P, T, C]), sb("gp_y0", [P, T, C]), sb("gp_n1", [P, T, C])
    st, mv = sb("gp_st", [P, T, 6]), sb("gp_mv", [P, T, 2])
    eps, power = sb("gp_eps", [P, T]), sb("gp_power", [P, T])
    seen = sb("gp_seen", [P, 1])
    ve, rs, vn, rs2 = (sb("gp_" + n, [P, T]) for n in ("ve", "rs", "vn", "rs2"))
    zT = sb("gp_zT", [P, KC, N])
    rest = [sb(f"gp_rest{i}", [P, N]) for i in range(2)]
    split = [sb(f"gp_split{i}", [P, 3, N], BF16) for i in range(2)]
    vb = sb("gp_v", [P, T, H, 2 * DK])
    p1, pA, pO = ps("gp_p1", [SE, N]), ps("gp_pA", [P, KC, N]), ps("gp_pO", [P, T, C])
    pQ = [ps(f"gp_pQ{i}", [P, N]) for i in range(3)]
    w_in, o_in, x_in, ones, half = (sem("gp_" + n) for n in ("w_in", "o_in", "x_in", "consts", "half_bias"))
    se1, silu1, se2, tanhed, gate, outed, silu3 = (sem("gp_" + n) for n in ("se1", "silu1", "se2", "tanh", "gated", "wout", "silu3"))
    added, stats, aggred, inv, y0d, n1d, turned, zd = (sem("gp_" + n) for n in ("added", "stats", "aggr", "rstd", "y0", "n1", "turned", "z"))
    part, hi, left, midd, lo, vd = (sem("gp_" + n) for n in ("part", "hi", "rest", "mid", "lo", "v"))
    y_out, v_out, waited = sem("gp_y_out"), sem("gp_v_out"), sem("gp_waited")
    s_out = [sem(f"gp_split_out{i}") for i in range(2)]
    INV = 6
    oT_d = dr["outT"].rearrange("(k p) n -> p k n", p=P)
    x_d = io["L0_attn_x"].rearrange("b l c -> (b l) c")
    LOADS = [(wse1[:], io["L0_attn_w_se1"].rearrange("(k p) n -> p k n", p=P)),
             (wse2[:], io["L0_attn_w_se2"].rearrange("s (k p) -> s k p", p=P)),
             (wout[:], io["L0_attn_w_out"].rearrange("(k p) n -> p k n", p=P)),
             (wqkv[:], io["L0_ffn_w_qkv"].rearrange("(k p) n -> p k n", p=P)),
             (bse1[:], io["L0_attn_b_se1"].rearrange("(s o) -> s o", o=1)),
             (bse2[:], io["L0_attn_b_se2"].rearrange("(k p) -> p k", p=P)),
             (ln_w[:], io["L0_ffn_ln1_w"].rearrange("(k p) -> p k", p=P)),
             (ln_b[:], io["L0_ffn_ln1_b"].rearrange("(k p) -> p k", p=P))]
    WAITS = 16 * len(LOADS)

    def tokens(d, i):
        return d[bass.ds(i * N, N), :].rearrange("(t p) c -> p t c", p=P)

    with nc.Block() as block, nc.allow_non_contiguous_dma(reason="per-channel vectors"):
        @block.sync
        def _(sp):
            def load_sums(i):
                sp.wait_ge(gate, i)
                sp.dma_start(oT[:], oT_d[:, :, bass.ds(i * N, N)]).then_inc(o_in, 16)

            def load_x(i):
                sp.wait_ge(added, i)
                sp.dma_start(xc[:], tokens(x_d, i)).then_inc(x_in, 16)

            def store_split(c, q):
                sp.wait_ge(lo, c * 4 + q + 1)
                dst = dr["qs"] if q < 2 else dr["ks"]
                sp.dma_start(dst.rearrange("s (k p) n -> k p s n", p=P)[q % 2, :, :, bass.ds(c * N, N)],
                             split[q % 2][:]).then_inc(s_out[q % 2], 16)

            def store_v(c):
                sp.wait_ge(vd, c * 2 + 2)
                sp.dma_start(tokens(dr["v"], c), vb[:].rearrange("p t h d -> p t (h d)")).then_inc(v_out, 16)

            def chunk(i, prev, more):
                if prev is not None:
                    store_split(prev, 0)
                if more:
                    load_sums(i + 1)
                if prev is not None:
                    store_split(prev, 1)
                    store_split(prev, 2)
                if more:
                    load_x(i + 1)
                sp.wait_ge(y0d, i * T + T)
                sp.dma_start(tokens(dr["y0"], i), y0[:]).then_inc(y_out, 16)
                if prev is not None:
                    store_split(prev, 3)
                    store_v(prev)

            load_sums(0)
            load_x(0)
            chunk(0, None, True)
            chunk(1, 0, True)
            with sp.Fori(2, CHUNKS - 1) as i:
                chunk(i, i - 1, True)
            chunk(CHUNKS - 1, CHUNKS - 2, False)
            for q in range(4):
                store_split(CHUNKS - 1, q)
            store_v(CHUNKS - 1)
            sp.wait_ge(y_out, 16 * CHUNKS)
            sp.wait_ge(v_out, 16 * CHUNKS)
            for u in range(2):
                sp.wait_ge(s_out[u], 16 * CHUNKS * 2)

        @block.scalar
        def _(a):
            for dst, src in LOADS:
                a.dma_start(dst, src).then_inc(w_in, 16)
            a.wait_ge(half, 1)

            def gate_in(i):
                a.wait_ge(se1, i + 1)
                nc.scalar.activation(s1[:], p1[:], ACT.Silu, bias=bse1[:, 0:1]).then_inc(silu1, 1)

            def gate_out(i):
                for k in range(KC):
                    a.wait_ge(se2, i * KC + k + 1)
                    nc.scalar.activation(th[:, k, :], pA[:, k, :], ACT.Tanh, bias=hb2[:, k:k + 1], scale=0.5).then_inc(tanhed, 1)

            def output(i):
                a.wait_ge(outed, i + 1)
                a.wait_ge(added, i)
                nc.scalar.activation(so[:], pO[:], ACT.Silu, scale=0.5).then_inc(silu3, 1)

            def z(i):
                a.wait_ge(turned, i + 1)
                for k in range(KC):
                    nc.scalar.activation(zT[:, k, :], pA[:, k, :], ACT.Identity, bias=ln_b[:, k:k + 1],
                                         scale=ln_w[:, k:k + 1]).then_inc(zd, 1)

            def top(c, q):
                u = q % 2
                a.wait_ge(part, c * PARTS + q + 1)
                a.wait_ge(s_out[u], (c * 2 + q // 2) * 16)
                a.activation(split[u][:, 0, :], pQ[q % 3][:], ACT.Copy, scale=DK ** -0.5 if q < 2 else 1.0).then_inc(hi, 1)
                a.wait_ge(left, c * 4 + q + 1)
                a.activation(split[u][:, 1, :], rest[u][:], ACT.Copy).then_inc(midd, 1)

            def values(c, q):
                a.wait_ge(part, c * PARTS + q + 1)
                a.wait_ge(v_out, c * 16)
                a.copy(vb[:, 2 * (q - 4):2 * (q - 4) + 2, :, 0:DK],
                       pQ[q % 3][:].rearrange("p (t h d) -> p t h d", t=2, h=H)).then_inc(vd, 1)

            def chunk(i, prev):
                gate_in(i)
                if prev is not None:
                    top(prev, 0)
                gate_out(i)
                if prev is not None:
                    top(prev, 1)
                    top(prev, 2)
                output(i)
                if prev is not None:
                    top(prev, 3)
                    values(prev, 4)
                    values(prev, 5)
                z(i)

            chunk(0, None)
            chunk(1, 0)
            with a.Fori(2, CHUNKS) as i:
                chunk(i, i - 1)
            for q in range(4):
                top(CHUNKS - 1, q)
            for q in range(4, 6):
                values(CHUNKS - 1, q)

        @block.vector
        def _(dve):
            v = nc.vector
            dve.wait_ge(w_in, WAITS)
            v.tensor_scalar(hb2[:], bse2[:], 0.5, None, ALU.mult).then_inc(half, 1)

            def remain(c, q):
                u = q % 2
                dve.wait_ge(hi, c * 4 + q + 1)
                dve.wait_ge(lo, c * 4 + q - 1) if q >= 2 else dve.wait_ge(lo, c * 4)
                v.scalar_tensor_tensor(out=rest[u][:], in0=pQ[q % 3][:], scalar=DK ** -0.5 if q < 2 else 1.0,
                                       in1=split[u][:, 0, :], op0=ALU.mult, op1=ALU.subtract).then_inc(left, 1)

            def chunk(i, prev):
                if prev is not None:
                    remain(prev, 0)
                dve.wait_ge(tanhed, i * KC + KC)
                dve.wait_ge(outed, i)
                v.scalar_tensor_tensor(out=gated[:], in0=th[:], scalar=1.0, in1=oT[:], op0=ALU.add,
                                       op1=ALU.mult).then_inc(gate, 1)
                if prev is not None:
                    remain(prev, 1)
                    remain(prev, 2)
                dve.wait_ge(silu3, i + 1)
                dve.wait_ge(x_in, i * 16 + 16)
                v.tensor_tensor(res[:], so[:], xc[:], ALU.add).then_inc(added, 1)
                dve.wait_ge(added, i + 1)
                for t in range(T):
                    v.bn_stats(st[:, t, :], res[:, t, :]).then_inc(stats, 1)
                dve.wait_ge(stats, i * T + T)
                v.tensor_copy(seen[:], st[:, T - 1, 0:1]).then_inc(waited, 1)
                for t in range(T):
                    v.bn_aggr(mv[:, t, :], st[:, t, :]).then_inc(aggred, 1)
                dve.wait_ge(inv, i * INV + 2)
                dve.wait_ge(y_out, i * 16)
                for t in range(T):
                    v.tensor_scalar(y0[:, t, :], res[:, t, :], mv[:, t, 0:1], rs[:, t:t + 1],
                                    ALU.subtract, ALU.mult).then_inc(y0d, 1)
                dve.wait_ge(inv, i * INV + INV)
                for t in range(T):
                    dve.wait_ge(y0d, i * T + t + 1)
                    v.tensor_scalar(n1[:, t, :], y0[:, t, :], rs2[:, t:t + 1], None, ALU.mult).then_inc(n1d, 1)
                if prev is not None:
                    remain(prev, 3)

            chunk(0, None)
            chunk(1, 0)
            with dve.Fori(2, CHUNKS) as i:
                chunk(i, i - 1)
            for q in range(4):
                remain(CHUNKS - 1, q)

        @block.gpsimd
        def _(pool):
            g = nc.gpsimd
            g.memset(eps[:], EPS).then_inc(ones, 1)
            g.memset(power[:], -0.5).then_inc(ones, 1)
            g.memset(vb[:, :, :, DK:2 * DK], 1.0).then_inc(ones, 1)
            pool.wait_ge(ones, 3)

            def low(c, q):
                u = q % 2
                pool.wait_ge(midd, c * 4 + q + 1)
                g.tensor_tensor(split[u][:, 2, :], rest[u][:], split[u][:, 1, :], ALU.subtract).then_inc(lo, 1)

            def chunk(i, prev):
                if prev is not None:
                    for q in range(3):
                        low(prev, q)
                c = Chain(pool, inv, i * INV)
                pool.wait_ge(aggred, i * T + T)
                pool.wait_ge(n1d, i * T)
                c.link(g.tensor_tensor(ve[:], mv[:, :, 1], eps[:], ALU.add))
                c.link(g.tensor_tensor(rs[:], ve[:], power[:], ALU.pow))
                c.link(g.tensor_tensor(vn[:], mv[:, :, 1], rs[:], ALU.mult))
                c.link(g.tensor_tensor(ve[:], vn[:], rs[:], ALU.mult))
                c.link(g.tensor_tensor(vn[:], ve[:], eps[:], ALU.add))
                c.link(g.tensor_tensor(rs2[:], vn[:], power[:], ALU.pow))
                if prev is not None:
                    low(prev, 3)

            chunk(0, None)
            chunk(1, 0)
            with pool.Fori(2, CHUNKS) as i:
                chunk(i, i - 1)
            for q in range(4):
                low(CHUNKS - 1, q)

        @block.tensor
        def _(pe):
            pe.wait_ge(w_in, WAITS)

            def parts(c, q):
                pe.wait_ge(zd, c * KC + KC)
                if q < 3:
                    pe.wait_ge(vd, c * 2)
                    pe.wait_ge(left, c * 4)
                else:
                    pe.wait_ge(left, c * 4 + q - 2)
                if q < 4:
                    for k in range(KC):
                        last = nc.tensor.matmul(pQ[q % 3][:], wqkv[:, k, q * P:(q + 1) * P], zT[:, k, :],
                                                start=(k == 0), stop=(k == KC - 1))
                else:
                    for t in range(2):
                        for k in range(KC):
                            tile = 2 * (q - 4) + t
                            last = nc.tensor.matmul(pQ[q % 3][:, t * C:(t + 1) * C], zT[:, k, tile * P:(tile + 1) * P],
                                                    wqkv[:, k, 2 * C:3 * C], start=(k == 0), stop=(k == KC - 1))
                last.then_inc(part, 1)

            def chunk(i, prev):
                pe.wait_ge(o_in, i * 16 + 16)
                pe.wait_ge(silu1, i)
                for k in range(KC):
                    last = nc.tensor.matmul(p1[:], wse1[:, k, :], oT[:, k, :], start=(k == 0), stop=(k == KC - 1))
                last.then_inc(se1, 1)
                if prev is not None:
                    parts(prev, 0)
                pe.wait_ge(silu1, i + 1)
                pe.wait_ge(zd, i * KC)
                for k in range(KC):
                    nc.tensor.matmul(pA[:, k, :], wse2[:, k, :], s1[:], start=True, stop=True).then_inc(se2, 1)
                if prev is not None:
                    parts(prev, 1)
                    parts(prev, 2)
                pe.wait_ge(gate, i + 1)
                pe.wait_ge(silu3, i)
                for t in range(T):
                    for k in range(KC):
                        last = nc.tensor.matmul(pO[:, t, :], gated[:, k, t * P:(t + 1) * P], wout[:, k, :],
                                                start=(k == 0), stop=(k == KC - 1))
                last.then_inc(outed, 1)
                if prev is not None:
                    for q in range(3, PARTS):
                        parts(prev, q)
                pe.wait_ge(tanhed, i * KC + KC)
                for t in range(T):
                    pe.wait_ge(n1d, i * T + t + 1)
                    for k in range(KC):
                        last = nc.tensor.transpose(pA[:, k, t * P:(t + 1) * P], n1[:, t, k * P:(k + 1) * P], ident[:])
                last.then_inc(turned, 1)

            chunk(0, None)
            chunk(1, 0)
            with pe.Fori(2, CHUNKS) as i:
                chunk(i, i - 1)
            for q in range(PARTS):
                parts(CHUNKS - 1, q)


def attention(nc, sem, sb, ps, io, dr, ident, w1, w2, w_in):
    UNITS = B * H // 2
    STACK = [(0, 0), (0, 1), (1, 0), (1, 1), (0, 2), (2, 0)]
    ROWS = DK * len(STACK)
    FULL = ROWS + 3
    HALF = L // 2
    PIECES = 2 * BT
    MAXIMA = 2 * PIECES
    RING = 4
    PV0, RED0 = 2, 2
    LOADS = 2 * len(STACK) * 16
    TOPS = 4
    PER = MAXIMA // BT
    TURN = 5

    qst = [sb(f"at_q{i}", [FULL, 2, L], BF16) for i in range(RING)]
    kst = [sb(f"at_k{i}", [FULL, 2, L], BF16) for i in range(RING)]
    vst = [sb(f"at_v{i}", [P, BT, 2, 2 * DK]) for i in range(RING)]
    pt = [sb(f"at_p{i}", [P, 2, HALF]) for i in range(4)]
    mx, top_ = [sb(f"at_mx{i}", [P, PIECES, 2]) for i in range(2)], sb("at_top", [P, PIECES])
    tail = sb("at_tail", [PIECES, P])
    top3 = [sb(f"at_top3{i}", [PIECES, 3, P], BF16) for i in range(2)]
    oe = sb("at_oe", [P, HALF])
    rden, yn = sb("at_rden", [P, 8, 2]), [sb(f"at_yn{i}", [P, 8, 2, 2 * DK]) for i in range(2)]
    pst = [ps(f"at_pst{i}", [P, 2, HALF]) for i in range(2)]
    pmx = [ps(f"at_pmx{i}", [P, HALF]) for i in range(2)]
    pacc, pm = ps("at_pacc", [P, HALF]), ps("at_pm", [P, 8, 2, 2 * DK])
    one_rows = sem("at_ones")
    ld = [sem(f"at_load{i}") for i in range(RING)]
    v_in = [sem(f"at_v_in{i}") for i in range(RING)]
    scored, exped, pv, red, mxmm = (sem("at_" + n) for n in ("scored", "exp", "pv", "reduced", "maxima"))
    topped, topT, split, rows_in, oed, oT, yd, rd = (sem("at_" + n) for n in ("top", "topT", "top_split", "top_rows", "acc_out", "outT", "y", "rden"))
    y_out = [sem(f"at_y_out{i}") for i in range(2)]
    negT = pm[0:PIECES, 0:2, :, :].rearrange("p t h d -> p (t h d)")

    with nc.Block() as block:
        def beside(w, u, s):
            ahead, m = (1, (BT - TURN + s) * PER) if s < TURN else (2, (s - TURN) * PER)
            if isinstance(w, int) and w + ahead >= UNITS:
                return []
            return [(w + ahead, (u + ahead) % RING, m + n) for n in range(PER)]

        def early():
            return [(0, 0, m) for m in range(MAXIMA)] + [(1, 1, m) for m in range((BT - TURN) * PER)]

        def turns(w):
            return not isinstance(w, int) or w + 1 < UNITS

        def units(eng, unit):
            for u in range(RING):
                unit(u, 0, u)
            with eng.Fori(1, UNITS // RING - 1) as i:
                for u in range(RING):
                    unit(i * RING + u, i, u)
            for u in range(RING):
                unit(UNITS - RING + u, UNITS // RING - 1, u)

        @block.sync
        def _(sp):
            def place(i, u):
                per = H // 2 // RING
                return i // per, (i % per) * RING + u

            def load(i, u):
                b, pair = place(i, u)
                def part(d, n):
                    return d[n, bass.ds(pair * (2 * DK), 2 * DK), bass.ds(b * L, L)].rearrange("(h d) n -> d h n", d=DK)
                for n, (pq, pk) in enumerate(STACK):
                    rows = slice(n * DK, (n + 1) * DK)
                    sp.dma_start(qst[u][rows, :, :], part(dr["qs"], pq)).then_inc(ld[u], 16)
                    sp.dma_start(kst[u][rows, :, :], part(dr["ks"], pk)).then_inc(ld[u], 16)
                sp.dma_start(vst[u][:].rearrange("p t h d -> p t (h d)"),
                             dr["v"][bass.ds(b * L, L), bass.ds(pair * (4 * DK), 4 * DK)].rearrange("(t p) n -> p t n", p=P)).then_inc(v_in[u], 16)

            def store_top(w, u):
                sp.wait_ge(split, w * TOPS + TOPS)
                for n in range(3):
                    sp.dma_start(qst[u][ROWS + n:ROWS + n + 1, :, :].rearrange("o h (t n) -> o (h t) n", t=BT),
                                 top3[u % 2][:, n, :]).then_inc(rows_in, 16)

            def store_y(w, i, u):
                b, pair = place(i, u - 1)
                sp.wait_ge(yd, w + 1)
                y = dr["Y"][bass.ds(b * L, L), bass.ds(pair * (2 * DK), 4 * DK)].rearrange("(x t p) c -> x p t c", x=2, p=P)
                src = yn[u // 2][:].rearrange("p (t x) q c -> p t x (q c)", x=2)
                for x in range(2):
                    sp.dma_start(y[x], src[:, :, x, :]).then_inc(y_out[u // 2], 16)

            def unit(w, i, u):
                first, left = isinstance(w, int) and w == 0, not isinstance(w, int) or w + 3 < UNITS
                if left and not first:
                    sp.wait_ge(pv, PV0 + w * BT)
                    load(i if u == 0 else i + 1, (u + 3) % RING)
                if u % 2:
                    q, hc = u // 2, HID // P // 2
                    sp.dma_start(w1[:, q, bass.ds(i, 1), :], io["L0_ffn_w1"][bass.ds(i, 1), q * P:(q + 1) * P, :].rearrange("e p n -> p e n")).then_inc(w_in, 16)
                    sp.dma_start(w2[:, q * hc:(q + 1) * hc, bass.ds(i, 1), :],
                                 io["L0_ffn_w2"][bass.ds(i, 1), q * hc * P:(q + 1) * hc * P, :].rearrange("e (t p) n -> p t e n", p=P)).then_inc(w_in, 16)
                elif not first:
                    store_y(w - 1, i if u else i - 1, (u - 1) % RING)
                if turns(w):
                    store_top(w + 1, (u + 1) % RING)

            for u in range(3):
                load(0, u)
            store_top(0, 0)
            sp.wait_ge(mxmm, 1)
            load(0, 3)
            units(sp, unit)
            store_y(UNITS - 1, UNITS // RING - 1, RING - 1)
            for n in range(2):
                sp.wait_ge(y_out[n], 32 * (UNITS // RING))
            sp.wait_ge(w_in, 16 * 2 * 2 * E)

        @block.gpsimd
        def _(pool):
            for k in kst:
                nc.gpsimd.memset(k[ROWS:FULL, :, :], 1.0).then_inc(one_rows, 1)

        @block.scalar
        def _(a):
            def out(w):
                a.wait_ge(pv, PV0 + (w + 1) * BT)
                a.wait_ge(oT, w)
                a.copy(oe[:], pacc[:]).then_inc(oed, 1)

            def unit(w, i, u):
                for s in range(BT):
                    for p in range(2):
                        a.wait_ge(scored, w * (2 * BT) + 2 * s + p + 1)
                        a.wait_ge(pv, w * BT + s + 1)
                        a.activation(pt[(2 * s + p) % 4][:], pst[p][:], ACT.Exp).then_inc(exped, 1)
                    if s == 0 and not (isinstance(w, int) and w == 0):
                        out(w - 1)

            units(a, unit)
            out(UNITS - 1)

        @block.vector
        def _(dve):
            v = nc.vector

            def maximum(w, u, m):
                dve.wait_ge(mxmm, w * MAXIMA + m + 1)
                v.reduce_max(mx[u % 2][:, m // 2, m % 2:m % 2 + 1], pmx[m % 2][:], AX.X).then_inc(red, 1)

            def tops(w, u):
                dve.wait_ge(red, RED0 + (w + 1) * MAXIMA)
                v.tensor_tensor(top_[:], mx[u % 2][:, :, 0], mx[u % 2][:, :, 1], ALU.max).then_inc(topped, 1)

            def split_tops(w, u, link):
                t = top3[u % 2]
                if link == 0:
                    dve.wait_ge(topT, w + 1)
                    ins = (v.tensor_scalar(t[:, 0, :], negT, -1.0, None, ALU.mult))
                elif link == 1:
                    dve.wait_ge(split, w * TOPS + link)
                    ins = (v.scalar_tensor_tensor(out=tail[:], in0=negT, scalar=-1.0, in1=t[:, 0, :], op0=ALU.mult, op1=ALU.subtract))
                elif link == 2:
                    dve.wait_ge(split, w * TOPS + link)
                    ins = (v.tensor_copy(t[:, 1, :], tail[:]))
                else:
                    dve.wait_ge(split, w * TOPS + link)
                    ins = (v.tensor_tensor(t[:, 2, :], tail[:], t[:, 1, :], ALU.subtract))
                ins.then_inc(split, 1)

            def invert(w):
                dve.wait_ge(oT, w + 1)
                v.reciprocal(rden[:], pm[:, :, :, DK]).then_inc(rd, 1)

            def normalise(w, i, u):
                dve.wait_ge(rd, w + 1)
                if u % 2 == 0:
                    dve.wait_ge(y_out[u // 2], i * 32)
                v.tensor_tensor(yn[u // 2][:, :, u % 2, :].rearrange("p t (h d) -> p t h d", h=2), pm[:, :, :, 0:DK],
                                rden[:].unsqueeze(3).to_broadcast([P, 8, 2, DK]), ALU.mult).then_inc(yd, 1)

            def unit(w, i, u):
                first = isinstance(w, int) and w == 0
                for s in range(BT):
                    ms = beside(w, u, s)
                    for n in range(PER):
                        if ms:
                            maximum(*ms[n])
                        if s == 2 and not first:
                            if n == 1:
                                invert(w - 1)
                            if n == 2:
                                normalise(w - 1, i if u else i - 1, (u - 1) % RING)
                        if turns(w):
                            if s == TURN - 1 and n == PER - 1:
                                tops(w + 1, u + 1)
                            link = (s - TURN) * PER + n - 1
                            if 0 <= link < TOPS:
                                split_tops(w + 1, u + 1, link)

            dve.sem_inc(red, RED0)
            for e in early():
                maximum(*e)
                if e[0] == 0 and e[2] == MAXIMA - 1:
                    tops(0, 0)
                if e[0] == 1 and e[2] < TOPS:
                    split_tops(0, 0, e[2])
            units(dve, unit)
            invert(UNITS - 1)
            normalise(UNITS - 1, UNITS // RING - 1, RING - 1)

        @block.tensor
        def _(pe):
            def maximum(w, u, m):
                h, nt, kh = m // (2 * BT), m // 2 % BT, m % 2
                if m == 0:
                    pe.wait_ge(ld[u], (w // RING + 1) * LOADS)
                pe.wait_ge(red, w * MAXIMA + m + 1)
                nc.tensor.matmul(pmx[kh][:], qst[u][0:ROWS, h, nt * P:(nt + 1) * P],
                                 kst[u][0:ROWS, h, kh * HALF:(kh + 1) * HALF], start=True, stop=True).then_inc(mxmm, 1)

            def turn_tops(w):
                pe.wait_ge(topped, w + 1)
                nc.tensor.transpose(negT, top_[:], ident[:]).then_inc(topT, 1)

            def turn_out(w):
                pe.wait_ge(oed, w + 1)
                pmf = pm[:].rearrange("p (t x) h d -> p t (x h d)", x=2)
                for t in range(4):
                    last = nc.tensor.transpose(pmf[:, t, :], oe[:, t * P:(t + 1) * P], ident[:])
                last.then_inc(oT, 1)

            def scores(w, u, s, p):
                if not (isinstance(w, int) and w == 0 and s == 0):
                    pe.wait_ge(exped, w * (2 * BT) + 2 * s + p - 1)
                for h in range(2):
                    last = nc.tensor.matmul(pst[p][:, h, :], kst[u][:, h, s * P:(s + 1) * P],
                                            qst[u][:, h, p * HALF:(p + 1) * HALF], start=True, stop=True)
                last.then_inc(scored, 1)

            def values(w, u, s):
                pe.wait_ge(exped, w * (2 * BT) + 2 * s + 2)
                if s == 0:
                    pe.wait_ge(oed, w)
                for p in range(2):
                    for h in range(2):
                        at = (2 * p + h) * 2 * DK
                        last = nc.tensor.matmul(pacc[at:at + 2 * DK, :], vst[u][:, s, h, :],
                                                pt[(2 * s + p) % 4][:, h, :], start=(s == 0), stop=(s == BT - 1))
                last.then_inc(pv, 1)

            def unit(w, i, u):
                first = isinstance(w, int) and w == 0
                pe.wait_ge(rows_in, (w + 1) * 48)
                pe.wait_ge(v_in[u], (i + 1) * 16)
                for s in range(BT):
                    ms = beside(w, u, s)
                    scores(w, u, s, 0)
                    for m in ms[0:1]:
                        maximum(*m)
                    scores(w, u, s, 1)
                    for m in ms[1:2]:
                        maximum(*m)
                    if s:
                        values(w, u, s - 1)
                    elif not first:
                        values(w - 1, (u - 1) % RING, BT - 1)
                    if s == 2 and not first:
                        if turns(w - 1):
                            pe.wait_ge(split, (w + 1) * TOPS)
                        turn_out(w - 1)
                    if s == TURN and turns(w):
                        if not first:
                            pe.wait_ge(yd, w)
                        turn_tops(w + 1)
                    for m in ms[2:]:
                        maximum(*m)

            pe.sem_inc(pv, PV0)
            pe.wait_ge(one_rows, RING)
            for e in early():
                maximum(*e)
                if e[0] == 0 and e[2] == MAXIMA - 1:
                    turn_tops(0)
            units(pe, unit)
            values(UNITS - 1, RING - 1, BT - 1)
            pe.wait_ge(yd, UNITS - 1)
            turn_out(UNITS - 1)


def project_and_gate(nc, sem, sb, ps, io, dr, ident, n2, logits):
    T = 4
    N = T * P
    CHUNKS = TOKENS // N
    INV = 2
    wp, gw, gb = sb("pg_wproj", [P, KC, C]), sb("pg_gw", [P, KC, E]), sb("pg_gb", [P, E])
    ln_w, ln_b = sb("pg_lnw", [P, KC]), sb("pg_lnb", [P, KC])
    yc, y0 = sb("pg_y", [P, T, C]), sb("pg_y0", [P, T, C])
    yT, zT = sb("pg_yT", [P, KC, N]), sb("pg_zT", [P, KC, N])
    x3 = sb("pg_x3", [P, T, C])
    x2, nc2 = sb("pg_x2", [P, T, C]), sb("pg_n2", [P, T, C])
    st, mv, seen = sb("pg_st", [P, T, 6]), sb("pg_mv", [P, T, 2]), sb("pg_seen", [P, 1])
    eps, power, ve, rs = (sb("pg_" + n, [P, T]) for n in ("eps", "power", "ve", "rs"))
    zero = sb("pg_zero", [P, C])
    pY, pO, pN, pG = ps("pg_pY", [P, KC, N]), ps("pg_pO", [P, T, C]), ps("pg_pN", [P, KC, N]), ps("pg_pG", [P, T, E])
    kept, summed = sem("pg_kept"), sem("pg_summed")
    w_in, y_in, y0_in, consts, zeroed = (sem("pg_" + n) for n in ("w_in", "y_in", "y0_in", "consts", "zeroed"))
    turned, yTd, outed, added, stats, waited, aggred, inv, n2d, nT, zd, gated, logd, x3_out = (sem("pg_" + n) for n in (
        "turned", "yT", "projected", "added", "stats", "waited", "aggr", "rstd", "n2", "n2T", "zT", "gate", "logits", "x3_out"))
    LOADS = [(wp[:], io["L0_ffn_w_proj"].rearrange("(k p) n -> p k n", p=P)),
             (gw[:], io["L0_ffn_gate_w"].rearrange("(k p) n -> p k n", p=P)),
             (gb[:], io["L0_ffn_gate_b"].rearrange("(o n) -> o n", o=1).to_broadcast([P, E])),
             (ln_w[:], io["L0_ffn_ln2_w"].rearrange("(k p) -> p k", p=P)),
             (ln_b[:], io["L0_ffn_ln2_b"].rearrange("(k p) -> p k", p=P))]
    WAITS = 16 * len(LOADS)

    def tokens(d, i):
        return d[bass.ds(i * N, N), :].rearrange("(t p) c -> p t c", p=P)

    def skewed(eng, chunk):
        chunk(0, None)
        chunk(1, 0)
        with eng.Fori(2, CHUNKS) as i:
            chunk(i, i - 1)
        chunk(None, CHUNKS - 1)

    with nc.Block() as block, nc.allow_non_contiguous_dma(reason="per-channel vectors"):
        @block.sync
        def _(sp):
            def each(i):
                sp.wait_ge(turned, i)
                sp.dma_start(yc[:], tokens(dr["Y"], i)).then_inc(y_in, 16)
                sp.wait_ge(summed, i)
                sp.dma_start(y0[:], tokens(dr["y0"], i)).then_inc(y0_in, 16)

            each(0)
            with sp.Fori(1, CHUNKS) as i:
                each(i)
            sp.wait_ge(consts, 3)
            sp.dma_start(dr["zs"].rearrange("(t p) c -> p t c", p=P),
                         zero[:].unsqueeze(1).to_broadcast([P, MT, C])).then_inc(zeroed, 16)
            sp.wait_ge(zeroed, 16)

        @block.gpsimd
        def _(pool):
            g = nc.gpsimd
            g.memset(eps[:], EPS).then_inc(consts, 1)
            g.memset(power[:], -0.5).then_inc(consts, 1)
            g.memset(zero[:], 0.0).then_inc(consts, 1)
            pool.wait_ge(consts, 3)
            def each(i):
                pool.wait_ge(added, i + 1)
                pool.wait_ge(x3_out, i * 16)
                g.tensor_tensor(x3[:], x2[:], y0[:], ALU.add).then_inc(summed, 1)
                c = Chain(pool, inv, i * INV)
                pool.wait_ge(aggred, i * T + T)
                pool.wait_ge(n2d, i * T)
                c.link(g.tensor_tensor(ve[:], mv[:, :, 1], eps[:], ALU.add))
                c.link(g.tensor_tensor(rs[:], ve[:], power[:], ALU.pow))
                assert c.n == INV

            each(0)
            with pool.Fori(1, CHUNKS) as i:
                each(i)

        @block.scalar
        def _(a):
            for dst, src in LOADS:
                a.dma_start(dst, src).then_inc(w_in, 16)

            def chunk(i, prev):
                if i is not None:
                    a.wait_ge(turned, i + 1)
                    a.wait_ge(outed, i)
                    a.copy(yT[:], pY[:]).then_inc(yTd, 1)
                if prev is not None:
                    a.wait_ge(nT, prev + 1)
                    a.wait_ge(gated, prev)
                    a.wait_ge(w_in, WAITS)
                    for k in range(KC):
                        a.activation(zT[:, k, :], pN[:, k, :], ACT.Identity, bias=ln_b[:, k:k + 1],
                                     scale=ln_w[:, k:k + 1]).then_inc(zd, 1)
                if i is not None:
                    a.wait_ge(summed, i + 1)
                    a.dma_start(tokens(dr["x3"], i), x3[:]).then_inc(x3_out, 16)
                    a.wait_ge(n2d, i * T + T)
                    a.copy(n2[:, bass.ds(i * T, T), :], nc2[:]).then_inc(kept, 1)

            a.wait_ge(w_in, WAITS)
            chunk(0, None)
            chunk(1, 0)
            with a.Fori(2, CHUNKS) as i:
                chunk(i, i - 1)
            chunk(None, CHUNKS - 1)
            a.wait_ge(x3_out, 16 * CHUNKS)

        @block.vector
        def _(dve):
            v = nc.vector
            dve.wait_ge(w_in, WAITS)

            def chunk(i, prev):
                if i is not None:
                    dve.wait_ge(outed, i + 1)
                    dve.wait_ge(y0_in, i * 16 + 16)
                    dve.wait_ge(summed, i)
                    v.tensor_tensor(x2[:], pO[:], y0[:], ALU.add).then_inc(added, 1)
                    dve.wait_ge(added, i + 1)
                    for t in range(T):
                        v.bn_stats(st[:, t, :], x2[:, t, :]).then_inc(stats, 1)
                    dve.wait_ge(stats, i * T + T)
                    v.tensor_copy(seen[:], st[:, T - 1, 0:1]).then_inc(waited, 1)
                    for t in range(T):
                        v.bn_aggr(mv[:, t, :], st[:, t, :]).then_inc(aggred, 1)
                if prev is not None:
                    dve.wait_ge(gated, prev + 1)
                    v.tensor_tensor(logits[:, bass.ds(prev * T, T), :], pG[:], gb[:].unsqueeze(1).to_broadcast([P, T, E]),
                                    ALU.add).then_inc(logd, 1)
                if i is not None:
                    dve.wait_ge(inv, i * INV + INV)
                    dve.wait_ge(nT, i)
                    dve.wait_ge(kept, i)
                    for t in range(T):
                        v.tensor_scalar(nc2[:, t, :], x2[:, t, :], mv[:, t, 0:1], rs[:, t:t + 1],
                                        ALU.subtract, ALU.mult).then_inc(n2d, 1)

            skewed(dve, chunk)

        @block.tensor
        def _(pe):
            pe.wait_ge(w_in, WAITS)

            def chunk(i, prev):
                if i is not None:
                    pe.wait_ge(y_in, i * 16 + 16)
                    pe.wait_ge(yTd, i)
                    for t in range(T):
                        for k in range(KC):
                            last = nc.tensor.transpose(pY[:, k, t * P:(t + 1) * P], yc[:, t, k * P:(k + 1) * P], ident[:])
                    last.then_inc(turned, 1)
                if prev is not None:
                    pe.wait_ge(zd, prev * KC)
                    pe.wait_ge(n2d, prev * T + T)
                    for t in range(T):
                        for k in range(KC):
                            last = nc.tensor.transpose(pN[:, k, t * P:(t + 1) * P], nc2[:, t, k * P:(k + 1) * P], ident[:])
                    last.then_inc(nT, 1)
                if i is not None:
                    pe.wait_ge(yTd, i + 1)
                    pe.wait_ge(added, i)
                    for t in range(T):
                        for k in range(KC):
                            last = nc.tensor.matmul(pO[:, t, :], yT[:, k, t * P:(t + 1) * P], wp[:, k, :],
                                                    start=(k == 0), stop=(k == KC - 1))
                    last.then_inc(outed, 1)
                if prev is not None:
                    pe.wait_ge(zd, prev * KC + KC)
                    pe.wait_ge(logd, prev)
                    for t in range(T):
                        for k in range(KC):
                            last = nc.tensor.matmul(pG[:, t, :], zT[:, k, t * P:(t + 1) * P], gw[:, k, :],
                                                    start=(k == 0), stop=(k == KC - 1))
                    last.then_inc(gated, 1)

            skewed(pe, chunk)


def dispatch(nc, sem, sb, ps, dr, n2, logits, slot, expert):
    top1, m8, first = sb("ds_max", [P, TILES]), sb("ds_m8", [P, TILES, E]), sb("ds_first", [P, TILES])
    eq, hot = sb("ds_eq", [P, TILES, E]), sb("ds_hot", [P, TILES, E])
    es, back = sb("ds_es", [P, E]), sb("ds_back", [P, E])
    lower, ones = sb("ds_lower", [P, P]), sb("ds_ones", [P, P])
    run = [sb(f"ds_run{i}", [P, TILES, E]) for i in range(2)]
    tot = sb("ds_tot", [P, TILES, E])
    cum = [sb(f"ds_cum{i}", [P, E]) for i in range(2)]
    tiles, start = sb("ds_tiles", [P, E]), sb("ds_start", [P, E])
    slotf = sb("ds_slotf", [P, TILES])
    js, past, exf = sb("ds_js", [1, MT]), sb("ds_past", [1, MT, E]), sb("ds_exf", [1, MT])
    pW, pT = ps("ds_pW", [P, TILES * E]), ps("ds_pT", [P, TILES * E])
    consts, d, hotd, counted, placed, sent = (sem("ds_" + n) for n in ("consts", "dve", "hot", "counted", "placed", "sent"))
    MAGIC = 1.5 * 2.0 ** 23

    with nc.Block() as block:
        @block.gpsimd
        def _(pool):
            g = nc.gpsimd
            g.iota(es[:], pattern=[[1, E]], base=0, channel_multiplier=0, allow_small_or_imprecise_dtypes=True).then_inc(consts, 1)
            g.iota(back[:], pattern=[[-1, E]], base=E, channel_multiplier=0, allow_small_or_imprecise_dtypes=True).then_inc(consts, 1)
            g.iota(js[:], pattern=[[1, MT]], base=0, channel_multiplier=0, allow_small_or_imprecise_dtypes=True).then_inc(consts, 1)
            g.memset(ones[:], 1.0).then_inc(consts, 1)
            pool.wait_ge(consts, 4)
            g.affine_select(out=lower[:], in_=ones[:], compare_op=ALU.is_gt, fill=0.0, base=0,
                            pattern=[[1, P]], channel_multiplier=-1).then_inc(consts, 1)
            pool.wait_ge(placed, 1)
            for t in range(TILES):
                pool.indirect_dma_start(out=dr["zs"], out_offset=bass.IndirectOffsetOnAxis(ap=slot[:, t:t + 1], axis=0),
                                        in_=n2[:, t, :], in_offset=None).then_inc(sent, 16)
            pool.wait_ge(sent, 16 * TILES)

        @block.tensor
        def _(pe):
            pe.wait_ge(consts, 5)
            pe.wait_ge(hotd, 1)
            h = hot[:].rearrange("p t e -> p (t e)")
            nc.tensor.matmul(pW[:], lower[:], h, start=True, stop=True)
            nc.tensor.matmul(pT[:], ones[:], h, start=True, stop=True).then_inc(counted, 1)

        @block.vector
        def _(dve):
            v = nc.vector
            c = Chain(dve, d)

            def over(a):
                return a[:].unsqueeze(2).to_broadcast([P, TILES, E])

            def row(a):
                return a[:].unsqueeze(1).to_broadcast([P, TILES, E])

            dve.wait_ge(consts, 5)
            c.link(v.tensor_reduce(top1[:], logits[:], AX.X, ALU.max))
            c.link(v.tensor_tensor(eq[:], logits[:], over(top1), ALU.is_equal))
            c.link(v.tensor_tensor(m8[:], eq[:], row(back), ALU.mult))
            c.link(v.tensor_reduce(first[:], m8[:], AX.X, ALU.max))
            v.tensor_tensor(hot[:], over(first), row(back), ALU.is_equal).then_inc(hotd, 1)
            dve.wait_ge(counted, 1)
            c.did(v.tensor_copy(tot[:].rearrange("p t e -> p (t e)"), pT[:]))
            c.link(v.tensor_copy(run[0][:].rearrange("p t e -> p (t e)"), pT[:]))
            u, n = 0, 1
            while n < TILES:
                c.did(v.tensor_copy(run[1 - u][:, 0:n, :], run[u][:, 0:n, :]))
                c.link(v.tensor_tensor(run[1 - u][:, n:, :], run[u][:, n:, :], run[u][:, :TILES - n, :], ALU.add))
                u, n = 1 - u, 2 * n
            c.link(v.tensor_scalar(tiles[:], run[u][:, TILES - 1, :], 1.0 / P, 127.0 / P - 0.5 + 1.0 / 256, ALU.mult, ALU.add))
            c.link(v.tensor_scalar(tiles[:], tiles[:], MAGIC, MAGIC, ALU.add, ALU.subtract))
            c.link(v.tensor_copy(cum[0][:], tiles[:]))
            w, n = 0, 1
            while n < E:
                c.did(v.tensor_copy(cum[1 - w][:, 0:n], cum[w][:, 0:n]))
                c.link(v.tensor_tensor(cum[1 - w][:, n:], cum[w][:, n:], cum[w][:, :E - n], ALU.add))
                w, n = 1 - w, 2 * n
            c.link(v.tensor_tensor(start[:], cum[w][:], tiles[:], ALU.subtract))
            c.link(v.tensor_scalar(start[:], start[:], float(P), None, ALU.mult))
            c.link(v.tensor_tensor(run[u][:], run[u][:], tot[:], ALU.subtract))
            c.link(v.tensor_tensor(tot[:].rearrange("p t e -> p (t e)"), pW[:], run[u][:].rearrange("p t e -> p (t e)"), ALU.add))
            c.link(v.tensor_tensor(run[u][:], tot[:], row(start), ALU.add))
            c.link(v.tensor_tensor(tot[:], run[u][:], hot[:], ALU.mult))
            c.link(v.reduce_sum(slotf[:], tot[:], AX.X))
            v.tensor_copy(slot[:], slotf[:]).then_inc(placed, 1)
            c.link(v.tensor_tensor(past[:], js[:].unsqueeze(2).to_broadcast([1, MT, E]),
                                   cum[w][0:1, :].unsqueeze(1).to_broadcast([1, MT, E]), ALU.is_ge))
            c.link(v.reduce_sum(exf[:], past[:], AX.X))
            c.link(v.tensor_scalar(exf[:], exf[:], float(E - 1), None, ALU.min))
            c.link(v.tensor_copy(expert[:], exf[:]))


def experts(nc, sem, sb, ps, io, dr, ident, w1, w2, expert):
    HC = HID // P
    ln_w, ln_b = sb("ex_lnw", [P, KC]), sb("ex_lnb", [P, KC])
    z = [sb(f"ex_z{i}", [P, C]) for i in range(2)]
    zT = sb("ex_zT", [P, KC, P])
    hs, hT, ys = sb("ex_h", [P, HID]), sb("ex_hT", [P, HC, P]), sb("ex_y", [P, C])
    pZ, pH, pT, pY = ps("ex_pZ", [P, KC, P]), ps("ex_pH", [P, HID]), ps("ex_pT", [P, HC, P]), ps("ex_pY", [P, C])
    w_in, z_in, turned, zd, up, gelu, hturned, hTd, down, yd, y_out = (sem("ex_" + n) for n in (
        "w_in", "z_in", "turned", "zT", "up", "gelu", "h_turned", "hT", "down", "y", "y_out"))

    def skewed(eng, tile):
        tile(0, None, True)
        tile(1, 0, True)
        with eng.Fori(2, MT - 1) as j:
            tile(j, j - 1, True)
        tile(MT - 1, MT - 2, False)
        tile(None, MT - 1, False)

    with nc.Block() as block, nc.allow_non_contiguous_dma(reason="per-channel vectors"):
        @block.sync
        def _(sp):
            sp.dma_start(ln_w[:], io["L0_ffn_ln2_w"].rearrange("(k p) -> p k", p=P)).then_inc(w_in, 16)
            sp.dma_start(ln_b[:], io["L0_ffn_ln2_b"].rearrange("(k p) -> p k", p=P)).then_inc(w_in, 16)

            def load(j):
                sp.wait_ge(turned, j)
                sp.dma_start(z[0][:], dr["zs"][bass.ds(j * P, P), :]).then_inc(z_in, 16)

            def tile(j, prev, more):
                if more:
                    load(j + 1)
                if prev is not None:
                    sp.wait_ge(yd, prev + 1)
                    sp.dma_start(dr["ys"][bass.ds(prev * P, P), :], ys[:]).then_inc(y_out, 16)

            load(0)
            skewed(sp, tile)
            sp.wait_ge(y_out, 16 * MT)

        @block.scalar
        def _(a):
            a.wait_ge(w_in, 32)

            def norm(j):
                a.wait_ge(turned, j + 1)
                a.wait_ge(up, j)
                for k in range(KC):
                    a.activation(zT[:, k, :], pZ[:, k, :], ACT.Identity, bias=ln_b[:, k:k + 1], scale=ln_w[:, k:k + 1]).then_inc(zd, 1)

            def tile(j, prev, more):
                if j is not None:
                    a.wait_ge(up, j + 1)
                    a.wait_ge(hturned, j)
                    a.activation(hs[:], pH[:], ACT.Gelu_apprx_tanh).then_inc(gelu, 1)
                if prev is not None:
                    a.wait_ge(down, prev + 1)
                    a.wait_ge(y_out, prev * 16)
                    a.copy(ys[:], pY[:]).then_inc(yd, 1)
                if more:
                    norm(j + 1)

            norm(0)
            skewed(a, tile)

        @block.vector
        def _(dve):
            def each(j):
                dve.wait_ge(hturned, j + 1)
                dve.wait_ge(down, j)
                nc.vector.tensor_copy(hT[:], pT[:]).then_inc(hTd, 1)

            each(0)
            with dve.Fori(1, MT) as j:
                each(j)

        @block.tensor
        def _(pe):
            def turn(j):
                pe.wait_ge(z_in, j * 16 + 16)
                pe.wait_ge(zd, j * KC)
                for k in range(KC):
                    last = nc.tensor.transpose(pZ[:, k, :], z[0][:, k * P:(k + 1) * P], ident[:])
                last.then_inc(turned, 1)

            def which(j):
                return pe.value_load(expert[0:1, bass.ds(j, 1)], min_val=0, max_val=E - 1)

            def tile(j, prev, more):
                if j is not None:
                    e = which(j)
                    pe.wait_ge(zd, j * KC + KC)
                    pe.wait_ge(gelu, j)
                    for n in range(HID // 512):
                        for k in range(KC):
                            last = nc.tensor.matmul(pH[:, n * 512:(n + 1) * 512], zT[:, k, :],
                                                    w1[:, k, bass.ds(e, 1), n * 512:(n + 1) * 512], start=(k == 0), stop=(k == KC - 1))
                    last.then_inc(up, 1)
                if more:
                    turn(j + 1)
                if prev is not None:
                    e = which(prev)
                    pe.wait_ge(hTd, prev + 1)
                    pe.wait_ge(yd, prev)
                    for c in range(HC):
                        last = nc.tensor.matmul(pY[:], hT[:, c, :], w2[:, c, bass.ds(e, 1), :], start=(c == 0), stop=(c == HC - 1))
                    last.then_inc(down, 1)
                if j is not None:
                    pe.wait_ge(gelu, j + 1)
                    pe.wait_ge(hTd, j)
                    for c in range(HC):
                        last = nc.tensor.transpose(pT[:, c, :], hs[:, c * P:(c + 1) * P], ident[:])
                    last.then_inc(hturned, 1)

            turn(0)
            skewed(pe, tile)


def combine(nc, sem, sb, io, dr, slot):
    T = 4
    N = T * P
    CHUNKS = TOKENS // N
    g_, x2, xo = ([sb(f"cb_{n}{i}", [P, T, C]) for i in range(2)] for n in ("g", "x2", "out"))
    st, mv, seen = sb("cb_st", [P, T, 6]), sb("cb_mv", [P, T, 2]), sb("cb_seen", [P, 1])
    eps, power, ve, rs = (sb("cb_" + n, [P, T]) for n in ("eps", "power", "ve", "rs"))
    consts, added, stats, waited, aggred, inv, outd = (sem("cb_" + n) for n in ("consts", "added", "stats", "waited", "aggr", "rstd", "out"))
    g_in, x_in, o_out = ([sem(f"cb_{n}{i}") for i in range(2)] for n in ("g_in", "x_in", "o_out"))
    out = io["out"].rearrange("b l c -> (b l) c")

    def tokens(d, i):
        return d[i * N:(i + 1) * N, :].rearrange("(t p) c -> p t c", p=P)

    with nc.Block() as block:
        @block.gpsimd
        def _(pool):
            nc.gpsimd.memset(eps[:], EPS).then_inc(consts, 1)
            nc.gpsimd.memset(power[:], -0.5).then_inc(consts, 1)
            pool.wait_ge(consts, 2)

            def gather(i):
                if i >= 2:
                    pool.wait_ge(added, i - 1)
                for t in range(T):
                    pool.indirect_dma_start(out=g_[i % 2][:, t, :], out_offset=None, in_=dr["ys"],
                                            in_offset=bass.IndirectOffsetOnAxis(ap=slot[:, i * T + t:i * T + t + 1], axis=0)
                                            ).then_inc(g_in[i % 2], 16)

            gather(0)
            for i in range(CHUNKS):
                if i + 1 < CHUNKS:
                    gather(i + 1)
                pool.wait_ge(aggred, (i + 1) * T)
                pool.wait_ge(outd, i * T)
                nc.gpsimd.tensor_tensor(ve[:], mv[:, :, 1], eps[:], ALU.add).then_inc(inv, 1)
                pool.wait_ge(inv, 2 * i + 1)
                nc.gpsimd.tensor_tensor(rs[:], ve[:], power[:], ALU.pow).then_inc(inv, 1)

        @block.sync
        def _(sp):
            for i in range(CHUNKS):
                if i >= 2:
                    sp.wait_ge(outd, (i - 1) * T)
                sp.dma_start(x2[i % 2][:], tokens(dr["x3"], i)).then_inc(x_in[i % 2], 16)

        @block.scalar
        def _(a):
            for i in range(CHUNKS):
                a.wait_ge(outd, (i + 1) * T)
                a.dma_start(tokens(out, i), xo[i % 2][:]).then_inc(o_out[i % 2], 16)
            for u in range(2):
                a.wait_ge(o_out[u], 16 * CHUNKS // 2)

        @block.vector
        def _(dve):
            v = nc.vector
            for i in range(CHUNKS):
                u = i % 2
                dve.wait_ge(g_in[u], 16 * T * (i // 2 + 1))
                dve.wait_ge(x_in[u], 16 * (i // 2 + 1))
                v.tensor_tensor(x2[u][:], x2[u][:], g_[u][:], ALU.add).then_inc(added, 1)
                dve.wait_ge(added, i + 1)
                for t in range(T):
                    v.bn_stats(st[:, t, :], x2[u][:, t, :]).then_inc(stats, 1)
                for t in range(T):
                    dve.wait_ge(stats, i * T + t + 1)
                    v.bn_aggr(mv[:, t, :], st[:, t, :]).then_inc(aggred, 1)
                dve.wait_ge(inv, 2 * i + 2)
                if i >= 2:
                    dve.wait_ge(o_out[u], 16 * (i // 2))
                for t in range(T):
                    v.tensor_scalar(xo[u][:, t, :], x2[u][:, t, :], mv[:, t, 0:1], rs[:, t:t + 1],
                                    ALU.subtract, ALU.mult).then_inc(outd, 1)


SCRATCH = {
    "outT": ([C, TOKENS], F32),
    "y0": ([TOKENS, C], F32),
    "qs": ([3, C, TOKENS], BF16),
    "ks": ([3, C, TOKENS], BF16),
    "v": ([TOKENS, H * 2 * DK], F32),
    "Y": ([TOKENS, C], F32),
    "x3": ([TOKENS, C], F32),
    "zs": ([MT * P, C], F32),
    "ys": ([MT * P, C], F32),
}


_INS = ["L0_attn_x", "L0_attn_w_wave", "L0_attn_b_wave", "L0_attn_w_query", "L0_attn_b_query", "L0_attn_key_weight",
        "L0_attn_w_se1", "L0_attn_b_se1", "L0_attn_w_se2", "L0_attn_b_se2", "L0_attn_w_out",
        "L0_ffn_ln1_w", "L0_ffn_ln1_b", "L0_ffn_w_qkv", "L0_ffn_w_proj", "L0_ffn_ln2_w", "L0_ffn_ln2_b",
        "L0_ffn_gate_w", "L0_ffn_gate_b", "L0_ffn_w1", "L0_ffn_w2"]


def kernel(**inputs):
    import numpy as _np
    import concourse.bacc as _bacc
    from concourse.bass_utils import run_bass_kernel_spmd as _run

    nc = _bacc.Bacc("TRN2", target_bir_lowering=False, num_devices=1)
    arrays, io = {}, {}
    for name in _INS:
        a = _np.ascontiguousarray(inputs[name])
        arrays[f"in_{name}"] = a
        io[name] = nc.dram_tensor(f"in_{name}", list(a.shape), mybir.dt.from_np(a.dtype), kind="ExternalInput").ap()
    io["out"] = nc.dram_tensor("out_0", [B, L, C], F32, kind="ExternalOutput").ap()
    dr = {n: nc.dram_tensor(f"scratch_{n}", shape, dt, kind="Internal").ap() for n, (shape, dt) in SCRATCH.items()}
    build(nc, io, dr)
    r = _run(nc, [arrays], core_ids=[0])
    return r.results[0]["out_0"]
```

```python
import concourse.bass as bass
from concourse import mybir
from contextlib import ExitStack

F32 = mybir.dt.float32
BF16 = mybir.dt.bfloat16
I32 = mybir.dt.int32
ALU = mybir.AluOpType
ACT = mybir.ActivationFunctionType
AX = mybir.AxisListType
P = 128

B, L, C = 4, 1024, 256
TOKENS = B * L
TILES = TOKENS // P
BT = L // P
KC = C // P
WH, POS, REACH = 8, 16, 16
WD = C // WH
STEPS = 2 * REACH + 1
NW = 3 * WH + WH * POS
SE = C // 4
H, DK = 16, 16
E, HID = 8, 1024
MT = TILES + E - 1
REGION = TOKENS + P
ROW = 2 * C + 4
EPS = 1e-5


class Chain:

    def __init__(self, eng, sem, base=0):
        self.eng, self.sem, self.base, self.n = eng, sem, base, 0

    def did(self, ins):
        ins.then_inc(self.sem, 1)
        self.n += 1
        return self.n

    def wait(self, n=None):
        self.eng.wait_ge(self.sem, self.base + (self.n if n is None else n))

    def link(self, ins):
        self.did(ins)
        self.wait()


def build(nc, io, dr):
    with ExitStack() as top:
        sems = {}

        def sem(name):
            assert name not in sems
            sems[name] = top.enter_context(nc.semaphore(name))
            return sems[name]

        def sb(ctx, name, shape, dt=F32):
            return ctx.enter_context(nc.sbuf_tensor(name, shape, dt))

        def ps(ctx, name, shape, dt=F32):
            return ctx.enter_context(nc.psum_tensor(name, shape, dt))

        ident = sb(top, "ident", [P, P])
        identb = sb(top, "identb", [P, P], BF16)
        constants(nc, sem, ident, identb)
        early = top.enter_context(ExitStack())
        gates, gate_loads = gate_weights(lambda *a: sb(early, *a), io)
        gates_in = sem("gate_weights_in")
        with ExitStack() as wave:
            par = {n: sb(wave, "par_" + n, [P, TILES]) for n in ("freq", "phase", "invf", "mid", "kmax")}
            par["lpos"] = sb(wave, "par_lpos", [P, TILES])
            par["alpha"] = sb(wave, "par_alpha", [P, TILES, WH])
            par["beta"] = sb(wave, "par_beta", [P, TILES, WH])
            wave_parameters(nc, sem, sb, ps, io, dr, ident, par)
            wave_sampling(nc, sem, sb, ps, io, dr, ident, identb, par, gate_loads, gates_in)
        with ExitStack() as ctx:
            gate_and_project(nc, sem, lambda *a: sb(ctx, *a), lambda *a: ps(ctx, *a), io, dr, ident, gates, gates_in)
        early.close()
        projs, proj_loads = projection_weights(lambda *a: sb(top, *a), io)
        projs_in = sem("projection_weights_in")
        w1 = sb(top, "w1", [P, KC, E, HID])
        w2 = sb(top, "w2", [P, HID // P, E, C])
        w_in = sem("experts_in")
        with ExitStack() as ctx:
            attention(nc, sem, lambda *a: sb(ctx, *a), lambda *a: ps(ctx, *a), io, dr, ident, w1, w2, w_in, proj_loads, projs_in)
        expert, at = sb(top, "expert", [1, MT], I32), sb(top, "tile_row", [1, MT], I32)
        with ExitStack() as ctx:
            project_and_route(nc, sem, lambda *a: sb(ctx, *a), lambda *a: ps(ctx, *a), io, dr, ident, projs, projs_in, expert, at)
        with ExitStack() as ctx:
            experts(nc, sem, lambda *a: sb(ctx, *a), lambda *a: ps(ctx, *a), io, dr, ident, w1, w2, expert, at)


def constants(nc, sem, ident, identb):
    zeroed, made = sem("ident_zeroed"), sem("ident_made")
    with nc.Block() as block:
        @block.gpsimd
        def _(pool):
            nc.gpsimd.memset(ident[:], 0.0).then_inc(zeroed, 1)
            pool.wait_ge(zeroed, 1)
            nc.gpsimd.affine_select(out=ident[:], in_=ident[:], compare_op=ALU.not_equal, fill=1.0, base=0,
                                    pattern=[[-1, P]], channel_multiplier=1).then_inc(made, 1)

        @block.vector
        def _(dve):
            dve.wait_ge(made, 1)
            nc.vector.tensor_copy(identb[:], ident[:])


def wave_parameters(nc, sem, sb, ps, io, dr, ident, par):
    with ExitStack() as ctx:
        tanhs = sb(ctx, "wp_tanh", [P, TILES, 3, WH])
        qk = sb(ctx, "wp_qk", [P, TILES, WH])
        kw = sb(ctx, "wp_kw", [P, POS])
        with ExitStack() as inner:
            project_waves(nc, sem, lambda *a: sb(inner, *a), lambda *a: ps(inner, *a), io, ident, kw, tanhs, qk)
        with ExitStack() as inner:
            wave_normalisers(nc, sem, lambda *a: sb(inner, *a), par, tanhs, qk, dr)


def project_waves(nc, sem, sb, ps, io, ident, kw, tanhs, qk):
    xb = [sb(f"pw_x{i}", [P, BT, C]) for i in range(2)]
    xT = [sb(f"pw_xT{i}", [P, KC, L]) for i in range(2)]
    w = sb("pw_w", [P, KC, NW])
    bias = sb("pw_bias", [P, NW])
    pre = sb("pw_pre", [P, BT, NW])
    act = sb("pw_act", [P, BT, NW])
    prod = sb("pw_prod", [P, BT, WH * POS])
    pT = ps("pw_pT", [P, KC, L])
    pW = ps("pw_pW", [P, BT // 2, 2, C])
    w_in, x_in = sem("wave_w_in"), [sem(f"wave_x_in{i}") for i in range(2)]
    turned, evac, mm = sem("wave_x_turned"), sem("wave_xT_ready"), sem("wave_projected")
    biased, silued, tanhed, qprod, qkd = (sem("wave_" + n) for n in ("biased", "silued", "tanhed", "qk_products", "qk_summed"))
    pW3 = pW[:, :, :, 0:NW]
    act4 = act[:, :, 0:3 * WH].rearrange("p t (g h) -> p t g h", g=3)
    x = io["L0_attn_x"].rearrange("b (t p) c -> b p t c", p=P)

    def row(a, n):
        return a.rearrange("(o n) -> o n", o=1).to_broadcast([P, n])

    with nc.Block() as block:
        @block.sync
        def _(sp):
            for b in range(B):
                if b >= 2:
                    sp.wait_ge(turned, b - 1)
                sp.dma_start(xb[b % 2][:], x[b]).then_inc(x_in[b % 2], 16)

        @block.scalar
        def _(a):
            a.dma_start(w[:, :, 0:3 * WH], io["L0_attn_w_wave"].rearrange("(k p) n -> p k n", p=P)).then_inc(w_in, 16)
            a.dma_start(w[:, :, 3 * WH:NW], io["L0_attn_w_query"].rearrange("(k p) n -> p k n", p=P)).then_inc(w_in, 16)
            a.dma_start(bias[:, 0:3 * WH], row(io["L0_attn_b_wave"], 3 * WH)).then_inc(w_in, 16)
            a.dma_start(bias[:, 3 * WH:NW], row(io["L0_attn_b_query"], WH * POS)).then_inc(w_in, 16)
            a.dma_start(kw[:], row(io["L0_attn_key_weight"], POS)).then_inc(w_in, 16)

            def evacuate(b):
                a.wait_ge(turned, b + 1)
                if b >= 2:
                    a.wait_ge(mm, b - 1)
                nc.scalar.copy(xT[b % 2][:, 1, :], pT[:, 1, :]).then_inc(evac, 1)

            evacuate(0)
            for b in range(B):
                if b + 1 < B:
                    evacuate(b + 1)
                a.wait_ge(biased, b + 1)
                if b:
                    a.wait_ge(qkd, b)
                    a.wait_ge(tanhed, 2 * b)
                nc.scalar.activation(act[:], pre[:], ACT.Silu).then_inc(silued, 1)
                a.wait_ge(silued, b + 1)
                at = tanhs[:, b * BT:(b + 1) * BT, :, :]
                nc.scalar.activation(at[:, :, 0:3:2, :], act4[:, :, 0:3:2, :], ACT.Tanh, scale=0.5).then_inc(tanhed, 1)
                nc.scalar.activation(at[:, :, 1, :], act4[:, :, 1, :], ACT.Tanh).then_inc(tanhed, 1)
            a.wait_ge(tanhed, 2 * B)

        @block.tensor
        def _(pe):
            def turn(b):
                pe.wait_ge(x_in[b % 2], 16 * (b // 2 + 1))
                if b:
                    pe.wait_ge(evac, 2 * b)
                for k in range(KC):
                    for t in range(BT):
                        last = nc.tensor.transpose(pT[:, k, t * P:(t + 1) * P], xb[b % 2][:, t, k * P:(k + 1) * P], ident[:])
                last.then_inc(turned, 1)

            turn(0)
            pe.wait_ge(w_in, 5 * 16)
            for b in range(B):
                if b + 1 < B:
                    turn(b + 1)
                else:
                    pe.wait_ge(evac, 2 * B)
                if b:
                    pe.wait_ge(biased, b)
                for t in range(BT):
                    for k in range(KC):
                        last = nc.tensor.matmul(pW[:, t // 2, t % 2, 0:NW], xT[b % 2][:, k, t * P:(t + 1) * P], w[:, k, :],
                                                start=(k == 0), stop=(k == KC - 1))
                last.then_inc(mm, 1)

        @block.vector
        def _(dve):
            def evacuate(b):
                dve.wait_ge(turned, b + 1)
                if b >= 2:
                    dve.wait_ge(mm, b - 1)
                nc.vector.tensor_copy(xT[b % 2][:, 0, :], pT[:, 0, :]).then_inc(evac, 1)

            evacuate(0)
            dve.wait_ge(w_in, 5 * 16)
            for b in range(B):
                if b + 1 < B:
                    evacuate(b + 1)
                dve.wait_ge(mm, b + 1)
                if b:
                    dve.wait_ge(silued, b)
                nc.vector.tensor_tensor(pre[:].rearrange("p (s t) n -> p s t n", t=2), pW3,
                                        bias[:].unsqueeze(1).unsqueeze(1).to_broadcast([P, BT // 2, 2, NW]),
                                        ALU.add).then_inc(biased, 1)
                dve.wait_ge(silued, b + 1)
                nc.vector.tensor_tensor(prod[:].rearrange("p t (h d) -> p (t h) d", h=WH),
                                        act[:, :, 3 * WH:NW].rearrange("p t (h d) -> p t h d", h=WH),
                                        kw[:].unsqueeze(1).to_broadcast([P, BT * WH, POS]).rearrange("p (t h) d -> p t h d", h=WH),
                                        ALU.mult).then_inc(qprod, 1)
                dve.wait_ge(qprod, b + 1)
                nc.vector.reduce_sum(qk[:, b * BT:(b + 1) * BT, :], prod[:].rearrange("p t (h d) -> p t h d", h=WH),
                                     AX.X).then_inc(qkd, 1)
            dve.wait_ge(qkd, B)


def wave_normalisers(nc, sem, sb, par, tanhs, qk, dr):
    NK = REACH + 1
    mean = sb("wn_sum", [P, TILES, 3])
    steps = sb("wn_steps", [P, STEPS])
    ks = sb("wn_ks", [P, NK])
    far = sb("wn_far", [P, NK])
    pos = sb("wn_pos", [P, TILES, STEPS])
    pos2 = sb("wn_pos2", [P, TILES, STEPS])
    inside = sb("wn_inside", [P, TILES, STEPS])
    cnt = sb("wn_count", [P, TILES, NK])
    any_ = sb("wn_any", [P, TILES, NK])
    tk = sb("wn_tk", [P, TILES, NK])
    tk2 = sb("wn_tk2", [P, TILES, NK])
    env = sb("wn_env", [P, TILES, NK])
    dec, g, kmin = (sb("wn_" + n, [P, TILES]) for n in ("dec", "g", "kmin"))
    a_, m1, m2, Z, Es, lnD = (sb("wn_" + n, [P, TILES, WH]) for n in ("a", "m1", "m2", "Z", "E", "lnD"))
    big = sb("wn_big", [P, TILES, WH, NK])
    big2 = sb("wn_big2", [P, TILES, WH, NK])
    consts, d, acted, asked = sem("wn_consts"), sem("wn_dve"), sem("wn_acted"), sem("wn_asked")
    freq, phase, invf, mid, kmax, lpos = (par[n] for n in ("freq", "phase", "invf", "mid", "kmax", "lpos"))
    alpha, beta = par["alpha"], par["beta"]

    def over(a, n):
        return a[:].unsqueeze(2).to_broadcast([P, TILES, n])

    def heads(a):
        return a[:].unsqueeze(3).to_broadcast([P, TILES, WH, NK])

    def dist(a):
        return a[:].unsqueeze(2).to_broadcast([P, TILES, WH, NK])

    with nc.Block() as block:
        @block.gpsimd
        def _(pool):
            nc.gpsimd.iota(lpos[:], pattern=[[0, B], [P, BT]], base=0, channel_multiplier=1,
                           allow_small_or_imprecise_dtypes=True).then_inc(consts, 1)
            nc.gpsimd.iota(steps[:], pattern=[[1, STEPS]], base=-REACH, channel_multiplier=0,
                           allow_small_or_imprecise_dtypes=True).then_inc(consts, 1)
            nc.gpsimd.iota(ks[:], pattern=[[1, NK]], base=0, channel_multiplier=0,
                           allow_small_or_imprecise_dtypes=True).then_inc(consts, 1)
            nc.gpsimd.iota(far[:], pattern=[[-1, NK]], base=1000, channel_multiplier=0,
                           allow_small_or_imprecise_dtypes=True).then_inc(consts, 1)

        @block.vector
        def _(dve):
            v = nc.vector
            c = Chain(dve, d)
            c.link(v.reduce_sum(mean[:], tanhs[:], AX.X))
            c.did(v.tensor_scalar(freq[:], mean[:, :, 0], 7.5 / WH, 8.5, ALU.mult, ALU.add))
            c.did(v.tensor_scalar(phase[:], mean[:, :, 1], 16.0 / WH, None, ALU.mult))
            c.link(v.tensor_scalar(dec[:], mean[:, :, 2], 4.75 / WH, 5.25, ALU.mult, ALU.add))
            c.did(v.tensor_scalar(dec[:], dec[:], 0.1, None, ALU.max))
            c.link(v.reciprocal(invf[:], freq[:]))
            c.link(v.reciprocal(g[:], dec[:]))
            dve.wait_ge(consts, 4)
            c.link(v.tensor_tensor(g[:], g[:], freq[:], ALU.mult))
            c.did(v.tensor_tensor(pos[:], steps[:].unsqueeze(1).to_broadcast([P, TILES, STEPS]), over(freq, STEPS), ALU.mult))
            c.link(v.tensor_tensor(mid[:], lpos[:], phase[:], ALU.add))
            c.did(v.tensor_tensor(pos2[:], pos[:], over(lpos, STEPS), ALU.add))
            c.link(v.tensor_scalar(mid[:], mid[:], -1.0, 0.5, ALU.mult, ALU.add))
            c.did(v.tensor_tensor(pos[:], pos2[:], over(phase, STEPS), ALU.add))
            c.link(v.tensor_tensor(mid[:], mid[:], invf[:], ALU.mult))
            c.link(v.tensor_scalar(pos2[:], pos[:], float(L), None, ALU.is_lt))
            c.link(v.scalar_tensor_tensor(out=inside[:], in0=pos[:], scalar=0.0, in1=pos2[:], op0=ALU.is_ge, op1=ALU.mult))
            c.did(v.tensor_copy(cnt[:, :, 0], inside[:, :, REACH]))
            c.link(v.tensor_tensor(cnt[:, :, 1:NK], inside[:, :, REACH + 1:STEPS], inside[:, :, REACH - 1::-1], ALU.add))
            c.link(v.tensor_scalar(any_[:], cnt[:], 0.0, None, ALU.is_gt))
            c.did(v.tensor_tensor(tk[:], any_[:], ks[:].unsqueeze(1).to_broadcast([P, TILES, NK]), ALU.mult))
            c.link(v.tensor_tensor(tk2[:], any_[:], far[:].unsqueeze(1).to_broadcast([P, TILES, NK]), ALU.mult))
            c.did(v.tensor_reduce(kmax[:], tk[:], AX.X, ALU.max))
            c.link(v.tensor_reduce(kmin[:], tk2[:], AX.X, ALU.max))
            c.did(v.tensor_scalar(kmin[:], kmin[:], -1.0, 1000.0, ALU.mult, ALU.add))
            c.link(v.scalar_tensor_tensor(out=a_[:], in0=qk[:], scalar=float(POS) ** -0.5, in1=over(freq, WH),
                                          op0=ALU.mult, op1=ALU.mult))
            c.did(v.tensor_tensor(m1[:], a_[:], over(kmax, WH), ALU.mult))
            c.link(v.tensor_tensor(m2[:], a_[:], over(kmin, WH), ALU.mult))
            c.did(v.tensor_tensor(big[:], heads(a_), ks[:].unsqueeze(1).unsqueeze(1).to_broadcast([P, TILES, WH, NK]), ALU.mult))
            c.link(v.tensor_tensor(m1[:], m1[:], m2[:], ALU.max))
            c.did(v.tensor_tensor(tk[:], over(g, NK), ks[:].unsqueeze(1).to_broadcast([P, TILES, NK]), ALU.mult))
            c.link(v.tensor_tensor(big2[:], big[:], heads(m1), ALU.subtract))
            v.tensor_scalar(big2[:], big2[:], 0.0, None, ALU.min).then_inc(asked, 1)
            dve.wait_ge(acted, 2)
            c.did(v.tensor_tensor(big2[:], big[:], dist(cnt), ALU.mult))
            c.link(v.tensor_tensor(alpha[:], a_[:], over(g, WH), ALU.subtract))
            c.did(v.reduce_sum(Z[:], big2[:], AX.X))
            c.link(v.tensor_tensor(beta[:], alpha[:], over(kmax, WH), ALU.mult))
            c.did(v.tensor_tensor(big[:], big2[:], dist(env), ALU.mult))
            c.link(v.tensor_tensor(beta[:], beta[:], m1[:], ALU.subtract))
            c.link(v.reduce_sum(Es[:], big[:], AX.X))
            v.scalar_tensor_tensor(out=lnD[:], in0=Z[:], scalar=1e-8, in1=Es[:], op0=ALU.mult, op1=ALU.add).then_inc(asked, 1)
            dve.wait_ge(acted, 3)
            c.link(v.tensor_tensor(beta[:], beta[:], m2[:], ALU.subtract))

        @block.scalar
        def _(a):
            a.wait_ge(asked, 1)
            nc.scalar.activation(big[:], big2[:], ACT.Exp).then_inc(acted, 1)
            nc.scalar.activation(env[:], tk[:], ACT.Exp, scale=-1.0).then_inc(acted, 1)
            a.wait_ge(asked, 2)
            nc.scalar.activation(m2[:], lnD[:], ACT.Ln).then_inc(acted, 1)


def wave_sampling(nc, sem, sb, ps, io, dr, ident, identb, par, later, later_in):
    MAGIC = 1.5 * 2.0 ** 23
    NEAR = 3
    G = 4
    assert (REACH * 16.0 + 16.0) < NEAR * P

    def near(g, r):
        i = G * g + r
        return list(range(max(0, i - NEAR), min(BT - 1, i + NEAR) + 1))

    width = [[len(near(g, r)) * P for r in range(G)] for g in range(2)]
    off = [[sum(width[g][:r]) for r in range(G)] for g in range(2)]
    slots = [[(j, r) for j in range(BT) for r in range(G) if j in near(g, r)] for g in range(2)]
    NS = len(slots[0])
    assert NS == len(slots[1])
    CH = 8
    chunks = [range(s, min(s + CH, NS)) for s in range(0, NS, CH)]
    NCH = len(chunks)
    UCH = NCH * (1 + WH)
    WMAX = max(map(max, width))
    RING = 3
    FULL0, FREE0, READY0, MM0, OUT0, ROUNDED0 = 2 * UCH, RING, WH * G, 2, 2, 2
    assert UCH % RING == 0

    with ExitStack() as ctx:
        A = [sb(ctx, f"ws_A{i}", [P, NS * P]) for i in range(2)]
        AT = [sb(ctx, f"ws_AT{h}", [P, NS, P]) for h in range(WH)]
        KB, HB, HT = ([sb(ctx, f"ws_{n}{g}", [P, NS * P], BF16) for g in range(2)] for n in ("steps", "hit", "hitT"))
        step, pos = ([sb(ctx, f"ws_{n}{i}", [P, WMAX]) for i in range(2)] for n in ("step", "pos"))
        raw = [sb(ctx, f"ws_raw{i}", [P, WMAX]) for i in range(2)]
        below = [sb(ctx, f"ws_below{i}", [P, WMAX], BF16) for i in range(2)]
        xb = sb(ctx, "ws_x", [P, BT, C])
        rows = sb(ctx, "ws_rows", [P, L])
        ot = [sb(ctx, f"ws_ot{i}", [P, G * P]) for i in range(2)]
        pA = [ps(ctx, f"ws_pA{i}", [P, CH * P]) for i in range(RING)]
        acc = [ps(ctx, f"ws_acc{i}", [P, G * P]) for i in range(2)]
        rows_made, x_in = sem("ws_rows_made"), sem("ws_x_in")
        raw_ready, clamped, rounded, placed, offset, kstep = (sem("ws_" + n) for n in ("raw", "clamped", "rounded", "placed", "offset", "kgen"))
        ready, full, free, mm, acc_out = (sem("ws_" + n) for n in ("exp", "chunk_full", "chunk_free", "products", "acc_out"))
        ot_out = [sem(f"ws_ot_out{i}") for i in range(2)]
        KSTEPS, OFFSETS, KSTEP0 = 4, 2, 8
        x = io["L0_attn_x"].rearrange("b (t p) c -> b p t c", p=P)
        outT = dr["outT"].rearrange("(q p) n -> q p n", p=P)

        def cols(g, r):
            return slice(off[g][r], off[g][r] + width[g][r])

        def mrows(g, r):
            return rows[:, near(g, r)[0] * P:(near(g, r)[-1] + 1) * P]

        with nc.Block() as block, nc.allow_non_contiguous_dma(reason="per-channel vectors"):
            @block.sync
            def _(sp):
                def load_x(b):
                    sp.dma_start(xb[:], x[b]).then_inc(x_in, 16)

                def store(n, hq):
                    sp.wait_ge(acc_out, OUT0 + n * 2 + hq + 1)
                    sp.dma_start(outT[hq, :, bass.ds(n * (G * P), G * P)], ot[hq][:]).then_inc(ot_out[hq], 16)

                load_x(0)
                for dst, src in later:
                    sp.dma_start(dst, src).then_inc(later_in, 16)
                store(0, 0)
                with sp.Fori(0, B - 1) as i:
                    store(i * 2, 1)
                    store(i * 2 + 1, 0)
                    sp.wait_ge(mm, MM0 + i * 4 + 4)
                    load_x(i + 1)
                    store(i * 2 + 1, 1)
                    store(i * 2 + 2, 0)
                store(2 * B - 2, 1)
                store(2 * B - 1, 0)
                store(2 * B - 1, 1)
                for hq in range(2):
                    sp.wait_ge(ot_out[hq], 16 * 2 * B)
                sp.wait_ge(later_in, 16 * len(later))

            @block.gpsimd
            def _(pool):
                nc.gpsimd.iota(rows[:], pattern=[[1, L]], base=0, channel_multiplier=0,
                               allow_small_or_imprecise_dtypes=True).then_inc(rows_made, 1)
                pool.wait_ge(rows_made, 1)

                def distance(n, g, r):
                    w, k, u = width[g][r], n * G + r, r % 2
                    t = bass.ds(k, 1)
                    pool.wait_ge(placed, k + 1)
                    g_.tensor_tensor(pos[u][:, 0:w], pos[u][:, 0:w], par["phase"][:, t].to_broadcast([P, w]), ALU.add).then_inc(offset, 1)
                    pool.wait_ge(offset, k * OFFSETS + 1)
                    g_.tensor_tensor(pos[u][:, 0:w], pos[u][:, 0:w], mrows(g, r), ALU.subtract).then_inc(offset, 1)

                def unit(n, g):
                    for r in range(G):
                        distance(n, g, r)

                g_ = nc.gpsimd
                unit(0, 0)
                with pool.Fori(0, B - 1) as i:
                    unit(i * 2 + 1, 1)
                    unit(i * 2 + 2, 0)
                unit(2 * B - 1, 1)

            @block.scalar
            def _(a):
                a.sem_inc(ready, READY0)
                a.sem_inc(acc_out, OUT0)

                def locate(n, g, r):
                    t = bass.ds(n * G + r, 1)
                    a.wait_ge(rounded, n * G + r + 1)
                    nc.scalar.activation(raw[r % 2][:, 0:width[g][r]], mrows(g, r), ACT.Identity,
                                         bias=par["mid"][:, t], scale=par["invf"][:, t]).then_inc(raw_ready, 1)

                def place(n, g, r):
                    w, t = width[g][r], bass.ds(n * G + r, 1)
                    a.wait_ge(rounded, ROUNDED0 + n * G + r + 1)
                    nc.scalar.activation(pos[r % 2][:, 0:w], step[r % 2][:, 0:w], ACT.Identity,
                                         bias=par["lpos"][:, t], scale=par["freq"][:, t]).then_inc(placed, 1)

                def exps(n, g, h):
                    a.wait_ge(full, FULL0 + n * UCH + NCH * h if h >= 2 else FULL0 + (n - 1) * UCH + NCH * (WH + h))
                    for r in range(G):
                        t = bass.ds(n * G + r, 1)
                        if h == 0:
                            a.wait_ge(kstep, KSTEP0 + (n * G + r + 1) * KSTEPS)
                        nc.scalar.activation(A[h % 2][:, cols(g, r)], KB[g][:, cols(g, r)], ACT.Exp,
                                             bias=par["beta"][:, t, h], scale=par["alpha"][:, t, h]).then_inc(ready, 1)

                def drain(n, hq):
                    a.wait_ge(mm, MM0 + n * 2 + hq + 1)
                    a.wait_ge(ot_out[hq], n * 16)
                    nc.scalar.copy(ot[hq][:], acc[hq][:]).then_inc(acc_out, 1)

                def unit(n, g, first, last):
                    for h in range(WH):
                        exps(n, g, h)
                        if h == 1 and not first:
                            drain(n - 1, 0)
                        if h == 5 and not first:
                            drain(n - 1, 1)
                        if not last:
                            for r in range(G):
                                if PLACE[r] == h:
                                    place(n + 1, 1 - g, r)
                                if LOCATE[r] == h:
                                    locate(n + 1, 1 - g, r)

                PLACE, LOCATE = (1, 3, 4, 6), (0, 0, 2, 3)
                a.wait_ge(rows_made, 1)
                for r in range(G):
                    if r:
                        place(0, 0, r - 1)
                    locate(0, 0, r)
                place(0, 0, G - 1)
                unit(0, 0, True, False)
                with a.Fori(0, B - 1) as i:
                    unit(i * 2 + 1, 1, False, False)
                    unit(i * 2 + 2, 0, False, False)
                unit(2 * B - 1, 1, False, True)
                drain(2 * B - 1, 0)
                drain(2 * B - 1, 1)

            @block.vector
            def _(dve):
                v = nc.vector
                dve.sem_inc(free, FREE0)
                dve.sem_inc(kstep, KSTEP0)
                dve.sem_inc(rounded, ROUNDED0)
                dve.wait_ge(rows_made, 1)

                def steps(n, g, r, link):
                    w, k = width[g][r], n * G + r
                    t, u = bass.ds(n * G + r, 1), r % 2
                    bits = step[u][:, 0:w].bitcast(I32)
                    if link == 0:
                        dve.wait_ge(raw_ready, k + 1)
                        v.tensor_scalar(raw[u][:, 0:w], raw[u][:, 0:w], float(REACH), float(-REACH), ALU.min, ALU.max).then_inc(clamped, 1)
                    elif link == 1:
                        dve.wait_ge(clamped, k + 1)
                        v.tensor_scalar(step[u][:, 0:w], raw[u][:, 0:w], MAGIC, MAGIC, ALU.add, ALU.subtract).then_inc(rounded, 1)
                    elif link == LATER:
                        dve.wait_ge(offset, (k + 1) * OFFSETS)
                        v.tensor_scalar(below[u][:, 0:w], pos[u][:, 0:w], 1.0, None, ALU.is_lt).then_inc(kstep, 1)
                    elif link == LATER + 1:
                        v.tensor_scalar(bits, bits, 0x7FFFFFFF, None, ALU.bitwise_and).then_inc(kstep, 1)
                    elif link == LATER + 2:
                        dve.wait_ge(kstep, KSTEP0 + k * KSTEPS + 1)
                        dve.wait_ge(full, FULL0 + n * UCH - 2 * UCH + NCH)
                        v.scalar_tensor_tensor(out=HB[g][:, cols(g, r)], in0=pos[u][:, 0:w], scalar=0.0,
                                               in1=below[u][:, 0:w], op0=ALU.is_ge, op1=ALU.mult).then_inc(kstep, 1)
                    elif link == LATER + 3:
                        dve.wait_ge(kstep, KSTEP0 + k * KSTEPS + 3)
                        dve.wait_ge(ready, READY0 + (n - 1) * (WH * G))
                        v.scalar_tensor_tensor(out=KB[g][:, cols(g, r)], in0=step[u][:, 0:w],
                                               scalar=par["kmax"][:, t], in1=HB[g][:, cols(g, r)],
                                               op0=ALU.subtract, op1=ALU.mult).then_inc(kstep, 1)

                def drain(n, g, c, h):
                    q = (c if h is None else NCH * (1 + h) + c)
                    dve.wait_ge(full, FULL0 + n * UCH + q + 1)
                    m = chunks[c]
                    w = len(m) * P
                    cs = slice(m[0] * P, m[0] * P + w)
                    p = pA[q % RING]
                    if h is None:
                        v.tensor_copy(HT[g][:, cs], p[:].bitcast(BF16)[:, 0:w]).then_inc(free, 1)
                    else:
                        v.tensor_tensor(AT[h][:].rearrange("p s l -> p (s l)")[:, cs], p[:, 0:w], HT[g][:, cs],
                                        ALU.mult).then_inc(free, 1)

                def unit(n, g, first, last):
                    dve.wait_ge(kstep, KSTEP0 + (n + 1) * G * KSTEPS)
                    for c in range(NCH):
                        drain(n, g, c, None)
                    dve.wait_ge(free, FREE0 + n * UCH + NCH)
                    for h in range(WH):
                        if h % 4 == 0:
                            dve.wait_ge(mm, MM0 + (n - 1) * 2 + h // 4 + 1)
                        for c in range(NCH):
                            drain(n, g, c, h)
                            for r in range(G):
                                if not last:
                                    steps(n + 1, 1 - g, r, h * NCH + c - APART * r)

                APART, LATER = 4, 5
                for i in range(APART * G + LATER):
                    for r in range(G):
                        steps(0, 0, r, i - APART * r)
                unit(0, 0, True, False)
                with dve.Fori(0, B - 1) as i:
                    unit(i * 2 + 1, 1, False, False)
                    unit(i * 2 + 2, 0, False, False)
                unit(2 * B - 1, 1, False, True)

            @block.tensor
            def _(pe):
                pe.sem_inc(full, FULL0)
                pe.sem_inc(mm, MM0)

                def turn(n, g, h, c):
                    if c == 0 and h is None:
                        pe.wait_ge(kstep, KSTEP0 + (n + 1) * G * KSTEPS)
                    elif c == 0:
                        pe.wait_ge(ready, READY0 + (n * WH + h + 1) * G)
                    q = (c if h is None else NCH * (1 + h) + c)
                    pe.wait_ge(free, n * UCH + q + 1)
                    p, m = pA[q % RING], chunks[c]
                    for s in m:
                        j, r = slots[g][s]
                        at = off[g][r] + (j - near(g, r)[0]) * P
                        to = slice((s - m[0]) * P, (s - m[0] + 1) * P)
                        if h is None:
                            last = nc.tensor.transpose(p[:].bitcast(BF16)[:, to], HB[g][:, at:at + P], identb[:])
                        else:
                            last = nc.tensor.transpose(p[:, to], A[h % 2][:, at:at + P], ident[:])
                    last.then_inc(full, 1)

                def products(n, g, hq, i):
                    order = [j for j in range(BT) if any(jj == j for jj, _ in slots[g])]
                    if g:
                        order.reverse()
                    if i == 0:
                        pe.wait_ge(free, FREE0 + n * UCH + NCH * (1 + 4 * (hq + 1)))
                        pe.wait_ge(acc_out, OUT0 + (n - 1) * 2 + hq + 1)
                    j = order[i]
                    rs = [r for jj, r in slots[g] if jj == j]
                    s = slots[g].index((j, rs[0]))
                    for h4 in range(4):
                        h = 4 * hq + h4
                        last = nc.tensor.matmul(acc[hq][h4 * WD:(h4 + 1) * WD, rs[0] * P:(rs[-1] + 1) * P],
                                                xb[:, j, h * WD:(h + 1) * WD],
                                                AT[h][:, s:s + len(rs), :],
                                                start=(i == 0), stop=(i == len(order) - 1))
                    if i == len(order) - 1:
                        last.then_inc(mm, 1)

                NJ = G + NEAR
                AT0, AT1 = (18, 19, 21, 22, 24, 25, 26), (5, 7, 8, 10, 11, 13, 14)
                assert NCH * 5 + RING <= AT0[0] and RING <= AT1[0] and len(AT0) == len(AT1) == NJ

                def unit(n, g, first, last):
                    for q in range(UCH):
                        turn(n, g, q // NCH - 1 if q >= NCH else None, q % NCH)
                        if q in AT1 and not first:
                            products(n - 1, 1 - g, 1, AT1.index(q))
                        if q in AT0:
                            if q == AT0[0] and g == 0:
                                pe.wait_ge(x_in, n * 8 + 16)
                            products(n, g, 0, AT0.index(q))

                unit(0, 0, True, False)
                with pe.Fori(0, B - 1) as i:
                    unit(i * 2 + 1, 1, False, False)
                    unit(i * 2 + 2, 0, False, False)
                unit(2 * B - 1, 1, False, True)
                for i in range(NJ):
                    products(2 * B - 1, 1, 1, i)


def gate_weights(sb, io):
    wse1, wse2, wout = sb("gp_wse1", [P, KC, SE]), sb("gp_wse2", [SE, KC, P]), sb("gp_wout", [P, KC, C])
    wqkv, bse1, bse2 = sb("gp_wqkv", [P, KC, 3 * C]), sb("gp_bse1", [SE, 1]), sb("gp_bse2", [P, KC])
    ln_w, ln_b = sb("gp_lnw", [P, KC]), sb("gp_lnb", [P, KC])
    loads = [(wse1[:], io["L0_attn_w_se1"].rearrange("(k p) n -> p k n", p=P)),
             (wse2[:], io["L0_attn_w_se2"].rearrange("s (k p) -> s k p", p=P)),
             (wout[:], io["L0_attn_w_out"].rearrange("(k p) n -> p k n", p=P)),
             (wqkv[:], io["L0_ffn_w_qkv"].rearrange("(k p) n -> p k n", p=P)),
             (bse1[:], io["L0_attn_b_se1"].rearrange("(s o) -> s o", o=1)),
             (bse2[:], io["L0_attn_b_se2"].rearrange("(k p) -> p k", p=P)),
             (ln_w[:], io["L0_ffn_ln1_w"].rearrange("(k p) -> p k", p=P)),
             (ln_b[:], io["L0_ffn_ln1_b"].rearrange("(k p) -> p k", p=P))]
    return (wse1, wse2, wout, wqkv, bse1, bse2, ln_w, ln_b), loads


def gate_and_project(nc, sem, sb, ps, io, dr, ident, weights, w_in):
    T = 4
    N = T * P
    CHUNKS = TOKENS // N
    PARTS = 6
    wse1, wse2, wout, wqkv, bse1, bse2, ln_w, ln_b = weights
    hb2 = sb("gp_hb2", [P, KC])
    oT, xc = sb("gp_oT", [P, 2, KC, N]), sb("gp_x", [P, T, C])
    s1, th, gated = sb("gp_s1", [SE, N]), sb("gp_th", [P, KC, N]), sb("gp_gated", [P, KC, N])
    so, res, y0, n1 = sb("gp_so", [P, T, C]), sb("gp_res", [P, T, C]), sb("gp_y0", [P, T, C]), sb("gp_n1", [P, T, C])
    st, mv = sb("gp_st", [P, T, 6]), sb("gp_mv", [P, T, 2])
    eps, power = sb("gp_eps", [P, T]), sb("gp_power", [P, T])
    seen = sb("gp_seen", [P, 1])
    ve, rs, vn, rs2 = (sb("gp_" + n, [P, T]) for n in ("ve", "rs", "vn", "rs2"))
    zT = sb("gp_zT", [P, KC, N])
    rest = [sb(f"gp_rest{i}", [P, N]) for i in range(2)]
    split = [sb(f"gp_split{i}", [P, 3, N], BF16) for i in range(2)]
    vb = sb("gp_v", [P, T, H, 2 * DK])
    p1, pA, pO = ps("gp_p1", [SE, N]), ps("gp_pA", [P, KC, N]), ps("gp_pO", [P, T, C])
    pQ = [ps(f"gp_pQ{i}", [P, N]) for i in range(3)]
    o_in, x_in, ones, half = (sem("gp_" + n) for n in ("o_in", "x_in", "consts", "half_bias"))
    se1, silu1, se2, tanhed, gate, outed, silu3 = (sem("gp_" + n) for n in ("se1", "silu1", "se2", "tanh", "gated", "wout", "silu3"))
    added, stats, aggred, inv, y0d, n1d, turned, zd = (sem("gp_" + n) for n in ("added", "stats", "aggr", "rstd", "y0", "n1", "turned", "z"))
    part, hi, left, midd, lo, vd = (sem("gp_" + n) for n in ("part", "hi", "rest", "mid", "lo", "v"))
    y_out, v_out, waited = sem("gp_y_out"), sem("gp_v_out"), sem("gp_waited")
    s_out = [sem(f"gp_split_out{i}") for i in range(2)]
    INV = 6
    oT_d = dr["outT"].rearrange("(k p) n -> p k n", p=P)
    x_d = io["L0_attn_x"].rearrange("b l c -> (b l) c")
    WAITS = 16 * len(weights)

    def tokens(d, i):
        return d[bass.ds(i * N, N), :].rearrange("(t p) c -> p t c", p=P)

    def ahead(eng, chunk):
        chunk(0, None, True)
        chunk(1, 0, True)
        with eng.Fori(2, CHUNKS - 1) as i:
            chunk(i, i - 1, True)
        chunk(CHUNKS - 1, CHUNKS - 2, False)

    with nc.Block() as block, nc.allow_non_contiguous_dma(reason="per-channel vectors"):
        @block.sync
        def _(sp):
            def load_sums(i):
                if not isinstance(i, int) or i >= 2:
                    sp.wait_ge(se1, i)
                sp.dma_start(oT[:, bass.ds(i % 2, 1), :, :].rearrange("p o k n -> p (o k) n"), oT_d[:, :, bass.ds(i * N, N)]).then_inc(o_in, 16)

            def load_x(i):
                sp.wait_ge(added, i)
                sp.dma_start(xc[:], tokens(x_d, i)).then_inc(x_in, 16)

            def store_split(c, q):
                sp.wait_ge(lo, c * 4 + q + 1)
                dst = dr["qs"] if q < 2 else dr["ks"]
                sp.dma_start(dst.rearrange("s (k p) n -> k p s n", p=P)[q % 2, :, :, bass.ds(c * N, N)],
                             split[q % 2][:]).then_inc(s_out[q % 2], 16)

            def store_v(c):
                sp.wait_ge(vd, c * 2 + 2)
                sp.dma_start(tokens(dr["v"], c), vb[:].rearrange("p t h d -> p t (h d)")).then_inc(v_out, 16)

            def chunk(i, prev):
                if not isinstance(i, int) or i + 1 < CHUNKS:
                    load_x(i + 1)
                if prev is not None:
                    for q in range(3):
                        store_split(prev, q)
                if not isinstance(i, int) or i + 2 < CHUNKS:
                    load_sums(i + 2)
                sp.wait_ge(y0d, i * T + T)
                sp.dma_start(tokens(dr["y0"], i), y0[:]).then_inc(y_out, 16)
                if prev is not None:
                    store_split(prev, 3)
                    store_v(prev)

            load_sums(0)
            load_x(0)
            sp.wait_ge(se1, 1)
            load_sums(1)
            chunk(0, None)
            chunk(1, 0)
            with sp.Fori(2, CHUNKS - 2) as i:
                chunk(i, i - 1)
            for i in range(CHUNKS - 2, CHUNKS):
                chunk(i, i - 1)
            for q in range(4):
                store_split(CHUNKS - 1, q)
            store_v(CHUNKS - 1)
            sp.wait_ge(y_out, 16 * CHUNKS)
            sp.wait_ge(v_out, 16 * CHUNKS)
            for u in range(2):
                sp.wait_ge(s_out[u], 16 * CHUNKS * 2)

        @block.scalar
        def _(a):
            a.wait_ge(half, 1)

            def gate_in(i):
                a.wait_ge(se1, i + 1)
                if not isinstance(i, int) or i:
                    a.wait_ge(se2, i * KC)
                nc.scalar.activation(s1[:], p1[:], ACT.Silu, bias=bse1[:, 0:1]).then_inc(silu1, 1)

            def gate_out(i):
                if not isinstance(i, int) or i:
                    a.wait_ge(gate, i)
                for k in range(KC):
                    a.wait_ge(se2, i * KC + k + 1)
                    nc.scalar.activation(th[:, k, :], pA[:, k, :], ACT.Tanh, bias=hb2[:, k:k + 1], scale=0.5).then_inc(tanhed, 1)

            def output(i):
                a.wait_ge(outed, i + 1)
                a.wait_ge(added, i)
                nc.scalar.activation(so[:], pO[:], ACT.Silu, scale=0.5).then_inc(silu3, 1)

            def z(i):
                a.wait_ge(turned, i + 1)
                for k in range(KC):
                    nc.scalar.activation(zT[:, k, :], pA[:, k, :], ACT.Identity, bias=ln_b[:, k:k + 1],
                                         scale=ln_w[:, k:k + 1]).then_inc(zd, 1)

            def top(c, q):
                u = q % 2
                a.wait_ge(part, c * PARTS + q + 1)
                a.wait_ge(s_out[u], (c * 2 + q // 2) * 16)
                a.activation(split[u][:, 0, :], pQ[q % 3][:], ACT.Copy, scale=DK ** -0.5 if q < 2 else 1.0).then_inc(hi, 1)
                a.wait_ge(left, c * 4 + q + 1)
                a.activation(split[u][:, 1, :], rest[u][:], ACT.Copy).then_inc(midd, 1)

            def values(c, q):
                a.wait_ge(part, c * PARTS + q + 1)
                a.wait_ge(v_out, c * 16)
                a.copy(vb[:, 2 * (q - 4):2 * (q - 4) + 2, :, 0:DK],
                       pQ[q % 3][:].rearrange("p (t h d) -> p t h d", t=2, h=H)).then_inc(vd, 1)

            def chunk(i, prev, more):
                output(i)
                if prev is not None:
                    top(prev, 0)
                if more:
                    gate_in(i + 1)
                if prev is not None:
                    top(prev, 1)
                    top(prev, 2)
                if more:
                    gate_out(i + 1)
                if prev is not None:
                    top(prev, 3)
                    values(prev, 4)
                    values(prev, 5)
                z(i)

            gate_in(0)
            gate_out(0)
            ahead(a, chunk)
            for q in range(4):
                top(CHUNKS - 1, q)
            for q in range(4, 6):
                values(CHUNKS - 1, q)

        @block.vector
        def _(dve):
            v = nc.vector
            dve.wait_ge(w_in, WAITS)
            v.tensor_scalar(hb2[:], bse2[:], 0.5, None, ALU.mult).then_inc(half, 1)

            def remain(c, q):
                u = q % 2
                dve.wait_ge(hi, c * 4 + q + 1)
                dve.wait_ge(lo, c * 4 + max(0, q - 1))
                v.scalar_tensor_tensor(out=rest[u][:], in0=pQ[q % 3][:], scalar=DK ** -0.5 if q < 2 else 1.0,
                                       in1=split[u][:, 0, :], op0=ALU.mult, op1=ALU.subtract).then_inc(left, 1)

            def gate_sums(i):
                dve.wait_ge(tanhed, i * KC + KC)
                if not isinstance(i, int) or i:
                    dve.wait_ge(outed, i)
                v.scalar_tensor_tensor(out=gated[:], in0=th[:], scalar=1.0,
                                       in1=oT[:, bass.ds(i % 2, 1), :, :].rearrange("p o k n -> p (o k) n"), op0=ALU.add,
                                       op1=ALU.mult).then_inc(gate, 1)

            def chunk(i, prev, more):
                dve.wait_ge(silu3, i + 1)
                dve.wait_ge(x_in, i * 16 + 16)
                v.tensor_tensor(res[:], so[:], xc[:], ALU.add).then_inc(added, 1)
                dve.wait_ge(added, i + 1)
                for t in range(T):
                    v.bn_stats(st[:, t, :], res[:, t, :]).then_inc(stats, 1)
                dve.wait_ge(stats, i * T + T)
                v.tensor_copy(seen[:], st[:, T - 1, 0:1]).then_inc(waited, 1)
                for t in range(T):
                    v.bn_aggr(mv[:, t, :], st[:, t, :]).then_inc(aggred, 1)
                if prev is not None:
                    remain(prev, 0)
                    remain(prev, 1)
                dve.wait_ge(inv, i * INV + 2)
                if not isinstance(i, int) or i:
                    dve.wait_ge(y_out, i * 16)
                for t in range(T):
                    v.tensor_scalar(y0[:, t, :], res[:, t, :], mv[:, t, 0:1], rs[:, t:t + 1],
                                    ALU.subtract, ALU.mult).then_inc(y0d, 1)
                dve.wait_ge(inv, i * INV + INV)
                for t in range(T):
                    dve.wait_ge(y0d, i * T + t + 1)
                    v.tensor_scalar(n1[:, t, :], y0[:, t, :], rs2[:, t:t + 1], None, ALU.mult).then_inc(n1d, 1)
                if prev is not None:
                    remain(prev, 2)
                if more:
                    gate_sums(i + 1)
                if prev is not None:
                    remain(prev, 3)

            gate_sums(0)
            ahead(dve, chunk)
            for q in range(4):
                remain(CHUNKS - 1, q)

        @block.gpsimd
        def _(pool):
            g = nc.gpsimd
            g.memset(eps[:], EPS).then_inc(ones, 1)
            g.memset(power[:], -0.5).then_inc(ones, 1)
            g.memset(vb[:, :, :, DK:2 * DK], 1.0).then_inc(ones, 1)
            pool.wait_ge(ones, 3)

            def low(c, q):
                u = q % 2
                pool.wait_ge(midd, c * 4 + q + 1)
                g.tensor_tensor(split[u][:, 2, :], rest[u][:], split[u][:, 1, :], ALU.subtract).then_inc(lo, 1)

            def chunk(i, prev):
                c = Chain(pool, inv, i * INV)
                pool.wait_ge(aggred, i * T + T)
                pool.wait_ge(n1d, i * T)
                c.link(g.tensor_tensor(ve[:], mv[:, :, 1], eps[:], ALU.add))
                c.link(g.tensor_tensor(rs[:], ve[:], power[:], ALU.pow))
                c.link(g.tensor_tensor(vn[:], mv[:, :, 1], rs[:], ALU.mult))
                c.link(g.tensor_tensor(ve[:], vn[:], rs[:], ALU.mult))
                c.link(g.tensor_tensor(vn[:], ve[:], eps[:], ALU.add))
                c.link(g.tensor_tensor(rs2[:], vn[:], power[:], ALU.pow))
                if prev is not None:
                    for q in range(4):
                        low(prev, q)

            chunk(0, None)
            chunk(1, 0)
            with pool.Fori(2, CHUNKS) as i:
                chunk(i, i - 1)
            for q in range(4):
                low(CHUNKS - 1, q)

        @block.tensor
        def _(pe):
            pe.wait_ge(w_in, WAITS)

            def parts(c, q):
                pe.wait_ge(zd, c * KC + KC)
                if q < 3:
                    pe.wait_ge(vd, c * 2)
                    pe.wait_ge(left, c * 4)
                else:
                    pe.wait_ge(left, c * 4 + q - 2)
                if q < 4:
                    for k in range(KC):
                        last = nc.tensor.matmul(pQ[q % 3][:], wqkv[:, k, q * P:(q + 1) * P], zT[:, k, :],
                                                start=(k == 0), stop=(k == KC - 1))
                else:
                    for t in range(2):
                        for k in range(KC):
                            tile = 2 * (q - 4) + t
                            last = nc.tensor.matmul(pQ[q % 3][:, t * C:(t + 1) * C], zT[:, k, tile * P:(tile + 1) * P],
                                                    wqkv[:, k, 2 * C:3 * C], start=(k == 0), stop=(k == KC - 1))
                last.then_inc(part, 1)

            def squeeze(i):
                pe.wait_ge(o_in, i * 16 + 16)
                if not isinstance(i, int) or i:
                    pe.wait_ge(silu1, i)
                for k in range(KC):
                    last = nc.tensor.matmul(p1[:], wse1[:, k, :], oT[:, bass.ds(i % 2, 1), k, :], start=(k == 0), stop=(k == KC - 1))
                last.then_inc(se1, 1)

            def excite(i):
                pe.wait_ge(silu1, i + 1)
                if not isinstance(i, int) or i >= 2:
                    pe.wait_ge(zd, (i - 1) * KC)
                for k in range(KC):
                    nc.tensor.matmul(pA[:, k, :], wse2[:, k, :], s1[:], start=True, stop=True).then_inc(se2, 1)

            def chunk(i, prev, more):
                pe.wait_ge(gate, i + 1)
                if prev is not None:
                    pe.wait_ge(silu3, i)
                for t in range(T):
                    for k in range(KC):
                        last = nc.tensor.matmul(pO[:, t, :], gated[:, k, t * P:(t + 1) * P], wout[:, k, :],
                                                start=(k == 0), stop=(k == KC - 1))
                last.then_inc(outed, 1)
                if prev is not None:
                    parts(prev, 0)
                if more:
                    squeeze(i + 1)
                if prev is not None:
                    parts(prev, 1)
                    parts(prev, 2)
                if more:
                    excite(i + 1)
                if prev is not None:
                    for q in range(3, PARTS):
                        parts(prev, q)
                pe.wait_ge(tanhed, (i + 2) * KC if more else (i + 1) * KC)
                for t in range(T):
                    pe.wait_ge(n1d, i * T + t + 1)
                    for k in range(KC):
                        last = nc.tensor.transpose(pA[:, k, t * P:(t + 1) * P], n1[:, t, k * P:(k + 1) * P], ident[:])
                last.then_inc(turned, 1)

            squeeze(0)
            excite(0)
            ahead(pe, chunk)
            for q in range(PARTS):
                parts(CHUNKS - 1, q)


def attention(nc, sem, sb, ps, io, dr, ident, w1, w2, w_in, later, later_in):
    UNITS = B * H // 2
    STACK = [(0, 0), (0, 1), (1, 0), (1, 1), (0, 2), (2, 0)]
    ROWS = DK * len(STACK)
    FULL = ROWS + 3
    HALF = L // 2
    PIECES = 2 * BT
    MAXIMA = 2 * PIECES
    RING = 4
    PV0 = 2
    BANKS = 3
    LOADS = 2 * len(STACK) * 16
    TOPS = 4
    PER = MAXIMA // BT
    ORDER = "SSMSMVMSM"
    TURN = 5

    qst = [sb(f"at_q{i}", [FULL, 2, L], BF16) for i in range(RING)]
    kst = [sb(f"at_k{i}", [FULL, 2, L], BF16) for i in range(RING)]
    vst = [sb(f"at_v{i}", [P, BT, 2, 2 * DK]) for i in range(RING)]
    pt = [sb(f"at_p{i}", [P, 2, HALF]) for i in range(4)]
    mx, top_ = [sb(f"at_mx{i}", [P, PIECES, 2]) for i in range(2)], sb("at_top", [P, PIECES])
    tail = sb("at_tail", [PIECES, P])
    top3 = [sb(f"at_top3{i}", [PIECES, 3, P], BF16) for i in range(2)]
    oe = sb("at_oe", [P, HALF])
    rden, yn = sb("at_rden", [P, 8, 2]), [sb(f"at_yn{i}", [P, 8, 2, 2 * DK]) for i in range(2)]
    pst = [ps(f"at_pst{i}", [P, HALF]) for i in range(BANKS)]
    pmx = [ps(f"at_pmx{i}", [P, HALF]) for i in range(BANKS)]
    pacc, pm = ps("at_pacc", [P, HALF]), ps("at_pm", [P, 8, 2, 2 * DK])
    one_rows = sem("at_ones")
    ld = [sem(f"at_load{i}") for i in range(RING)]
    v_in = [sem(f"at_v_in{i}") for i in range(RING)]
    scored, exped, pv, red, mxmm = (sem("at_" + n) for n in ("scored", "exp", "pv", "reduced", "maxima"))
    topped, topT, split, rows_in, oed, oT, yd, rd = (sem("at_" + n) for n in ("top", "topT", "top_split", "top_rows", "acc_out", "outT", "y", "rden"))
    y_out = [sem(f"at_y_out{i}") for i in range(2)]
    negT = pm[0:PIECES, 0:2, :, :].rearrange("p t h d -> p (t h d)")

    with nc.Block() as block, nc.allow_non_contiguous_dma(reason="per-channel vectors"):
        def bank(k):
            return k % BANKS if k < 4 * BT // BANKS * BANKS else k - 4 * BT // BANKS * BANKS

        def since(w, k):
            for back in range(1, 2 * BANKS):
                if bank((k - back) % (4 * BT)) == bank(k):
                    return None if isinstance(w, int) and w * 4 * BT + k < back else w * (4 * BT) + k - back + 1

        def beside(w, u, s):
            ahead, m = (1, (BT - TURN + s) * PER) if s < TURN else (2, (s - TURN) * PER)
            if isinstance(w, int) and w + ahead >= UNITS:
                return []
            return [(w + ahead, (u + ahead) % RING, m + n) for n in range(PER)]

        def early():
            return [(0, 0, m) for m in range(MAXIMA)] + [(1, 1, m) for m in range((BT - TURN) * PER)]

        def turns(w):
            return not isinstance(w, int) or w + 1 < UNITS

        def units(eng, unit):
            for u in range(RING):
                unit(u, 0, u)
            with eng.Fori(1, UNITS // RING - 1) as i:
                for u in range(RING):
                    unit(i * RING + u, i, u)
            for u in range(RING):
                unit(UNITS - RING + u, UNITS // RING - 1, u)

        @block.sync
        def _(sp):
            def place(i, u):
                per = H // 2 // RING
                return i // per, (i % per) * RING + u

            def load(i, u):
                b, pair = place(i, u)
                def part(d, n):
                    return d[n, bass.ds(pair * (2 * DK), 2 * DK), bass.ds(b * L, L)].rearrange("(h d) n -> d h n", d=DK)
                for n, (pq, pk) in enumerate(STACK):
                    rows = slice(n * DK, (n + 1) * DK)
                    sp.dma_start(qst[u][rows, :, :], part(dr["qs"], pq)).then_inc(ld[u], 16)
                    sp.dma_start(kst[u][rows, :, :], part(dr["ks"], pk)).then_inc(ld[u], 16)
                sp.dma_start(vst[u][:].rearrange("p t h d -> p t (h d)"),
                             dr["v"][bass.ds(b * L, L), bass.ds(pair * (4 * DK), 4 * DK)].rearrange("(t p) n -> p t n", p=P)).then_inc(v_in[u], 16)

            def store_top(w, u):
                sp.wait_ge(split, w * TOPS + TOPS)
                for n in range(3):
                    sp.dma_start(qst[u][ROWS + n:ROWS + n + 1, :, :].rearrange("o h (t n) -> o (h t) n", t=BT),
                                 top3[u % 2][:, n, :]).then_inc(rows_in, 16)

            def store_y(w, i, u):
                b, pair = place(i, u - 1)
                sp.wait_ge(yd, w + 1)
                y = dr["Y"][bass.ds(b * L, L), bass.ds(pair * (2 * DK), 4 * DK)].rearrange("(x t p) c -> x p t c", x=2, p=P)
                src = yn[u // 2][:].rearrange("p (t x) q c -> p t x (q c)", x=2)
                for x in range(2):
                    sp.dma_start(y[x], src[:, :, x, :]).then_inc(y_out[u // 2], 16)

            def unit(w, i, u):
                first, left = isinstance(w, int) and w == 0, not isinstance(w, int) or w + 3 < UNITS
                if left and not first:
                    sp.wait_ge(pv, PV0 + w * BT)
                    load(i if u == 0 else i + 1, (u + 3) % RING)
                if u % 2:
                    q, hc = u // 2, HID // P // 2
                    sp.dma_start(w1[:, q, bass.ds(i, 1), :], io["L0_ffn_w1"][bass.ds(i, 1), q * P:(q + 1) * P, :].rearrange("e p n -> p e n")).then_inc(w_in, 16)
                    sp.dma_start(w2[:, q * hc:(q + 1) * hc, bass.ds(i, 1), :],
                                 io["L0_ffn_w2"][bass.ds(i, 1), q * hc * P:(q + 1) * hc * P, :].rearrange("e (t p) n -> p t e n", p=P)).then_inc(w_in, 16)
                elif not first:
                    store_y(w - 1, i if u else i - 1, (u - 1) % RING)
                if turns(w):
                    store_top(w + 1, (u + 1) % RING)

            for u in range(3):
                load(0, u)
            store_top(0, 0)
            sp.wait_ge(mxmm, 1)
            load(0, 3)
            for dst, src in later:
                sp.dma_start(dst, src).then_inc(later_in, 16)
            units(sp, unit)
            store_y(UNITS - 1, UNITS // RING - 1, RING - 1)
            for n in range(2):
                sp.wait_ge(y_out[n], 32 * (UNITS // RING))
            sp.wait_ge(w_in, 16 * 2 * 2 * E)
            sp.wait_ge(later_in, 16 * len(later))

        @block.gpsimd
        def _(pool):
            for k in kst:
                nc.gpsimd.memset(k[ROWS:FULL, :, :], 1.0).then_inc(one_rows, 1)

        @block.scalar
        def _(a):
            def out(w):
                a.wait_ge(pv, PV0 + (w + 1) * BT)
                a.wait_ge(oT, w)
                a.copy(oe[:], pacc[:]).then_inc(oed, 1)

            def unit(w, i, u):
                for s in range(BT):
                    for k in range(4 * s, 4 * s + 4):
                        a.wait_ge(scored, w * (4 * BT) + k + 1)
                        a.wait_ge(pv, w * BT + s + 1)
                        a.activation(pt[k // 2 % 4][:, k % 2, :], pst[bank(k)][:], ACT.Exp).then_inc(exped, 1)
                    if s == 0 and not (isinstance(w, int) and w == 0):
                        out(w - 1)

            units(a, unit)
            out(UNITS - 1)

        @block.vector
        def _(dve):
            v = nc.vector

            def maximum(w, u, m):
                dve.wait_ge(mxmm, w * MAXIMA + m + 1)
                v.reduce_max(mx[u % 2][:, m // 2, m % 2:m % 2 + 1], pmx[bank(m)][:], AX.X).then_inc(red, 1)

            def tops(w, u):
                dve.wait_ge(red, (w + 1) * MAXIMA)
                v.tensor_tensor(top_[:], mx[u % 2][:, :, 0], mx[u % 2][:, :, 1], ALU.max).then_inc(topped, 1)

            def split_tops(w, u, link):
                t = top3[u % 2]
                if link == 0:
                    dve.wait_ge(topT, w + 1)
                    ins = (v.tensor_scalar(t[:, 0, :], negT, -1.0, None, ALU.mult))
                elif link == 1:
                    dve.wait_ge(split, w * TOPS + link)
                    ins = (v.scalar_tensor_tensor(out=tail[:], in0=negT, scalar=-1.0, in1=t[:, 0, :], op0=ALU.mult, op1=ALU.subtract))
                elif link == 2:
                    dve.wait_ge(split, w * TOPS + link)
                    ins = (v.tensor_copy(t[:, 1, :], tail[:]))
                else:
                    dve.wait_ge(split, w * TOPS + link)
                    ins = (v.tensor_tensor(t[:, 2, :], tail[:], t[:, 1, :], ALU.subtract))
                ins.then_inc(split, 1)

            def invert(w):
                dve.wait_ge(oT, w + 1)
                v.reciprocal(rden[:], pm[:, :, :, DK]).then_inc(rd, 1)

            def normalise(w, i, u):
                dve.wait_ge(rd, w + 1)
                if u % 2 == 0:
                    dve.wait_ge(y_out[u // 2], i * 32)
                v.tensor_tensor(yn[u // 2][:, :, u % 2, :].rearrange("p t (h d) -> p t h d", h=2), pm[:, :, :, 0:DK],
                                rden[:].unsqueeze(3).to_broadcast([P, 8, 2, DK]), ALU.mult).then_inc(yd, 1)

            def unit(w, i, u):
                first = isinstance(w, int) and w == 0
                for s in range(BT):
                    ms = beside(w, u, s)
                    for n in range(PER):
                        if ms:
                            maximum(*ms[n])
                        if s == 2 and not first:
                            if n == 1:
                                invert(w - 1)
                            if n == 2:
                                normalise(w - 1, i if u else i - 1, (u - 1) % RING)
                        if turns(w):
                            if s == TURN - 1 and n == PER - 1:
                                tops(w + 1, u + 1)
                            link = (s - TURN) * PER + n - 1
                            if 0 <= link < TOPS:
                                split_tops(w + 1, u + 1, link)

            for e in early():
                maximum(*e)
                if e[0] == 0 and e[2] == MAXIMA - 1:
                    tops(0, 0)
                if e[0] == 1 and e[2] < TOPS:
                    split_tops(0, 0, e[2])
            units(dve, unit)
            invert(UNITS - 1)
            normalise(UNITS - 1, UNITS // RING - 1, RING - 1)

        @block.tensor
        def _(pe):
            def maximum(w, u, m):
                h, nt, kh = m // (2 * BT), m // 2 % BT, m % 2
                if m == 0:
                    pe.wait_ge(ld[u], (w // RING + 1) * LOADS)
                if since(w, m) is not None:
                    pe.wait_ge(red, since(w, m))
                nc.tensor.matmul(pmx[bank(m)][:], qst[u][0:ROWS, h, nt * P:(nt + 1) * P],
                                 kst[u][0:ROWS, h, kh * HALF:(kh + 1) * HALF], start=True, stop=True).then_inc(mxmm, 1)

            def turn_tops(w):
                pe.wait_ge(topped, w + 1)
                nc.tensor.transpose(negT, top_[:], ident[:]).then_inc(topT, 1)

            def turn_out(w):
                pe.wait_ge(oed, w + 1)
                pmf = pm[:].rearrange("p (t x) h d -> p t (x h d)", x=2)
                for t in range(4):
                    last = nc.tensor.transpose(pmf[:, t, :], oe[:, t * P:(t + 1) * P], ident[:])
                last.then_inc(oT, 1)

            def scores(w, u, k):
                t, p, h = k // 4, k // 2 % 2, k % 2
                if since(w, k) is not None:
                    pe.wait_ge(exped, since(w, k))
                nc.tensor.matmul(pst[bank(k)][:], kst[u][:, h, t * P:(t + 1) * P],
                                 qst[u][:, h, p * HALF:(p + 1) * HALF], start=True, stop=True).then_inc(scored, 1)

            def values(w, u, s):
                pe.wait_ge(exped, w * (4 * BT) + 4 * s + 4)
                if s == 0:
                    pe.wait_ge(oed, w)
                for p in range(2):
                    for h in range(2):
                        at = (2 * p + h) * 2 * DK
                        last = nc.tensor.matmul(pacc[at:at + 2 * DK, :], vst[u][:, s, h, :],
                                                pt[(2 * s + p) % 4][:, h, :], start=(s == 0), stop=(s == BT - 1))
                last.then_inc(pv, 1)

            def unit(w, i, u):
                first = isinstance(w, int) and w == 0
                pe.wait_ge(rows_in, (w + 1) * 48)
                pe.wait_ge(v_in[u], (i + 1) * 16)
                for s in range(BT):
                    ms = beside(w, u, s)
                    k, n = 4 * s, 0
                    for what in ORDER:
                        if what == "S":
                            scores(w, u, k)
                            k += 1
                        elif what == "M":
                            if ms:
                                maximum(*ms[n])
                            n += 1
                        elif what == "V":
                            if s:
                                values(w, u, s - 1)
                            elif not first:
                                values(w - 1, (u - 1) % RING, BT - 1)
                            if s == 2 and not first:
                                if turns(w - 1):
                                    pe.wait_ge(split, (w + 1) * TOPS)
                                turn_out(w - 1)
                            if s == TURN and turns(w):
                                if not first:
                                    pe.wait_ge(yd, w)
                                turn_tops(w + 1)

            pe.sem_inc(pv, PV0)
            for e in early():
                maximum(*e)
                if e[0] == 0 and e[2] == MAXIMA - 1:
                    turn_tops(0)
            pe.wait_ge(one_rows, RING)
            units(pe, unit)
            values(UNITS - 1, RING - 1, BT - 1)
            pe.wait_ge(yd, UNITS - 1)
            turn_out(UNITS - 1)


def projection_weights(sb, io):
    wp, gw, gb = sb("pg_wproj", [P, KC, C]), sb("pg_gw", [P, KC, E]), sb("pg_gb", [P, E])
    ln_w, ln_b = sb("pg_lnw", [P, KC]), sb("pg_lnb", [P, KC])
    loads = [(wp[:], io["L0_ffn_w_proj"].rearrange("(k p) n -> p k n", p=P)),
             (gw[:], io["L0_ffn_gate_w"].rearrange("(k p) n -> p k n", p=P)),
             (gb[:], io["L0_ffn_gate_b"].rearrange("(o n) -> o n", o=1).to_broadcast([P, E])),
             (ln_w[:], io["L0_ffn_ln2_w"].rearrange("(k p) -> p k", p=P)),
             (ln_b[:], io["L0_ffn_ln2_b"].rearrange("(k p) -> p k", p=P))]
    return (wp, gw, gb, ln_w, ln_b), loads


def project_and_route(nc, sem, sb, ps, io, dr, ident, weights, w_in, expert, at):
    T = 4
    N = T * P
    CHUNKS = TOKENS // N
    INV = 2
    wp, gw, gb, ln_w, ln_b = weights
    yc, y0 = sb("pg_y", [P, T, C]), sb("pg_y0", [P, 2 * T, C])
    yT, zT = sb("pg_yT", [P, KC, N]), sb("pg_zT", [P, KC, N])
    RING = 3
    rows = sb("pg_rows", [P, RING * T, ROW])
    logits = sb("pg_logits", [P, T, E])
    top1, eq, m8, first = sb("pg_max", [P, T]), sb("pg_eq", [P, T, E]), sb("pg_m8", [P, T, E]), sb("pg_first", [P, T])
    hot, lower, ones = sb("pg_hot", [P, T, E], BF16), sb("pg_lower", [P, P], BF16), sb("pg_ones", [P, P], BF16)
    back, next_, region = sb("pg_back", [P, E]), sb("pg_next", [P, E]), sb("pg_region", [P, E])
    place, mine, slotf = sb("pg_place", [P, T, E]), sb("pg_mine", [P, T, E]), sb("pg_slotf", [P, T])
    slot = sb("pg_slot", [P, TILES], I32)
    lane, padrow, padf, pad = sb("pg_lane", [P, 1]), sb("pg_padrow", [P, ROW]), sb("pg_padf", [P, E]), sb("pg_pad", [P, E], I32)
    tiles, start, base = sb("pg_tiles", [1, E]), sb("pg_start", [1, E]), sb("pg_base", [1, E])
    cum = [sb(f"pg_cum{i}", [1, E]) for i in range(2)]
    js, past, begun, owner, spot = sb("pg_js", [1, MT]), *(sb("pg_" + n, [1, MT, E]) for n in ("past", "begun", "owner", "spot"))
    exf, atf, extra, js128 = (sb("pg_" + n, [1, MT]) for n in ("exf", "atf", "extra", "js128"))
    x2, nc2 = sb("pg_x2", [P, T, C]), sb("pg_n2", [P, T, C])
    st, mv, seen = sb("pg_st", [P, T, 6]), sb("pg_mv", [P, T, 2]), sb("pg_seen", [P, 1])
    eps, power, ve, rs = (sb("pg_" + n, [P, T]) for n in ("eps", "power", "ve", "rs"))
    pY, pO, pN, pG = ps("pg_pY", [P, KC, N]), ps("pg_pO", [P, T, C]), ps("pg_pN", [P, KC, N]), ps("pg_pG", [P, T, E])
    pC = ps("pg_pC", [P, T + 1, E])
    kept, summed, numbered, hotd, counted, placed, padded, route, table = (sem("pg_" + n) for n in (
        "kept", "summed", "numbered", "hot", "counted", "placed", "padded", "route", "table"))
    sent = [sem(f"pg_sent{i}") for i in range(RING)]
    pads_sent = sem("pg_pads_sent")
    MAGIC = 1.5 * 2.0 ** 23
    y_in, consts = (sem("pg_" + n) for n in ("y_in", "consts"))
    y0_in = [sem(f"pg_y0_in{i}") for i in range(2)]
    turned, yTd, outed, added, stats, waited, aggred, inv, n2d, nT, zd, gated = (sem("pg_" + n) for n in (
        "turned", "yT", "projected", "added", "stats", "waited", "aggr", "rstd", "n2", "n2T", "zT", "gate"))
    ROUTE, PLACES, CONSTS = 5, 4, 13
    WAITS = 16 * len(weights)

    def tokens(d, i):
        return d[bass.ds(i * N, N), :].rearrange("(t p) c -> p t c", p=P)

    def skewed(eng, chunk):
        chunk(0, None, None)
        chunk(1, 0, None)
        with eng.Fori(2, CHUNKS - 1) as i:
            chunk(i, i - 1, i - 2)
        chunk(CHUNKS - 1, CHUNKS - 2, CHUNKS - 3)
        chunk(None, CHUNKS - 1, CHUNKS - 2)
        chunk(None, None, CHUNKS - 1)

    with nc.Block() as block, nc.allow_non_contiguous_dma(reason="per-channel vectors"):
        @block.sync
        def _(sp):
            def each(i, u):
                if not isinstance(i, int) or i:
                    sp.wait_ge(turned, i)
                sp.dma_start(yc[:], tokens(dr["Y"], i)).then_inc(y_in, 16)
                if not isinstance(i, int) or i >= 2:
                    sp.wait_ge(summed, i - 1)
                sp.dma_start(y0[:, u * T:(u + 1) * T, :], tokens(dr["y0"], i)).then_inc(y0_in[u], 16)

            each(0, 0)
            each(1, 1)
            with sp.Fori(1, CHUNKS // 2) as k:
                for u in range(2):
                    each(k * 2 + u, u)

        @block.gpsimd
        def _(pool):
            g = nc.gpsimd

            def count(dst, pattern, base=0, channel=0):
                g.iota(dst, pattern=pattern, base=base, channel_multiplier=channel,
                       allow_small_or_imprecise_dtypes=True).then_inc(consts, 1)

            g.memset(eps[:], EPS).then_inc(consts, 1)
            g.memset(power[:], -0.5).then_inc(consts, 1)
            g.memset(ones[:], 1.0).then_inc(consts, 1)
            g.memset(padrow[:], 0.0).then_inc(consts, 1)
            pool.wait_ge(consts, 4)
            g.affine_select(out=lower[:], in_=ones[:], compare_op=ALU.is_gt, fill=0.0, base=0,
                            pattern=[[1, P]], channel_multiplier=-1).then_inc(consts, 1)
            count(back[:], [[-1, E]], base=E)
            count(next_[:], [[REGION, E]])
            count(region[:], [[REGION, E]])
            count(lane[:], [[1, 1]], channel=1)
            count(js[:], [[1, MT]])
            count(js128[:], [[P, MT]])
            count(padrow[:, 2 * C:2 * C + 1].bitcast(I32), [[1, 1]], base=TOKENS, channel=1)
            g.memset(rows[:, :, 2 * C:], 0.0).then_inc(consts, 1)
            pool.wait_ge(consts, CONSTS)

            def send(i):
                pool.wait_ge(placed, i + 1)
                pool.wait_ge(kept, i + 1)
                pool.wait_ge(numbered, (i + 1) * T)
                for t in range(T):
                    pool.indirect_dma_start(out=dr["routed"], out_offset=bass.IndirectOffsetOnAxis(ap=slot[:, i * T + t:i * T + t + 1], axis=0),
                                            in_=rows[:, i % RING * T + t, :], in_offset=None).then_inc(sent[i % RING], 16)

            for i in range(CHUNKS):
                pool.wait_ge(aggred, i * T + T)
                if i:
                    pool.wait_ge(n2d, i * T)
                g.tensor_tensor(ve[:], mv[:, :, 1], eps[:], ALU.add).then_inc(inv, 1)
                pool.wait_ge(inv, i * INV + 1)
                g.tensor_tensor(rs[:], ve[:], power[:], ALU.pow).then_inc(inv, 1)
                mine_ = slice(i % RING * T, (i % RING + 1) * T)
                if i >= RING:
                    pool.wait_ge(sent[i % RING], i // RING * T * 16)
                g.tensor_tensor(rows[:, mine_, C:2 * C], x2[:], y0[:, i % 2 * T:(i % 2 + 1) * T, :], ALU.add).then_inc(summed, 1)
                for t in range(T):
                    g.iota(rows[:, i % RING * T + t, 2 * C:2 * C + 1].bitcast(I32), pattern=[[1, 1]],
                           base=(i * T + t) * P, channel_multiplier=1).then_inc(numbered, 1)
                if i >= 2:
                    send(i - 2)
            send(CHUNKS - 2)
            send(CHUNKS - 1)
            pool.wait_ge(padded, 2)
            for e in range(E):
                pool.indirect_dma_start(out=dr["routed"], out_offset=bass.IndirectOffsetOnAxis(ap=pad[:, e:e + 1], axis=0),
                                        in_=padrow[:], in_offset=None).then_inc(pads_sent, 16)
            for u in range(RING):
                pool.wait_ge(sent[u], len(range(u, CHUNKS, RING)) * T * 16)
            pool.wait_ge(pads_sent, E * 16)

        @block.scalar
        def _(a):
            def turn_out(i):
                a.wait_ge(turned, i + 1)
                if not isinstance(i, int) or i:
                    a.wait_ge(outed, i)
                a.copy(yT[:], pY[:]).then_inc(yTd, 1)

            turn_out(0)

            def chunk(i, prev, pp):
                if i is not None and not (isinstance(i, int) and i == CHUNKS - 1):
                    turn_out(i + 1)
                if prev is not None:
                    a.wait_ge(nT, prev + 1)
                    a.wait_ge(gated, prev)
                    a.wait_ge(w_in, WAITS)
                    for k in range(KC):
                        a.activation(zT[:, k, :], pN[:, k, :], ACT.Identity, bias=ln_b[:, k:k + 1],
                                     scale=ln_w[:, k:k + 1]).then_inc(zd, 1)
                if prev is not None:
                    a.wait_ge(summed, prev + 1)
                    a.wait_ge(n2d, prev * T + T)
                    a.copy(rows[:, bass.ds(prev % RING * T, T), 0:C], nc2[:]).then_inc(kept, 1)

            a.wait_ge(w_in, WAITS)
            skewed(a, chunk)

        @block.vector
        def _(dve):
            v = nc.vector
            dve.wait_ge(w_in, WAITS)

            dve.wait_ge(consts, CONSTS)

            def each_token(a):
                return a[:].unsqueeze(2).to_broadcast([P, T, E])

            def each_expert(a):
                return a[:].unsqueeze(1).to_broadcast([P, T, E])

            def route_chunk(i):
                c = Chain(dve, route, i * (ROUTE + PLACES))
                dve.wait_ge(gated, i + 1)
                c.link(v.tensor_tensor(logits[:], pG[:], each_expert(gb), ALU.add))
                c.link(v.tensor_reduce(top1[:], logits[:], AX.X, ALU.max))
                c.link(v.tensor_tensor(eq[:], logits[:], each_token(top1), ALU.is_equal))
                c.link(v.tensor_tensor(m8[:], eq[:], each_expert(back), ALU.mult))
                c.link(v.tensor_reduce(first[:], m8[:], AX.X, ALU.max))
                v.tensor_tensor(hot[:], each_token(first), each_expert(back), ALU.is_equal).then_inc(hotd, 1)
                assert c.n == ROUTE

            def place_chunk(i, before):
                c = Chain(dve, route, i * (ROUTE + PLACES) + before)
                dve.wait_ge(counted, i + 1)
                c.link(v.tensor_tensor(place[:], pC[:, 0:T, :], each_expert(next_), ALU.add))
                c.link(v.tensor_tensor(next_[:], next_[:], pC[:, T, :], ALU.add))
                c.link(v.tensor_tensor(mine[:], place[:], hot[:], ALU.mult))
                c.link(v.reduce_sum(slotf[:], mine[:], AX.X))
                v.tensor_copy(slot[:, bass.ds(i * T, T)], slotf[:]).then_inc(placed, 1)
                assert c.n == PLACES

            def chunk(i, prev, pp):
                if i is not None:
                    dve.wait_ge(outed, i + 1)
                    dve.wait_ge(y0_in[0], (i // 2 + 1) * 16)
                    if not isinstance(i, int) or i:
                        dve.wait_ge(y0_in[1], (i + 1) // 2 * 16)
                    dve.wait_ge(summed, i)
                    if not isinstance(i, int) or i:
                        dve.wait_ge(n2d, i * T)
                    v.tensor_tensor(x2[:], pO[:], y0[:, bass.ds(i % 2 * T, T), :], ALU.add).then_inc(added, 1)
                    dve.wait_ge(added, i + 1)
                    for t in range(T):
                        v.bn_stats(st[:, t, :], x2[:, t, :]).then_inc(stats, 1)
                    dve.wait_ge(stats, i * T + T)
                    v.tensor_copy(seen[:], st[:, T - 1, 0:1]).then_inc(waited, 1)
                    for t in range(T):
                        v.bn_aggr(mv[:, t, :], st[:, t, :]).then_inc(aggred, 1)
                if i is not None:
                    dve.wait_ge(inv, i * INV + INV)
                    dve.wait_ge(nT, i)
                    dve.wait_ge(kept, i)
                    for t in range(T):
                        v.tensor_scalar(nc2[:, t, :], x2[:, t, :], mv[:, t, 0:1], rs[:, t:t + 1],
                                        ALU.subtract, ALU.mult).then_inc(n2d, 1)
                if pp is not None:
                    place_chunk(pp, ROUTE)
                if prev is not None:
                    route_chunk(prev)

            skewed(dve, chunk)

            c = Chain(dve, table)
            dve.wait_ge(placed, CHUNKS)
            v.tensor_scalar(padf[:], next_[:], lane[:], None, ALU.add).then_inc(padded, 1)
            dve.wait_ge(padded, 1)
            v.tensor_copy(pad[:], padf[:]).then_inc(padded, 1)
            c.link(v.tensor_tensor(tiles[:], next_[0:1, :], region[0:1, :], ALU.subtract))
            c.link(v.tensor_scalar(tiles[:], tiles[:], 1.0 / P, 127.0 / P - 0.5 + 1.0 / 256, ALU.mult, ALU.add))
            c.link(v.tensor_scalar(tiles[:], tiles[:], MAGIC, MAGIC, ALU.add, ALU.subtract))
            c.link(v.tensor_copy(cum[0][:], tiles[:]))
            w, n = 0, 1
            while n < E:
                c.did(v.tensor_copy(cum[1 - w][:, 0:n], cum[w][:, 0:n]))
                c.link(v.tensor_tensor(cum[1 - w][:, n:], cum[w][:, n:], cum[w][:, :E - n], ALU.add))
                w, n = 1 - w, 2 * n

            def each_tile(a):
                return a[:].unsqueeze(1).to_broadcast([1, MT, E])

            def for_experts(a):
                return a[:].unsqueeze(2).to_broadcast([1, MT, E])

            c.link(v.tensor_tensor(start[:], cum[w][:], tiles[:], ALU.subtract))
            c.did(v.tensor_tensor(past[:], for_experts(js), each_tile(cum[w]), ALU.is_ge))
            c.link(v.tensor_tensor(begun[:], for_experts(js), each_tile(start), ALU.is_ge))
            c.link(v.tensor_scalar(start[:], start[:], -float(P), None, ALU.mult))
            c.link(v.tensor_tensor(base[:], start[:], region[0:1, :], ALU.add))
            c.did(v.tensor_tensor(owner[:], begun[:], past[:], ALU.subtract))
            c.link(v.tensor_tensor(spot[:], for_experts(js128), each_tile(base), ALU.add))
            c.link(v.tensor_tensor(spot[:], spot[:], owner[:], ALU.mult))
            c.did(v.reduce_sum(atf[:], spot[:], AX.X))
            c.did(v.reduce_sum(exf[:], past[:], AX.X))
            c.link(v.tensor_scalar(extra[:], past[:, :, E - 1], next_[0:1, E - 1:E], None, ALU.mult))
            c.link(v.tensor_tensor(atf[:], atf[:], extra[:], ALU.add))
            c.link(v.tensor_scalar(exf[:], exf[:], float(E - 1), None, ALU.min))
            c.did(v.tensor_copy(at[:], atf[:]))
            c.link(v.tensor_copy(expert[:], exf[:]))

        @block.tensor
        def _(pe):
            pe.wait_ge(w_in, WAITS)

            pe.wait_ge(consts, CONSTS)

            def turn(i):
                pe.wait_ge(y_in, i * 16 + 16)
                if not isinstance(i, int) or i:
                    pe.wait_ge(yTd, i)
                for t in range(T):
                    for k in range(KC):
                        last = nc.tensor.transpose(pY[:, k, t * P:(t + 1) * P], yc[:, t, k * P:(k + 1) * P], ident[:])
                last.then_inc(turned, 1)

            turn(0)

            def chunk(i, prev, pp):
                if i is not None:
                    pe.wait_ge(yTd, i + 1)
                    pe.wait_ge(added, i)
                    for t in range(T):
                        for k in range(KC):
                            last = nc.tensor.matmul(pO[:, t, :], yT[:, k, t * P:(t + 1) * P], wp[:, k, :],
                                                    start=(k == 0), stop=(k == KC - 1))
                    last.then_inc(outed, 1)
                if i is not None and not (isinstance(i, int) and i == CHUNKS - 1):
                    turn(i + 1)
                if prev is not None:
                    pe.wait_ge(zd, prev * KC)
                    pe.wait_ge(n2d, prev * T + T)
                    for t in range(T):
                        for k in range(KC):
                            last = nc.tensor.transpose(pN[:, k, t * P:(t + 1) * P], nc2[:, t, k * P:(k + 1) * P], ident[:])
                    last.then_inc(nT, 1)
                if pp is not None:
                    pe.wait_ge(hotd, pp + 1)
                    for t in range(T):
                        for b in range(t):
                            nc.tensor.matmul(pC[:, t, :], ones[:], hot[:, b, :], start=(b == 0), stop=False)
                        nc.tensor.matmul(pC[:, t, :], lower[:], hot[:, t, :], start=(t == 0), stop=True)
                    for t in range(T):
                        last = nc.tensor.matmul(pC[:, T, :], ones[:], hot[:, t, :], start=(t == 0), stop=(t == T - 1))
                    last.then_inc(counted, 1)
                if prev is not None:
                    pe.wait_ge(zd, prev * KC + KC)
                    if pp is not None:
                        pe.wait_ge(hotd, prev)
                    for t in range(T):
                        for k in range(KC):
                            last = nc.tensor.matmul(pG[:, t, :], zT[:, k, t * P:(t + 1) * P], gw[:, k, :],
                                                    start=(k == 0), stop=(k == KC - 1))
                    last.then_inc(gated, 1)

            skewed(pe, chunk)


def experts(nc, sem, sb, ps, io, dr, ident, w1, w2, expert, at):
    HC = HID // P
    ln_w, ln_b = sb("ex_lnw", [P, KC]), sb("ex_lnb", [P, KC])
    RES, OUTS = 8, 4
    z = sb("ex_z", [P, C])
    res = sb("ex_res", [P, RES, ROW - C])
    x, xo, st, mv, seen = sb("ex_x", [P, C]), sb("ex_out", [P, OUTS, C]), sb("ex_st", [P, 6]), sb("ex_mv", [P, 2]), sb("ex_seen", [P, 1])
    eps, power, ve, rs = (sb("ex_" + n, [P, 1]) for n in ("eps", "power", "ve", "rs"))
    zT = sb("ex_zT", [P, KC, P])
    hs, hT = sb("ex_h", [P, HID]), sb("ex_hT", [P, HC, P])
    pZ, pH, pT, pY = ps("ex_pZ", [P, KC, P]), ps("ex_pH", [P, HID]), ps("ex_pT", [P, HC, P]), ps("ex_pY", [P, C])
    w_in, z_in, turned, zd, up, gelu, hturned, hTd, down, added = (sem("ex_" + n) for n in (
        "w_in", "z_in", "turned", "zT", "up", "gelu", "h_turned", "hT", "down", "added"))
    res_in, consts, stats, waited, aggred, inv, outd = (sem("ex_" + n) for n in ("res_in", "consts", "stats", "waited", "aggr", "rstd", "out"))
    sent = [sem(f"ex_sent{i}") for i in range(2)]
    out = io["out"].rearrange("b l c -> (b l) c")

    def skewed(eng, tile):
        tile(0, None, True)
        tile(1, 0, True)
        with eng.Fori(2, MT - 1) as j:
            tile(j, j - 1, True)
        tile(MT - 1, MT - 2, False)
        tile(None, MT - 1, False)

    with nc.Block() as block, nc.allow_non_contiguous_dma(reason="per-channel vectors"):
        @block.sync
        def _(sp):
            sp.dma_start(ln_w[:], io["L0_ffn_ln2_w"].rearrange("(k p) -> p k", p=P)).then_inc(w_in, 16)
            sp.dma_start(ln_b[:], io["L0_ffn_ln2_b"].rearrange("(k p) -> p k", p=P)).then_inc(w_in, 16)

            def load(j):
                row = sp.value_load(at[0:1, bass.ds(j, 1)], min_val=0, max_val=E * REGION - P)
                if not isinstance(j, int) or j:
                    sp.wait_ge(turned, j)
                sp.dma_start(z[:], dr["routed"][bass.ds(row, P), 0:C]).then_inc(z_in, 16)
                sp.dma_start(res[:, bass.ds(j % RES, 1), :].rearrange("p o c -> p (o c)"), dr["routed"][bass.ds(row, P), C:ROW]).then_inc(res_in, 16)

            load(0)
            with sp.Fori(1, MT) as j:
                load(j)

        @block.gpsimd
        def _(pool):
            g = nc.gpsimd
            g.memset(eps[:], EPS).then_inc(consts, 1)
            g.memset(power[:], -0.5).then_inc(consts, 1)
            pool.wait_ge(consts, 2)
            for j in range(MT):
                if j >= 2:
                    pool.wait_ge(sent[j % 2], j // 2 * 16)
                pool.wait_ge(aggred, j + 1)
                if j:
                    pool.wait_ge(outd, j)
                g.tensor_tensor(ve[:], mv[:, 1:2], eps[:], ALU.add).then_inc(inv, 1)
                pool.wait_ge(inv, 2 * j + 1)
                g.tensor_tensor(rs[:], ve[:], power[:], ALU.pow).then_inc(inv, 1)
                pool.wait_ge(outd, j + 1)
                pool.indirect_dma_start(out=out, out_offset=bass.IndirectOffsetOnAxis(ap=res[:, j % RES, C:C + 1].bitcast(I32), axis=0),
                                        in_=xo[:, j % OUTS, :], in_offset=None, bounds_check=TOKENS - 1,
                                        oob_is_err=False).then_inc(sent[j % 2], 16)
            for u in range(2):
                pool.wait_ge(sent[u], len(range(u, MT, 2)) * 16)

        @block.scalar
        def _(a):
            a.wait_ge(w_in, 32)

            def norm(j):
                a.wait_ge(turned, j + 1)
                a.wait_ge(up, j)
                for k in range(KC):
                    a.activation(zT[:, k, :], pZ[:, k, :], ACT.Identity, bias=ln_b[:, k:k + 1], scale=ln_w[:, k:k + 1]).then_inc(zd, 1)

            def tile(j, prev, more):
                if j is not None:
                    a.wait_ge(up, j + 1)
                    a.wait_ge(hturned, j)
                    a.activation(hs[:], pH[:], ACT.Gelu_apprx_tanh).then_inc(gelu, 1)
                if more:
                    norm(j + 1)

            norm(0)
            skewed(a, tile)

        @block.vector
        def _(dve):
            v = nc.vector

            def tile(j, prev, more):
                if prev is not None:
                    dve.wait_ge(down, prev + 1)
                    dve.wait_ge(res_in, prev * 16 + 16)
                    if not isinstance(prev, int) or prev:
                        dve.wait_ge(outd, prev)
                    v.tensor_tensor(x[:], pY[:], res[:, bass.ds(prev % RES, 1), 0:C].rearrange("p o c -> p (o c)"), ALU.add).then_inc(added, 1)
                    dve.wait_ge(added, prev + 1)
                    v.bn_stats(st[:], x[:]).then_inc(stats, 1)
                    dve.wait_ge(stats, prev + 1)
                    v.tensor_copy(seen[:], st[:, 0:1]).then_inc(waited, 1)
                    v.bn_aggr(mv[:], st[:]).then_inc(aggred, 1)
                if j is not None:
                    dve.wait_ge(hturned, j + 1)
                    if prev is not None:
                        dve.wait_ge(down, j)
                    v.tensor_copy(hT[:], pT[:]).then_inc(hTd, 1)
                if prev is not None:
                    dve.wait_ge(inv, prev * 2 + 2)
                    v.tensor_scalar(xo[:, bass.ds(prev % OUTS, 1), :].rearrange("p o c -> p (o c)"), x[:], mv[:, 0:1], rs[:],
                                    ALU.subtract, ALU.mult).then_inc(outd, 1)

            skewed(dve, tile)

        @block.tensor
        def _(pe):
            def turn(j):
                pe.wait_ge(z_in, j * 16 + 16)
                pe.wait_ge(zd, j * KC)
                for k in range(KC):
                    last = nc.tensor.transpose(pZ[:, k, :], z[:, k * P:(k + 1) * P], ident[:])
                last.then_inc(turned, 1)

            def which(j):
                return pe.value_load(expert[0:1, bass.ds(j, 1)], min_val=0, max_val=E - 1)

            def tile(j, prev, more):
                if j is not None:
                    e = which(j)
                    pe.wait_ge(zd, j * KC + KC)
                    pe.wait_ge(gelu, j)
                    for n in range(HID // 512):
                        for k in range(KC):
                            last = nc.tensor.matmul(pH[:, n * 512:(n + 1) * 512], zT[:, k, :],
                                                    w1[:, k, bass.ds(e, 1), n * 512:(n + 1) * 512], start=(k == 0), stop=(k == KC - 1))
                    last.then_inc(up, 1)
                if more:
                    turn(j + 1)
                if prev is not None:
                    e = which(prev)
                    pe.wait_ge(hTd, prev + 1)
                    if j is None or not isinstance(j, int) or prev:
                        pe.wait_ge(added, prev)
                    for c in range(HC):
                        last = nc.tensor.matmul(pY[:], hT[:, c, :], w2[:, c, bass.ds(e, 1), :], start=(c == 0), stop=(c == HC - 1))
                    last.then_inc(down, 1)
                if j is not None:
                    pe.wait_ge(gelu, j + 1)
                    pe.wait_ge(hTd, j)
                    for c in range(HC):
                        last = nc.tensor.transpose(pT[:, c, :], hs[:, c * P:(c + 1) * P], ident[:])
                    last.then_inc(hturned, 1)

            turn(0)
            skewed(pe, tile)


SCRATCH = {
    "outT": ([C, TOKENS], F32),
    "y0": ([TOKENS, C], F32),
    "qs": ([3, C, TOKENS], BF16),
    "ks": ([3, C, TOKENS], BF16),
    "v": ([TOKENS, H * 2 * DK], F32),
    "Y": ([TOKENS, C], F32),
    "routed": ([E * REGION, ROW], F32),
}


_INS = ["L0_attn_x", "L0_attn_w_wave", "L0_attn_b_wave", "L0_attn_w_query", "L0_attn_b_query", "L0_attn_key_weight",
        "L0_attn_w_se1", "L0_attn_b_se1", "L0_attn_w_se2", "L0_attn_b_se2", "L0_attn_w_out",
        "L0_ffn_ln1_w", "L0_ffn_ln1_b", "L0_ffn_w_qkv", "L0_ffn_w_proj", "L0_ffn_ln2_w", "L0_ffn_ln2_b",
        "L0_ffn_gate_w", "L0_ffn_gate_b", "L0_ffn_w1", "L0_ffn_w2"]


def kernel(**inputs):
    import numpy as _np
    import concourse.bacc as _bacc
    from concourse.bass_utils import run_bass_kernel_spmd as _run

    nc = _bacc.Bacc("TRN2", target_bir_lowering=False, num_devices=1)
    arrays, io = {}, {}
    for name in _INS:
        a = _np.ascontiguousarray(inputs[name])
        arrays[f"in_{name}"] = a
        io[name] = nc.dram_tensor(f"in_{name}", list(a.shape), mybir.dt.from_np(a.dtype), kind="ExternalInput").ap()
    io["out"] = nc.dram_tensor("out_0", [B, L, C], F32, kind="ExternalOutput").ap()
    dr = {n: nc.dram_tensor(f"scratch_{n}", shape, dt, kind="Internal").ap() for n, (shape, dt) in SCRATCH.items()}
    build(nc, io, dr)
    r = _run(nc, [arrays], core_ids=[0])
    return r.results[0]["out_0"]
```
